# Optimizing a Trainium2 kernel written in Bass

```python
import numpy as np
import jax
import jax.numpy as jnp

def _softmax(x, axis=-1):
    return jax.nn.softmax(x, axis=axis)

def _gelu(x):
    return jax.nn.gelu(x, approximate=True)

def _silu(x):
    return jax.nn.silu(x)

def _sigmoid(x):
    return jax.nn.sigmoid(x)

def _layernorm(x, axis=-1, eps=1e-05):
    m = jnp.mean(x, axis=axis, keepdims=True)
    v = jnp.var(x, axis=axis, keepdims=True)
    return (x - m) / jnp.sqrt(v + eps)

def _scatter_add(tgt, idx, src, axis=0):
    return tgt.at[idx].add(src)

def _segment_sum(src, seg, n):
    return jax.ops.segment_sum(src, seg, n)
kernel_name = 'mk_decoder_postln_d1_seqx_r4_81aeb2'

def setup_inputs(seed: int=0):
    np.random.seed(seed)
    _w = jnp.asarray

    def _rec_inputs():
        import jax
        import jax.numpy as jnp
        _rk = jax.random.key(seed)
        x = -0.0002928 + 1 * jax.random.normal(jax.random.fold_in(_rk, 1), (8, 112, 256), jnp.float32)
        _lenS = 112 - jax.random.randint(jax.random.fold_in(_rk, 7), (8,), 0, max(1, 112 // 4) + 1, jnp.int32)
        _lenS2 = 375 - jax.random.randint(jax.random.fold_in(_rk, 8), (8,), 0, max(1, 375 // 4) + 1, jnp.int32)
        _ctx_1024P = jax.random.normal(jax.random.fold_in(_rk, 11), (8, 16, 256), jnp.float32)
        _ctx_1024c = jax.random.dirichlet(jax.random.fold_in(_rk, 511), 0.3 * jnp.ones((16,), jnp.float32), (8, 375))
        _ctx_1024t = jnp.einsum('bsk,bkd->bsd', _ctx_1024c, _ctx_1024P)
        _ctx_1024t = _ctx_1024t * jax.lax.rsqrt(jnp.mean(jnp.square(_ctx_1024t)) + 1e-12) * 0.953939
        ctx_1024 = -1.39393e-06 + 0.999914 * (_ctx_1024t + 0.3 * jax.random.normal(jax.random.fold_in(_rk, 611), (8, 375, 256), jnp.float32))
        _validS = jnp.arange(112)[None, :] < _lenS[:, None]
        _validS2 = jnp.arange(375)[None, :] < _lenS2[:, None]
        _causal = jnp.tril(jnp.ones((112, 112), dtype=bool))
        mask_1x1xSxS2_ik0 = jnp.where(jnp.broadcast_to(_validS2[0:1, None, None, :], (1, 1, 112, 375)), 0, 1).astype(jnp.int32)
        return (x, ctx_1024, mask_1x1xSxS2_ik0)
    x, ctx_1024, mask_1x1xSxS2_ik0 = _rec_inputs()

    def _L0_attn_setup():
        import jax, jax.numpy as jnp
        import numpy as np
        DIM = 256
        HEADS = 16
        DIM_HEAD = 64
        INNER = HEADS * DIM_HEAD
        key = jax.random.key(seed)
        kx, kqkv, kwo, kbo = jax.random.split(key, 4)
        x = jax.random.normal(kx, (4, 512, DIM), dtype=jnp.float32)
        w_qkv = jax.random.normal(kqkv, (DIM, 3 * INNER), dtype=jnp.float32) * (1.0 / np.sqrt(DIM))
        w_out = jax.random.normal(kwo, (INNER, DIM), dtype=jnp.float32) * (1.0 / np.sqrt(INNER))
        b_out = jax.random.normal(kbo, (DIM,), dtype=jnp.float32) * 0.01
        return {'x': x, 'w_qkv': w_qkv, 'w_out': w_out, 'b_out': b_out}
    _L0_attn_all = _L0_attn_setup()
    _L0_attn_in = {k: v for k, v in _L0_attn_all.items() if k in ('w_qkv', 'w_out', 'b_out')}
    del _L0_attn_all

    def _L0_xattn_setup():
        import jax, jax.numpy as jnp
        import numpy as np
        NEG_INF = -10000000000.0
        D_MODEL = 256
        NUM_HEADS = 16
        HEAD_DIM = D_MODEL // NUM_HEADS
        B, S = (2, 512)

        def _split_heads(x):
            b, s, _ = x.shape
            return x.reshape(b, s, NUM_HEADS, HEAD_DIM).transpose(0, 2, 1, 3)
        key = jax.random.key(seed)
        ks = jax.random.split(key, 12)
        std = 1.0 / np.sqrt(D_MODEL)
        inp = {'query': jax.random.normal(ks[0], (B, S, D_MODEL), jnp.float32), 'key': jax.random.normal(ks[1], (B, S, D_MODEL), jnp.float32), 'value': jax.random.normal(ks[2], (B, S, D_MODEL), jnp.float32), 'mask': jnp.tril(jnp.ones((S, S), jnp.int32))[None, None, :, :], 'Wq': jax.random.normal(ks[3], (D_MODEL, D_MODEL), jnp.float32) * std, 'bq': jax.random.normal(ks[4], (D_MODEL,), jnp.float32) * std, 'Wk': jax.random.normal(ks[5], (D_MODEL, D_MODEL), jnp.float32) * std, 'bk': jax.random.normal(ks[6], (D_MODEL,), jnp.float32) * std, 'Wv': jax.random.normal(ks[7], (D_MODEL, D_MODEL), jnp.float32) * std, 'bv': jax.random.normal(ks[8], (D_MODEL,), jnp.float32) * std, 'Wo': jax.random.normal(ks[9], (D_MODEL, D_MODEL), jnp.float32) * std, 'bo': jax.random.normal(ks[10], (D_MODEL,), jnp.float32) * std}
        return inp
    _L0_xattn_all = _L0_xattn_setup()
    _L0_xattn_in = {k: v for k, v in _L0_xattn_all.items() if k in ('Wq', 'bq', 'Wk', 'bk', 'Wv', 'bv', 'Wo', 'bo')}
    del _L0_xattn_all

    def _L0_ffn_setup():
        import jax, jax.numpy as jnp
        import numpy as np
        B, T, C, H, E = (1, 64, 256, 512, 8)
        STD = 0.02
        key = jax.random.key(seed)
        ks = jax.random.split(key, 8)
        f32 = jnp.float32
        return {'x': jax.random.normal(ks[0], (B, T, C), f32), 'up': jax.random.normal(ks[1], (E, H, C), f32) * STD, 'gate': jax.random.normal(ks[2], (E, H, C), f32) * STD, 'down': jax.random.normal(ks[3], (E, C, H), f32) * STD, 'router': jax.random.normal(ks[4], (E, C), f32) * STD, 'w_up_s': jax.random.normal(ks[5], (H, C), f32) * STD, 'w_gate_s': jax.random.normal(ks[6], (H, C), f32) * STD, 'w_down_s': jax.random.normal(ks[7], (C, H), f32) * STD}
    _L0_ffn_all = _L0_ffn_setup()
    _L0_ffn_in = {k: v for k, v in _L0_ffn_all.items() if k in ('up', 'gate', 'down', 'router', 'w_up_s', 'w_gate_s', 'w_down_s')}
    del _L0_ffn_all
    return {'x': x, 'ctx_1024': ctx_1024, 'mask_1x1xSxS2_ik0': mask_1x1xSxS2_ik0, 'L0_attn_w_qkv': _L0_attn_in['w_qkv'], 'L0_attn_w_out': _L0_attn_in['w_out'], 'L0_attn_b_out': _L0_attn_in['b_out'], 'L0_xattn_Wq': _L0_xattn_in['Wq'], 'L0_xattn_bq': _L0_xattn_in['bq'], 'L0_xattn_Wk': _L0_xattn_in['Wk'], 'L0_xattn_bk': _L0_xattn_in['bk'], 'L0_xattn_Wv': _L0_xattn_in['Wv'], 'L0_xattn_bv': _L0_xattn_in['bv'], 'L0_xattn_Wo': _L0_xattn_in['Wo'], 'L0_xattn_bo': _L0_xattn_in['bo'], 'L0_ffn_up': _L0_ffn_in['up'], 'L0_ffn_gate': _L0_ffn_in['gate'], 'L0_ffn_down': _L0_ffn_in['down'], 'L0_ffn_router': _L0_ffn_in['router'], 'L0_ffn_w_up_s': _L0_ffn_in['w_up_s'], 'L0_ffn_w_gate_s': _L0_ffn_in['w_gate_s'], 'L0_ffn_w_down_s': _L0_ffn_in['w_down_s']}

def reference(x, ctx_1024, mask_1x1xSxS2_ik0, L0_attn_w_qkv, L0_attn_w_out, L0_attn_b_out, L0_xattn_Wq, L0_xattn_bq, L0_xattn_Wk, L0_xattn_bk, L0_xattn_Wv, L0_xattn_bv, L0_xattn_Wo, L0_xattn_bo, L0_ffn_up, L0_ffn_gate, L0_ffn_down, L0_ffn_router, L0_ffn_w_up_s, L0_ffn_w_gate_s, L0_ffn_w_down_s):
    import jax
    import jax.numpy as jnp

    def _L0_attn_ref(x, w_qkv, w_out, b_out):
        import jax, jax.numpy as jnp
        import numpy as np
        DIM = 256
        HEADS = 16
        DIM_HEAD = 64
        INNER = HEADS * DIM_HEAD
        b, n, _ = x.shape
        scale = 1.0 / np.sqrt(DIM_HEAD)
        qkv = x @ w_qkv
        q, k, v = jnp.split(qkv, 3, axis=-1)
        reshape = lambda z: z.reshape(b, n, HEADS, DIM_HEAD).transpose(0, 2, 1, 3)
        q, k, v = (reshape(q), reshape(k), reshape(v))
        sim = jnp.einsum('bhid,bhjd->bhij', q, k) * scale
        attn = jax.nn.softmax(sim, axis=-1)
        out = jnp.einsum('bhij,bhjd->bhid', attn, v)
        out = out.transpose(0, 2, 1, 3).reshape(b, n, INNER)
        return out @ w_out + b_out

    def _L0_xattn_ref(query, key, value, mask, Wq, bq, Wk, bk, Wv, bv, Wo, bo):
        import jax, jax.numpy as jnp
        import numpy as np
        NEG_INF = -10000000000.0
        D_MODEL = 256
        NUM_HEADS = 16
        HEAD_DIM = D_MODEL // NUM_HEADS
        B, S = (2, 512)

        def _split_heads(x):
            b, s, _ = x.shape
            return x.reshape(b, s, NUM_HEADS, HEAD_DIM).transpose(0, 2, 1, 3)
        q = _split_heads(query @ Wq.T + bq)
        k = _split_heads(key @ Wk.T + bk)
        v = _split_heads(value @ Wv.T + bv)
        scale = 1.0 / jnp.sqrt(jnp.float32(HEAD_DIM))
        scores = jnp.einsum('bhqd,bhkd->bhqk', q, k) * scale
        scores = jnp.where(mask == 0, NEG_INF, scores)
        probs = jax.nn.softmax(scores, axis=-1)
        out = jnp.einsum('bhqk,bhkd->bhqd', probs, v)
        out = out.transpose(0, 2, 1, 3).reshape(query.shape[0], -1, D_MODEL)
        return out @ Wo.T + bo

    def _L0_ffn_ref(x, up, gate, down, router, w_up_s, w_gate_s, w_down_s):
        import jax, jax.numpy as jnp
        import numpy as np
        B, T, C, H, E = (1, 64, 256, 512, 8)
        STD = 0.02
        b, t, c = x.shape
        x_ = x.reshape(b * t, c)
        logits = x_ @ router.T
        idx = jnp.argmax(logits, axis=-1)
        onehot = jax.nn.one_hot(idx, router.shape[0], dtype=x.dtype)
        u = jnp.einsum('bc,ehc->ebh', x_, up)
        g = jnp.einsum('bc,ehc->ebh', x_, gate)
        h = jax.nn.silu(g) * u
        ye = jnp.einsum('ebh,ech->ebc', h, down)
        y = jnp.einsum('ebc,be->bc', ye, onehot)
        ys = jax.nn.silu(x_ @ w_gate_s.T) * (x_ @ w_up_s.T) @ w_down_s.T
        return (y + ys).reshape(b, t, c)
    x = _layernorm(x + _L0_attn_ref(x, L0_attn_w_qkv, L0_attn_w_out, L0_attn_b_out), axis=-1)
    x = _layernorm(x + _L0_xattn_ref(x, ctx_1024, ctx_1024, mask_1x1xSxS2_ik0, L0_xattn_Wq, L0_xattn_bq, L0_xattn_Wk, L0_xattn_bk, L0_xattn_Wv, L0_xattn_bv, L0_xattn_Wo, L0_xattn_bo), axis=-1)
    x = _layernorm(x + _L0_ffn_ref(x, L0_ffn_up, L0_ffn_gate, L0_ffn_down, L0_ffn_router, L0_ffn_w_up_s, L0_ffn_w_gate_s, L0_ffn_w_down_s), axis=-1)
    return x

_drawn_inputs = setup_inputs


def setup_inputs(seed=0):
    import zlib

    import numpy as np

    out = dict(_drawn_inputs(seed))
    spreads = {}
    factors = {'L0_attn_b_out': 6.631, 'L0_xattn_bq': 3.764, 'L0_xattn_bk': 8.0}
    for name, (base, spread) in spreads.items():
        noise = np.random.default_rng([zlib.crc32(name.encode()), seed]).standard_normal(out[name].shape)
        drawn = base * np.exp(spread * noise) if base else spread * noise
        out[name] = jnp.asarray(drawn.astype(out[name].dtype))
    for name, factor in factors.items():
        out[name] = (out[name] * factor).astype(out[name].dtype)
    return out
```

```python
from contextlib import ExitStack

import concourse.bass as bass
from concourse import mybir

dt = mybir.dt
F32, F32R, BF16, I32, U32 = dt.float32, dt.float32r, dt.bfloat16, dt.int32, dt.uint32
ALU = mybir.AluOpType
ACT = mybir.ActivationFunctionType
AX = mybir.AxisListType

B, S, C = 8, 112, 256
KC = C // 128
H = 16
D1 = 64
INNER = H * D1
G1 = 4
S2 = 375
KT = 3
SK = S2 // KT
D2 = C // H
VP = 32
E, HID = 8, 512
HT = HID // 128
T = B * S
TILE = 128
ROUTED_TILES = (T - E) // TILE + E
EPS = 1e-5
MASKED = -1e30
PAIRS = B // 2


def build(nc, a, out):
    ctx = ExitStack()
    with ctx:
        def sb(name, shape, d=F32):
            return ctx.enter_context(nc.sbuf_tensor(name, shape, d))

        def sem(name):
            return ctx.enter_context(nc.semaphore(name))

        def sems(name, n):
            return [sem(f"{name}_{j}") for j in range(n)]

        bank = [ctx.enter_context(nc.psum_tensor(f"bank{j}", [128, 512], F32)) for j in range(8)]
        slots_x = nc.dram_tensor("slots_x", (ROUTED_TILES * TILE, C), F32, kind="Internal").ap()
        slots_y = nc.dram_tensor("slots_y", (ROUTED_TILES * TILE, C), F32, kind="Internal").ap()

        ident = sb("ident", [128, 128])
        identb = sb("identb", [128, 128], BF16)
        minus_half = sb("minus_half", [S, 1])
        xres = sb("xres", [S, B, C])
        x2T = sb("x2T", [128, KC, T])
        wx = sb("wx", [128, 4, KC, C])
        cols = sb("cols", [128, 2, KC])
        rows = sb("rows", [128, 3, C])
        ybuf = sb("ybuf", [S, 2, C])
        stats = sb("stats", [S, 2, 6])
        mv = sb("mv", [S, 2, 2])
        veps = sb("veps", [S, 2])
        rstd = sb("rstd", [S, 2])
        xb = sb("xb", [S, 2, C])
        ugs = sb("ugs", [128, KC, 2 * HID])
        dns = sb("dns", [128, HT, C])
        zeros = sb("zeros", [128, C])

        UG, DN = KC * 2 * HID, HT * C
        ARENA = E * (UG + DN)
        arena = sb("arena", [128, ARENA])
        top = [0]

        def carve(n):
            top[0] += n
            assert top[0] <= ARENA
            return arena[:, top[0] - n:top[0]]

        wqkv = carve(KC * 3 * INNER).rearrange("p (k n) -> p k n", k=KC)
        wout = carve(INNER // 128 * C).rearrange("p (k n) -> p k n", n=C)
        xT = [carve(KC * S).rearrange("p (k n) -> p k n", k=KC) for _ in range(2)]
        v1 = [carve(INNER)[0:S] for _ in range(2)]
        qT = [carve(8 * S).rearrange("p (k n) -> p k n", k=8) for _ in range(2)]
        kT = [carve(8 * S).rearrange("p (k n) -> p k n", k=8) for _ in range(2)]
        p1 = [carve(G1 * S)[0:S].rearrange("p (k n) -> p k n", k=G1) for _ in range(4)]
        pT1 = [carve(G1 * S)[0:S].rearrange("p (k n) -> p k n", k=G1) for _ in range(2)]
        oT1 = [carve(8 * S).rearrange("p (k n) -> p k n", k=8) for _ in range(2)]
        ug = arena[:, 0:E * UG].rearrange("p (e k n) -> p e k n", e=E, k=KC)
        dn = arena[:, E * UG:ARENA].rearrange("p (e k n) -> p e k n", e=E, k=HT)
        nm1 = sb("nm1", [S, H])
        rs1 = sb("rs1", [S, H])
        rc1 = sb("rc1", [S, H])

        mid = sb("mid", [128, 2, 2 * KC * S2])
        ctxT, kT2 = (mid[:, j, :].rearrange("p (b k n) -> p b k n", b=2, k=KC) for j in range(2))
        v2_all = sb("v2", [128, 2 * KT * H * VP])
        v2 = v2_all[0:SK, :].rearrange("p (b k h d) -> p b k h d", b=2, k=KT, h=H)
        qm = sb("qm", [128, 2, KC, 2, S])
        qscale = sb("qscale", [128, 2, S])
        halves = sb("halves", [128, 2])
        x1c = sb("x1c", [S, 2, C])
        x1T = sb("x1T", [128, KC, S])
        p2_all = sb("p2", [128, 3 * S2])
        p2 = p2_all[0:S, :].rearrange("p (k n) -> p k n", k=3)
        pT2 = sb("pT2", [SK, 2, KT, S])
        nm2 = sb("nm2", [S, H])
        oT2 = sb("oT2", [128, 4, S])
        o2 = sb("o2", [S, C])
        rc2 = sb("rc2", [S, H])
        on2T = sb("on2T", [128, KC, S])
        mask_i = sb("mask_i", [S, S2], I32)
        mask0 = sb("mask0", [S, S2])
        allm = sb("allm", [S, 1])
        anym = sb("anym", [S, 1])
        anyw = sb("anyw", [S, 128])
        bias = sb("bias", [S, S2], BF16)
        x2c = sb("x2c", [S, 2, C])

        hTs = sb("hTs", [128, HT, 4 * S])
        gs = sb("gs", [128, 4 * S])
        routerT = sb("routerT", [128, KC, E])
        upto = sb("upto", [S, S])
        ones = sb("ones", [S, 128])
        logit = sb("logit", [S, B, E])
        top8 = sb("top8", [S, B, 8])
        tidx = sb("tidx", [S, B, 8], U32)
        choice = sb("choice", [S, B])
        onehot = sb("onehot", [S, B, E])
        incl = sb("incl", [S, B, E])
        cnt = sb("cnt", [128, B + 1, E])
        fills = sb("fills", [128, E, 7])
        ntile = sb("ntile", [128, E])
        ends = sb("ends", [128, E + 1])
        pos = sb("pos", [S, B, E])
        slotf = sb("slotf", [S, B])
        slot = sb("slot", [S, B], U32)
        steps7 = sb("steps7", [128, 7])
        eidx = sb("eidx", [128, E])
        tiles_i = sb("tiles_i", [1, ROUTED_TILES])
        past = sb("past", [1, ROUTED_TILES, E - 1])
        expertf = sb("expertf", [1, ROUTED_TILES])
        expert = sb("expert", [1, ROUTED_TILES], I32)
        xs = sb("xs", [128, 2, C])
        xsT = sb("xsT", [128, 2, KC, 128])
        hr = mid[:, 0, 0:2 * HID].rearrange("p (b n) -> p b n", b=2)
        hrT = mid[:, 1, 0:2 * HID].rearrange("p (b k n) -> p b k n", b=2, k=HT)
        gr = p2_all[:, 2 * C:2 * C + HID]
        yr = p2_all[:, 0:2 * C].rearrange("p (b n) -> p b n", b=2)
        ysh = v2_all[0:S, 0:B * C].rearrange("p (b n) -> p b n", b=B)
        ygat = xres
        mv3 = sb("mv3", [S, B, 2])
        st3 = sb("st3", [S, B, 6])
        ve3 = sb("ve3", [S, B])
        rs3 = sb("rs3", [S, B])

        pause = sem("pause")
        consts = sem("consts")
        w_loaded = {n: sem(f"w_{n}") for n in ("v", "q", "k", "out", "x", "small", "mask", "shared")}
        w_experts = sem("w_experts")
        xT_loaded = sems("xT_loaded", 2)
        zeroed = sem("zeroed")
        proj1 = sems("proj1", 6)
        evac1 = sems("evac1", 6)
        scores1 = sems("scores1", 4)
        max1 = sems("max1", 4)
        exp1 = sems("exp1", 4)
        rcp1 = sem("rcp1")
        norm1 = sems("norm1", 4)
        turn1 = sems("turn1", 4)
        pt1 = sems("pt1", 4)
        pv1 = sems("pv1", 4)
        ot1 = sems("ot1", 2)
        wout1 = sem("wout1")
        xb1 = sem("xb1")
        y1, st1, ag1, ve1, rstd1, x1_done = (sem(n) for n in ("y1", "st1", "ag1", "ve1", "rstd1", "x1_done"))

        ctx_loaded = sems("ctx_loaded", 2)
        prep = sem("prep")
        q_any = sem("q_any")
        v2_ones = sem("v2_ones")
        x1c_done = sem("x1c_done")
        xb2 = sem("xb2")
        x1t_pe, x1t_sb, q_pe, q_sb = (sem(n) for n in ("x1t_pe", "x1t_sb", "q_pe", "q_sb"))
        k_pe, k_sb, v_pe, v_sb = sems("k_pe", KC), sems("k_sb", KC), sems("v_pe", KT), sems("v_sb", KT)
        scores2 = sems("scores2", 4)
        max2 = sems("max2", 4)
        exp2 = sems("exp2", 4)
        turn2 = sems("turn2", 4)
        pt2 = sems("pt2", 4)
        pv2_last = sems("pv2_last", 4)
        ot2 = sem("ot2")
        on_pe, rc_done, on_sb, ont_pe, ont_sb = (sem(n) for n in ("on_pe", "rc_done", "on_sb", "ont_pe", "ont_sb"))
        wo_pe = sem("wo_pe")
        y2, st2, ag2, ve2, rstd2, x2_done, x2_kept = (sem(n) for n in ("y2", "st2", "ag2", "ve2", "rstd2", "x2_done", "x2_kept"))
        x2t_pe, x2t_sb = sem("x2t_pe"), sem("x2t_sb")

        s_logit, s_route, s_incl, s_eload = sem("s_logit"), sem("s_route"), sem("s_incl"), sem("s_eload")
        sh_gu, sh_g, sh_h, sh_y, sh_ysb = (sem(n) for n in ("sh_gu", "sh_g", "sh_h", "sh_y", "sh_ysb"))
        scattered, gathered = sem("scattered"), sem("gathered")
        xs_loaded, ys_stored = sems("xs_loaded", 2), sems("ys_stored", 2)
        xst_pe, xst_sb, gu_pe, g_sb, h_sb, ht_pe, ht_sb, yr_pe, yr_sb = (
            sem(n) for n in ("xst_pe", "xst_sb", "gu_pe", "g_sb", "h_sb", "ht_pe", "ht_sb", "yr_pe", "yr_sb"))
        fin, ve3s, rstd3, done3, stored = sem("fin"), sem("ve3s"), sem("rstd3"), sem("done3"), sem("stored")

        PE_S1, PE_J1, PE_T1, PE_U1, PE_W1 = bank[0:2], bank[2:4], bank[4], bank[5:7], bank[7]
        PE_S2, PE_T2, PE_V2, PE_M2, PE_J2 = bank[0:3], bank[3:5], bank[5], bank[6], bank[7]

        def head1(g, n):
            return 2 * G1 * (g // 2) + 2 * n + g % 2

        def heads_done(b, h):
            return b * (H // 4) + (h // 4 + 1)

        def over_batches(eng, step):
            for p in range(2):
                step(p, p, 0, p == 0, False)
            with eng.Fori(1, PAIRS - 1) as i:
                for p in range(2):
                    step(i * 2 + p, p, i, False, False)
            for p in range(2):
                step(B - 2 + p, p, PAIRS - 1, False, p == 1)

        ROUTE_ONEHOT, ROUTE_SLOTS, ROUTE_EXPERTS = 4, 21, 24

        block = ctx.enter_context(nc.Block())

        @block.sync
        def _(sp):
            for p in range(2):
                sp.dma_start(xT[p], a["xT"][p]).then_inc(xT_loaded[p], 16)
            for n, part in (("v", 2), ("q", 0), ("k", 1)):
                cut = slice(part * INNER, (part + 1) * INNER)
                sp.dma_start(wqkv[:, :, cut], a["wqkv"][:, :, cut]).then_inc(w_loaded[n], 16)
            sp.dma_start(wout, a["wout"]).then_inc(w_loaded["out"], 16)
            sp.dma_start(xres[:], a["x"]).then_inc(w_loaded["x"], 16)
            for j, n in enumerate(("b_out", "bv", "bo")):
                sp.dma_start(rows[:, j, :], a[n].to_broadcast([128, C])).then_inc(w_loaded["small"], 16)
            sp.dma_start(mask_i[:], a["mask"]).then_inc(w_loaded["mask"], 16)
            sp.dma_start(cols[:, 0, :], a["bq"]).then_inc(w_loaded["small"], 16)
            sp.dma_start(cols[:, 1, :], a["bk"]).then_inc(w_loaded["small"], 16)
            sp.dma_start(routerT[:], a["router"]).then_inc(w_loaded["small"], 16)
            for j, n in enumerate(("wq", "wk", "wv", "wo")):
                sp.dma_start(wx[:, j], a[n]).then_inc(w_loaded["small"], 16)
            for p in range(2):
                sp.dma_start(ctxT[:, p], a["ctxT"][p]).then_inc(ctx_loaded[p], 16)
            sp.dma_start(ugs[:], a["ug"][E]).then_inc(w_loaded["shared"], 16)
            sp.dma_start(dns[:], a["dn"][E]).then_inc(w_loaded["shared"], 16)

            def load_xT(b, p, i):
                sp.wait_ge(proj1[5], b - 1)
                sp.dma_start(xT[p], a["xT"][b]).then_inc(xT_loaded[p], 16)

            with sp.Fori(1, PAIRS) as i:
                for p in range(2):
                    load_xT(i * 2 + p, p, i)
            sp.wait_ge(consts, 3)
            for t in range(ROUTED_TILES):
                sp.dma_start(slots_x[t * TILE:(t + 1) * TILE, :], zeros[:]).then_inc(zeroed, 16)
            sp.wait_ge(wout1, B)
            for e in range(E):
                sp.dma_start(ug[:, e], a["ug"][e]).then_inc(w_experts, 16)
                sp.dma_start(dn[:, e], a["dn"][e]).then_inc(w_experts, 16)
                if e % 2 == 1 and 2 <= e + 1 < B:
                    for p in range(2):
                        b = e + 1 + p
                        sp.wait_ge(v_pe[KT - 1], b - 1)
                        sp.dma_start(ctxT[:, p], a["ctxT"][b]).then_inc(ctx_loaded[p], 16)

            def load_tile(t, p, first):
                if not first:
                    sp.wait_ge(xst_pe, t - 1)
                sp.dma_start(xs[:, p], slots_x[bass.ds(t * TILE, TILE), :]).then_inc(xs_loaded[p], 16)

            def store_tile(t, p):
                sp.wait_ge(yr_sb, t + 1)
                sp.dma_start(slots_y[bass.ds(t * TILE, TILE), :], yr[:, p]).then_inc(ys_stored[p], 16)

            sp.wait_ge(scattered, 16 * B)
            for p in range(2):
                load_tile(p, p, True)
            with sp.Fori(0, ROUTED_TILES // 2 - 1) as i:
                for p in range(2):
                    load_tile(i * 2 + 2 + p, p, False)
                    store_tile(i * 2 + p, p)
            for p in range(2):
                store_tile(ROUTED_TILES - 2 + p, p)
            for b in range(B):
                sp.wait_ge(done3, b + 1)
                sp.dma_start(out[b], ygat[:, b]).then_inc(stored, 16)
            sp.wait_ge(stored, 16 * B)

        @block.gpsimd
        def _(g):
            g.memset(ident[:], 0.0).then_inc(consts, 1)
            g.memset(minus_half[:], -0.5).then_inc(consts, 1)
            g.memset(zeros[:], 0.0).then_inc(consts, 1)
            g.wait_ge(consts, 3)
            g.affine_select(out=ident[:], in_=ident[:], compare_op=ALU.not_equal, fill=1.0, base=0,
                            pattern=[[-1, 128]], channel_multiplier=1).then_inc(consts, 1)
            g.wait_ge(consts, 4)
            g.tensor_copy(identb[:], ident[:]).then_inc(consts, 1)
            g.wait_ge(consts, 5)
            g.memset(ones[:], 1.0).then_inc(consts, 1)
            g.memset(v2_all[:], 0.0).then_inc(v2_ones, 1)
            g.wait_ge(v2_ones, 1)
            g.memset(v2[:, :, :, :, D2:D2 + 1], 1.0).then_inc(v2_ones, 1)
            g.wait_ge(consts, 6)
            g.affine_select(out=upto[:], in_=ones[:, 0:S], compare_op=ALU.is_ge, fill=0.0, base=0,
                            pattern=[[1, S]], channel_multiplier=-1).then_inc(consts, 1)
            g.iota(steps7[:], pattern=[[TILE, 7]], base=0, channel_multiplier=0,
                   allow_small_or_imprecise_dtypes=True).then_inc(consts, 1)
            g.iota(eidx[:], pattern=[[1, E]], base=0, channel_multiplier=0,
                   allow_small_or_imprecise_dtypes=True).then_inc(consts, 1)
            g.iota(tiles_i[:], pattern=[[1, ROUTED_TILES]], base=0, channel_multiplier=0,
                   allow_small_or_imprecise_dtypes=True).then_inc(consts, 1)

            g.wait_ge(w_loaded["x"], 16)
            g.wait_ge(w_loaded["small"], 16 * 10)

            def stage1(b, p, i, first, last):
                if not (isinstance(b, int) and b < 2):
                    g.wait_ge(y1, b - 1)
                g.tensor_tensor(xb[:, p], xres[:, b], rows[0:S, 0], ALU.add).then_inc(xb1, 1)
                g.wait_ge(ve1, b + 1)
                g.tensor_tensor(rstd[:, p:p + 1], veps[:, p:p + 1], minus_half[:], ALU.pow).then_inc(rstd1, 1)

            over_batches(g, stage1)

            def copy_x1(b, p, first):
                g.wait_ge(x1_done, b + 1)
                if not first:
                    g.wait_ge(x1t_pe, b - 1)
                    g.wait_ge(xb2, b - 1)
                g.sem_inc(pause, 1)
                g.tensor_copy(x1c[:, p], xres[:, b]).then_inc(x1c_done, 1)

            def stage2(b, p, i, first, last):
                if not last:
                    copy_x1(b + 1, 1 - p, first)
                g.wait_ge(x1c_done, b + 1)
                if not (isinstance(b, int) and b < 2):
                    g.wait_ge(y2, b - 1)
                g.tensor_tensor(xb[:, p], x1c[:, p], rows[0:S, 2], ALU.add).then_inc(xb2, 1)
                if not first:
                    tail(b - 1, 1 - p)

            def tail(b, p):
                g.wait_ge(ve2, b + 1)
                g.tensor_tensor(rstd[:, p:p + 1], veps[:, p:p + 1], minus_half[:], ALU.pow).then_inc(rstd2, 1)
                g.wait_ge(x2_done, b + 1)
                g.sem_inc(pause, 1)
                g.tensor_copy(xres[:, b], x2c[:, p]).then_inc(x2_kept, 1)

            copy_x1(0, 0, True)
            over_batches(g, stage2)
            tail(B - 1, 1)

            g.wait_ge(s_route, ROUTE_SLOTS)
            g.wait_ge(zeroed, 16 * ROUTED_TILES)
            g.wait_ge(x2_kept, B)
            for b in range(B):
                g.indirect_dma_start(slots_x, bass.IndirectOffsetOnAxis(slot[:, b:b + 1], 0), xres[:, b], None).then_inc(scattered, 16)
            for p in range(2):
                g.wait_ge(ys_stored[p], 16 * (ROUTED_TILES // 2))
            for b in range(B):
                g.indirect_dma_start(ygat[:, b], None, slots_y, bass.IndirectOffsetOnAxis(slot[:, b:b + 1], 0)).then_inc(gathered, 16)
            for b in range(B):
                g.wait_ge(ve3s, b + 1)
                g.tensor_tensor(rs3[:, b:b + 1], ve3[:, b:b + 1], minus_half[:], ALU.pow).then_inc(rstd3, 1)


        @block.tensor
        def _(pe):
            pe.wait_ge(consts, 4)

            def project1(c, b, p, i, first):
                if c == 0:
                    pe.wait_ge(xT_loaded[p], (i + 1) * 16)
                if first and c in (0, 2, 4):
                    pe.wait_ge(w_loaded["vqk"[c // 2]], 16)
                if c >= 2:
                    pe.wait_ge(evac1[c - 2], b + 1)
                elif not first:
                    pe.wait_ge(evac1[c + 4], b)
                J = PE_J1[c % 2]
                if c < 2:
                    for k in range(KC):
                        mm = pe.matmul(J[0:S, :], xT[p][:, k, :], wqkv[:, k, 2 * INNER + 512 * c:2 * INNER + 512 * (c + 1)],
                                       start=(k == 0), stop=(k == KC - 1))
                else:
                    for n in range(4):
                        col = (c - 2) * 512 + n * 128
                        for k in range(KC):
                            mm = pe.matmul(J[:, n * S:(n + 1) * S], wqkv[:, k, col:col + 128], xT[p][:, k, :],
                                           start=(k == 0), stop=(k == KC - 1))
                mm.then_inc(proj1[c], 1)

            def score1(g, b, p, first):
                pe.wait_ge(evac1[5 if g >= 2 else 4], b + 1)
                pe.wait_ge(evac1[3 if g >= 2 else 2], b + 1)
                if g >= 2:
                    pe.wait_ge(exp1[g - 2], b + 1)
                elif not first:
                    pe.wait_ge(exp1[g + 2], b)
                for n in range(G1):
                    h = head1(g, n)
                    r = slice(64 * (h % 2), 64 * (h % 2) + 64)
                    mm = pe.matmul(PE_S1[g % 2][0:S, n * S:(n + 1) * S], qT[p][r, h // 2, :], kT[p][r, h // 2, :],
                                   start=True, stop=True)
                mm.then_inc(scores1[g], 1)

            def turn(g, b, first):
                pe.wait_ge(norm1[g], b + 1)
                if g >= 1:
                    pe.wait_ge(pt1[g - 1], b + 1)
                elif not first:
                    pe.wait_ge(pt1[3], b)
                for n in range(G1):
                    mm = pe.transpose(PE_T1[0:S, n * S:(n + 1) * S], p1[g][:, n, :], ident[0:S, 0:S])
                mm.then_inc(turn1[g], 1)

            def value1(g, b, p, first):
                pe.wait_ge(pt1[g], b + 1)
                if g == 0:
                    pe.wait_ge(evac1[1], b + 1)
                if g % 2 == 0 and not first:
                    pe.wait_ge(ot1[g // 2], b)
                for n in range(G1):
                    h = head1(g, n)
                    col = (h // 2 % 4) * S
                    mm = pe.matmul(PE_U1[g // 2][64 * (h % 2):64 * (h % 2) + 64, col:col + S],
                                   v1[p][:, h * D1:(h + 1) * D1], pT1[g % 2][:, n, :], start=True, stop=True)
                mm.then_inc(pv1[g], 1)

            def out1(b, p, first):
                pe.wait_ge(ot1[1], b + 1)
                pe.wait_ge(ot1[0], b + 1)
                if first:
                    pe.wait_ge(w_loaded["out"], 16)
                else:
                    pe.wait_ge(y1, b)
                for k in range(8):
                    mm = pe.matmul(PE_W1[0:S, 0:C], oT1[p][:, k, :], wout[:, k, :], start=(k == 0), stop=(k == 7))
                mm.then_inc(wout1, 1)

            for c in range(6):
                project1(c, 0, 0, 0, True)

            def stage1(b, p, i, first, last):
                j = i + p
                proj = (lambda c: None) if last else (lambda c: project1(c, b + 1, 1 - p, j, False))
                score1(0, b, p, first)
                score1(1, b, p, first)
                if not first:
                    out1(b - 1, 1 - p, isinstance(b, int) and b == 1)
                proj(0)
                score1(2, b, p, first)
                proj(1)
                score1(3, b, p, first)
                turn(0, b, first)
                for g in range(4):
                    proj(g + 2)
                    value1(g, b, p, first)
                    if g < 3:
                        turn(g + 1, b, first)

            over_batches(pe, stage1)
            out1(B - 1, 1, False)

            M, J = PE_M2, PE_J2

            def turn_x1(b, p, first):
                pe.wait_ge(x1c_done, b + 1)
                for k in range(KC):
                    mm = pe.transpose(M[:, k * S:(k + 1) * S], x1c[:, p, k * 128:(k + 1) * 128], ident[0:S, 0:S])
                mm.then_inc(x1t_pe, 1)

            def project_q(b, p):
                pe.wait_ge(x1t_sb, b + 1)
                for m in range(KC):
                    for k in range(KC):
                        mm = pe.matmul(M[:, m * S:(m + 1) * S], wx[:, 0, k, m * 128:(m + 1) * 128], x1T[:, k, :],
                                       start=(k == 0), stop=(k == KC - 1))
                mm.then_inc(q_pe, 1)

            def project_k(m, b, p, i, first):
                if m == 0:
                    pe.wait_ge(ctx_loaded[p], (i + 1) * 16)
                    if not first:
                        pe.wait_ge(v_sb[KT - 1], b)
                else:
                    pe.wait_ge(k_sb[m - 1], b + 1)
                for k in range(KC):
                    mm = pe.matmul(J[:, 0:S2], wx[:, 1, k, m * 128:(m + 1) * 128], ctxT[:, p, k, :],
                                   start=(k == 0), stop=(k == KC - 1))
                mm.then_inc(k_pe[m], 1)

            def project_v(t, b, p):
                pe.wait_ge(v_sb[t - 1] if t else k_sb[KC - 1], b + 1)
                for k in range(KC):
                    mm = pe.matmul(J[0:SK, 0:C], ctxT[:, p, k, t * SK:(t + 1) * SK], wx[:, 2, k, :],
                                   start=(k == 0), stop=(k == KC - 1))
                mm.then_inc(v_pe[t], 1)

            def score2(h, b, p, first):
                if h >= 3:
                    pe.wait_ge(exp2[(h - 3) % 4], heads_done(b, h - 3))
                elif not first:
                    pe.wait_ge(exp2[(max(j for j in range(H) if j % 3 == h)) % 4], heads_done(b - 1, max(j for j in range(H) if j % 3 == h)))
                if h == 0:
                    pe.wait_ge(q_sb, b + 1)
                    pe.wait_ge(k_sb[KC - 1], b + 1)
                m, r = h // 8, slice(32 * (h % 8 // 2), 32 * (h % 8 // 2) + 32)
                pe.matmul(PE_S2[h % 3][0:S, 0:S2], identb[0:S, 0:S], bias[:], start=True, stop=False)
                pe.matmul(PE_S2[h % 3][0:S, 0:S2], qm[r, p, m, h % 2, :], kT2[r, p, m, :],
                          start=False, stop=True).then_inc(scores2[h % 4], 1)

            def turn2_(h, b, first):
                pe.wait_ge(exp2[h % 4], heads_done(b, h))
                if h >= 2:
                    pe.wait_ge(pt2[(h - 2) % 4], heads_done(b, h - 2))
                elif not first:
                    pe.wait_ge(pt2[(H - 2 + h) % 4], heads_done(b - 1, H - 2 + h))
                for t in range(KT):
                    mm = pe.transpose(PE_T2[h % 2][0:SK, t * S:(t + 1) * S], p2[:, h % 3, t * SK:(t + 1) * SK], ident[0:S, 0:S])
                mm.then_inc(turn2[h % 4], 1)

            def value2(h, b, p, first):
                pe.wait_ge(pt2[h % 4], heads_done(b, h))
                if h == 0:
                    pe.wait_ge(v_sb[KT - 1], b + 1)
                    if not first:
                        pe.wait_ge(ot2, b)
                r = slice(32 * (h % 4), 32 * (h % 4) + 32)
                for t in range(KT):
                    mm = pe.matmul(PE_V2[r, (h // 4) * S:(h // 4 + 1) * S], v2[:, p, t, h, :], pT2[:, h % 2, t, :],
                                   start=(t == 0), stop=(t == KT - 1))
                mm.then_inc(pv2_last[h % 4], 1)

            def turn_o(b):
                pe.wait_ge(ot2, b + 1)
                for n in range(4):
                    mm = pe.transpose(M[0:S, n * 128:(n + 1) * 128], oT2[:, n, :], ident[:])
                mm.then_inc(on_pe, 1)

            def turn_on(b):
                pe.wait_ge(on_sb, b + 1)
                for k in range(KC):
                    mm = pe.transpose(M[:, k * S:(k + 1) * S], o2[:, k * 128:(k + 1) * 128], ident[0:S, 0:S])
                mm.then_inc(ont_pe, 1)

            def out2(b):
                pe.wait_ge(ont_sb, b + 1)
                for k in range(KC):
                    mm = pe.matmul(M[0:S, 0:C], on2T[:, k, :], wx[:, 3, k, :], start=(k == 0), stop=(k == KC - 1))
                mm.then_inc(wo_pe, 1)

            def turn_x2(b, p):
                pe.wait_ge(x2_done, b + 1)
                for k in range(KC):
                    mm = pe.transpose(M[:, k * S:(k + 1) * S], x2c[:, p, k * 128:(k + 1) * 128], ident[0:S, 0:S])
                mm.then_inc(x2t_pe, 1)

            pe.wait_ge(prep, 5)
            pe.wait_ge(y1, B)
            pe.wait_ge(consts, 4)
            pe.matmul(PE_J2[:, 0:S], anyw[:], ident[0:S, 0:S], start=True, stop=True).then_inc(q_any, 1)
            pe.wait_ge(w_loaded["small"], 16 * 10)
            pe.wait_ge(prep, 9)
            turn_x1(0, 0, True)
            project_q(0, 0)
            for m in range(KC):
                project_k(m, 0, 0, 0, True)
            for t in range(KT):
                project_v(t, 0, 0)
            pe.wait_ge(consts, 5)

            def stage2(b, p, i, first, last):
                j = i + p

                def turn_x1_next():
                    if not (isinstance(b, int) and b < 2):
                        pe.wait_ge(x2t_sb, b - 1)
                    turn_x1(b + 1, 1 - p, False)

                def turn_o_prev():
                    if last:
                        pe.wait_ge(x2t_sb, b - 1)
                    else:
                        pe.wait_ge(x1t_sb, b + 2)
                    turn_o(b - 1)

                def project_q_next():
                    if not first:
                        pe.wait_ge(on_sb, b)
                    project_q(b + 1, 1 - p)

                def turn_on_prev():
                    if not last:
                        pe.wait_ge(q_sb, b + 2)
                    turn_on(b - 1)

                nxt = {} if last else {
                    0: turn_x1_next, 4: project_q_next,
                    5: lambda: project_k(0, b + 1, 1 - p, j, False), 7: lambda: project_k(1, b + 1, 1 - p, j, False),
                    9: lambda: project_v(0, b + 1, 1 - p), 11: lambda: project_v(1, b + 1, 1 - p),
                    13: lambda: project_v(2, b + 1, 1 - p)}
                prev = {} if first else {
                    2: turn_o_prev, 6: turn_on_prev, 8: lambda: out2(b - 1), 14: lambda: turn_x2(b - 1, 1 - p)}

                for h in range(H + 3):
                    if h < H:
                        score2(h, b, p, first)
                    if h in nxt:
                        nxt[h]()
                    if h in prev:
                        prev[h]()
                    if 2 <= h < H + 2:
                        turn2_(h - 2, b, first)
                    if h >= 3:
                        value2(h - 3, b, p, first)

            over_batches(pe, stage2)
            pe.wait_ge(x2t_sb, B - 1)
            turn_o(B - 1)
            turn_on(B - 1)
            out2(B - 1)
            turn_x2(B - 1, 1)

            pe.wait_ge(x2t_sb, B)
            for b in range(B):
                for k in range(KC):
                    mm = pe.matmul(bank[0][0:S, b * E:(b + 1) * E], x2T[:, k, b * S:(b + 1) * S], routerT[:, k, :],
                                   start=(k == 0), stop=(k == KC - 1))
            mm.then_inc(s_logit, 1)
            pe.wait_ge(w_loaded["shared"], 32)
            n_gu = 0
            for grp in range(2):
                for m in range(HT):
                    if n_gu >= 2:
                        pe.wait_ge(sh_h, n_gu - 1)
                    for part in range(2):
                        for k in range(KC):
                            mm = pe.matmul(bank[2 + 2 * (n_gu % 2) + part][:, 0:4 * S],
                                           ugs[:, k, part * HID + m * 128:part * HID + (m + 1) * 128],
                                           x2T[:, k, grp * 4 * S:(grp + 1) * 4 * S], start=(k == 0), stop=(k == KC - 1))
                    mm.then_inc(sh_gu, 1)
                    n_gu += 1
                    if n_gu == 1:
                        pe.wait_ge(s_route, ROUTE_ONEHOT)
                        pe.matmul(bank[1][0:S, 0:B * E], upto[:], onehot[:].rearrange("p b e -> p (b e)"), start=True, stop=True)
                        pe.matmul(bank[1][:, B * E:2 * B * E], ones[:], onehot[:].rearrange("p b e -> p (b e)"),
                                  start=True, stop=True).then_inc(s_incl, 1)
                pe.wait_ge(sh_h, n_gu)
                for n in range(4):
                    b = grp * 4 + n
                    if b >= 2:
                        pe.wait_ge(sh_ysb, b - 1)
                    for m in range(HT):
                        mm = pe.matmul(bank[6 + b % 2][0:S, 0:C], hTs[:, m, n * S:(n + 1) * S], dns[:, m, :],
                                       start=(m == 0), stop=(m == HT - 1))
                    mm.then_inc(sh_y, 1)

            pe.wait_ge(s_route, ROUTE_EXPERTS)
            pe.wait_ge(w_experts, 32 * E)
            pe.wait_ge(sh_ysb, B)
            XB, GB, UB, HB, YB = bank[0], bank[2:4], bank[4:6], bank[1], bank[6]

            def head_tile(t, p, i, first):
                pe.wait_ge(xs_loaded[p], (i + 1) * 16)
                if not first:
                    pe.wait_ge(xst_sb, t)
                for k in range(KC):
                    mm = pe.transpose(XB[:, k * 128:(k + 1) * 128], xs[:, p, k * 128:(k + 1) * 128], ident[:])
                mm.then_inc(xst_pe, 1)

            def gate_up(t, p, e, early):
                pe.wait_ge(xst_sb, t + 1)
                if not early:
                    pe.wait_ge(h_sb, t - 1)
                for part, bk in ((0, GB[p]), (1, UB[p])):
                    for k in range(KC):
                        mm = pe.matmul(bk[:, :], xsT[:, p, k, :], ug[:, e, k, part * HID:(part + 1) * HID],
                                       start=(k == 0), stop=(k == KC - 1))
                mm.then_inc(gu_pe, 1)

            def turn_h(t, p, first):
                pe.wait_ge(h_sb, t + 1)
                if not first:
                    pe.wait_ge(ht_sb, t)
                for m in range(HT):
                    mm = pe.transpose(HB[:, m * 128:(m + 1) * 128], hr[:, p, m * 128:(m + 1) * 128], ident[:])
                mm.then_inc(ht_pe, 1)

            def down(t, p, e, first):
                pe.wait_ge(ht_sb, t + 1)
                if not first:
                    pe.wait_ge(yr_sb, t)
                for m in range(HT):
                    mm = pe.matmul(YB[:, 0:C], hrT[:, p, m, :], dn[:, e, m, :], start=(m == 0), stop=(m == HT - 1))
                mm.then_inc(yr_pe, 1)

            def expert_of(t):
                return pe.value_load(expert[0:1, bass.ds(t, 1)], min_val=0, max_val=E - 1)

            last = ROUTED_TILES - 1
            head_tile(0, 0, 0, True)
            e = expert_of(0)
            gate_up(0, 0, e, True)
            head_tile(1, 1, 0, False)
            gate_up(1, 1, expert_of(1), True)
            turn_h(0, 0, True)
            head_tile(2, 0, 1, False)
            down(0, 0, expert_of(0), True)

            def step(t, p, i):
                gate_up(t + 1, 1 - p, expert_of(t + 1), False)
                turn_h(t, p, False)
                head_tile(t + 2, p, i + 1, False)
                down(t, p, expert_of(t), False)

            with pe.Fori(0, (ROUTED_TILES - 4) // 2) as i:
                step(i * 2 + 1, 1, i)
                step(i * 2 + 2, 0, i + 1)
            t = last - 2
            step(t, t % 2, t // 2)
            gate_up(last, 1, expert_of(last), False)
            turn_h(last - 1, 0, False)
            down(last - 1, 0, expert_of(last - 1), False)
            turn_h(last, 1, False)
            down(last, 1, expert_of(last), False)


        @block.scalar
        def _(act):
            def evac_v(c, b, p, first):
                act.wait_ge(proj1[c], b + 1)
                if not first:
                    act.wait_ge(pv1[3], b - 1)
                act.activation(v1[p][:, 512 * c:512 * (c + 1)], PE_J1[c][0:S, :], ACT.Copy).then_inc(evac1[c], 1)

            def exps(g, b, first):
                act.wait_ge(max1[g], b + 1)
                if not first:
                    act.wait_ge(turn1[g], b)
                for n in range(G1):
                    h = G1 * g + n
                    e = act.activation(p1[g][:, n, :], PE_S1[g % 2][0:S, n * S:(n + 1) * S], ACT.Exp,
                                       bias=nm1[:, h:h + 1], accum_out=rs1[:, h:h + 1])
                e.then_inc(exp1[g], 1)

            def evac_o(half, b, p, early):
                act.wait_ge(pv1[2 * half + 1], b + 1)
                if half == 0 and not early:
                    act.wait_ge(wout1, b - 1)
                act.activation(oT1[p][:, 4 * half:4 * half + 4, :],
                               PE_U1[half][:, 0:4 * S].rearrange("p (k n) -> p k n", k=4), ACT.Copy).then_inc(ot1[half], 1)

            for c in range(2):
                evac_v(c, 0, 0, True)

            def stage1(b, p, i, first, last):
                early = isinstance(b, int) and b < 2
                exps(0, b, first)
                exps(1, b, first)
                if not last:
                    evac_v(0, b + 1, 1 - p, first)
                exps(2, b, first)
                if not last:
                    evac_v(1, b + 1, 1 - p, first)
                exps(3, b, first)
                evac_o(0, b, p, early)
                evac_o(1, b, p, early)

            over_batches(act, stage1)

            def evac_k(m, b, p, first):
                act.wait_ge(k_pe[m], b + 1)
                if m == 0 and not first:
                    act.wait_ge(scores2[3], heads_done(b - 2, H - 1))
                act.activation(kT2[:, p, m, :], PE_J2[:, 0:S2], ACT.Identity, bias=cols[:, 1, m:m + 1]).then_inc(k_sb[m], 1)

            def exps2(h, b, first):
                act.wait_ge(max2[h % 4], heads_done(b, h))
                if h >= 3:
                    act.wait_ge(turn2[(h - 3) % 4], heads_done(b, h - 3))
                elif not first:
                    act.wait_ge(turn2[(max(j for j in range(H) if j % 3 == h)) % 4], heads_done(b - 1, max(j for j in range(H) if j % 3 == h)))
                act.activation(p2[:, h % 3, :], PE_S2[h % 3][0:S, 0:S2], ACT.Exp, bias=nm2[:, h:h + 1]).then_inc(exp2[h % 4], 1)

            def evac_pt(h, b, first):
                act.wait_ge(turn2[h % 4], heads_done(b, h))
                if h >= 2:
                    act.wait_ge(pv2_last[(h - 2) % 4], heads_done(b, h - 2))
                elif not first:
                    act.wait_ge(pv2_last[(H - 2 + h) % 4], heads_done(b - 1, H - 2 + h))
                act.activation(pT2[:, h % 2], PE_T2[h % 2][0:SK, 0:KT * S].rearrange("p (k n) -> p k n", k=KT),
                               ACT.Copy).then_inc(pt2[h % 4], 1)

            def turn_evac(kind, b, p):
                if kind == "x1":
                    act.wait_ge(x1t_pe, b + 1)
                    act.activation(x1T[:], PE_M2[:, 0:KC * S].rearrange("p (k n) -> p k n", k=KC), ACT.Copy).then_inc(x1t_sb, 1)
                if kind == "on":
                    act.wait_ge(ont_pe, b + 1)
                    act.activation(on2T[:], PE_M2[:, 0:KC * S].rearrange("p (k n) -> p k n", k=KC), ACT.Copy).then_inc(ont_sb, 1)
                if kind == "x2":
                    act.wait_ge(x2t_pe, b + 1)
                    act.activation(x2T[:, :, bass.ds(b * S, S)], PE_M2[:, 0:KC * S].rearrange("p (k n) -> p k n", k=KC),
                                   ACT.Copy).then_inc(x2t_sb, 1)

            act.wait_ge(w_loaded["small"], 16 * 10)
            turn_evac("x1", 0, 0)
            for m in range(KC):
                evac_k(m, 0, 0, True)

            def stage2(b, p, i, first, last):
                for h in range(H + 3):
                    if h < H:
                        exps2(h, b, first)
                    if not last:
                        if h == 1:
                            turn_evac("x1", b + 1, 1 - p)
                        if h in (6, 8):
                            evac_k((h - 6) // 2, b + 1, 1 - p, first)
                    if not first:
                        if h == 7:
                            turn_evac("on", b - 1, 1 - p)
                        if h == 15:
                            turn_evac("x2", b - 1, 1 - p)
                    if 2 <= h < H + 2 and h % 2 == 0:
                        evac_pt(h - 2, b, first)

            over_batches(act, stage2)
            turn_evac("on", B - 1, 1)
            turn_evac("x2", B - 1, 1)

            for n in range(2 * HT):
                act.wait_ge(sh_gu, n + 1)
                if n >= 1:
                    act.wait_ge(sh_h, n)
                act.activation(gs[:], bank[2 + 2 * (n % 2)][:, 0:4 * S], ACT.Silu).then_inc(sh_g, 1)

            def tile(t, p, first):
                act.wait_ge(gu_pe, t + 1)
                if not first:
                    act.wait_ge(h_sb, t)
                act.activation(gr[:], bank[2 + p][:], ACT.Silu).then_inc(g_sb, 1)
                act.wait_ge(ht_pe, t + 1)
                act.activation(hrT[:, p], bank[1][:].rearrange("p (k n) -> p k n", k=HT), ACT.Copy).then_inc(ht_sb, 1)

            def tile_ahead(t, p):
                act.wait_ge(gu_pe, t + 2)
                act.wait_ge(h_sb, t + 1)
                act.activation(gr[:], bank[2 + 1 - p][:], ACT.Silu).then_inc(g_sb, 1)
                act.wait_ge(ht_pe, t + 1)
                act.activation(hrT[:, p], bank[1][:].rearrange("p (k n) -> p k n", k=HT), ACT.Copy).then_inc(ht_sb, 1)

            act.wait_ge(gu_pe, 1)
            act.wait_ge(sh_h, 2 * HT)
            act.activation(gr[:], bank[2][:], ACT.Silu).then_inc(g_sb, 1)
            tile_ahead(0, 0)
            with act.Fori(0, (ROUTED_TILES - 2) // 2) as i:
                tile_ahead(i * 2 + 1, 1)
                tile_ahead(i * 2 + 2, 0)
            act.wait_ge(ht_pe, ROUTED_TILES)
            act.activation(hrT[:, 1], bank[1][:].rearrange("p (k n) -> p k n", k=HT), ACT.Copy).then_inc(ht_sb, 1)

        @block.vector
        def _(v):
            v.wait_ge(w_loaded["mask"], 16)
            v.tensor_scalar(mask0[:], mask_i[:], 0.0, None, ALU.is_equal).then_inc(prep, 1)
            v.wait_ge(prep, 1)
            v.tensor_reduce(allm[:], mask0[:], AX.X, ALU.min).then_inc(prep, 1)
            v.wait_ge(prep, 2)
            v.tensor_scalar(anym[:], allm[:], -1.0, 1.0, ALU.mult, ALU.add).then_inc(prep, 1)
            v.wait_ge(prep, 3)
            v.wait_ge(consts, 6)
            v.tensor_scalar(anyw[:], ones[:], anym[:], None, ALU.mult).then_inc(prep, 1)
            v.tensor_scalar(bias[:], mask0[:], anym[:], MASKED, ALU.mult, ALU.mult).then_inc(prep, 1)
            by_parity = ident[:].rearrange("p (g j d) -> p g j d", j=2, d=D2)
            for j in range(2):
                v.tensor_reduce(halves[:, j:j + 1], by_parity[:, :, j, :], AX.XY, ALU.add).then_inc(prep, 1)

            def evac_qk(c, b, p, first):
                v.wait_ge(proj1[c], b + 1)
                if not first:
                    v.wait_ge(scores1[3], b - 1)
                dst = (qT if c < 4 else kT)[p][:, 4 * (c % 2):4 * (c % 2) + 4, :]
                v.tensor_scalar(dst, PE_J1[c % 2][:, 0:4 * S].rearrange("p (k n) -> p k n", k=4),
                                D1 ** -0.5 if c < 4 else 1.0, None, ALU.mult).then_inc(evac1[c], 1)

            def rowmax(g, b, first):
                v.wait_ge(scores1[g], b + 1)
                if not first:
                    v.wait_ge(exp1[g], b)
                v.tensor_reduce(nm1[:, G1 * g:G1 * g + G1], PE_S1[g % 2][0:S, 0:G1 * S].rearrange("p (k n) -> p k n", k=G1),
                                AX.X, ALU.max, negate=True).then_inc(max1[g], 1)

            def normalise(g, b):
                c = slice(G1 * g, G1 * g + G1)
                v.wait_ge(exp1[g], b + 1)
                v.reciprocal(rc1[:, c], rs1[:, c]).then_inc(rcp1, 1)
                v.wait_ge(rcp1, b * 4 + (g + 1))
                v.tensor_tensor(p1[g], p1[g], rc1[:, c].unsqueeze(2).to_broadcast([S, G1, S]), ALU.mult).then_inc(norm1[g], 1)

            def evac_pt(g, b, first):
                v.wait_ge(turn1[g], b + 1)
                if g >= 2:
                    v.wait_ge(pv1[g - 2], b + 1)
                elif not first:
                    v.wait_ge(pv1[g + 2], b)
                v.tensor_copy(pT1[g % 2], PE_T1[0:S, 0:G1 * S].rearrange("p (k n) -> p k n", k=G1)).then_inc(pt1[g], 1)

            def layernorm_a(src, done, added, b, p, sy, ss, sa, sv):
                v.wait_ge(done, b + 1)
                v.wait_ge(added, b + 1)
                v.tensor_tensor(ybuf[:, p], src, xb[:, p], ALU.add).then_inc(sy, 1)
                v.wait_ge(sy, b + 1)
                v.bn_stats(stats[:, p], ybuf[:, p]).then_inc(ss, 1)
                v.wait_ge(ss, b + 1)
                v.sem_inc(pause, 1)
                v.bn_aggr(mv[:, p], stats[:, p]).then_inc(sa, 1)
                v.wait_ge(sa, b + 1)
                v.tensor_scalar(veps[:, p:p + 1], mv[:, p, 1:2], EPS, None, ALU.add).then_inc(sv, 1)

            def ln1_a(b, p):
                layernorm_a(PE_W1[0:S, 0:C], wout1, xb1, b, p, y1, st1, ag1, ve1)

            def ln1_b(b, p):
                v.wait_ge(rstd1, b + 1)
                v.tensor_scalar(xres[:, b], ybuf[:, p], mv[:, p, 0:1], rstd[:, p:p + 1], ALU.subtract, ALU.mult).then_inc(x1_done, 1)

            for c in range(2, 6):
                evac_qk(c, 0, 0, True)

            def stage1(b, p, i, first, last):
                rowmax(0, b, first)
                rowmax(1, b, first)
                if not first:
                    ln1_a(b - 1, 1 - p)
                normalise(0, b)
                rowmax(2, b, first)
                normalise(1, b)
                rowmax(3, b, first)
                if not first:
                    ln1_b(b - 1, 1 - p)
                evac_pt(0, b, first)
                if not last:
                    evac_qk(2, b + 1, 1 - p, first)
                normalise(2, b)
                evac_pt(1, b, first)
                if not last:
                    evac_qk(3, b + 1, 1 - p, first)
                normalise(3, b)
                evac_pt(2, b, first)
                if not last:
                    evac_qk(4, b + 1, 1 - p, first)
                evac_pt(3, b, first)
                if not last:
                    evac_qk(5, b + 1, 1 - p, first)

            over_batches(v, stage1)
            ln1_a(B - 1, 1)
            ln1_b(B - 1, 1)
            v.wait_ge(q_any, 1)
            for j in range(2):
                v.tensor_scalar(qscale[:, j, :], PE_J2[:, 0:S], halves[:, j:j + 1], D2 ** -0.5, ALU.mult, ALU.mult).then_inc(prep, 1)

            def evac_q(b, p, first):
                v.wait_ge(q_pe, b + 1)
                if not first:
                    v.wait_ge(scores2[3], heads_done(b - 2, H - 1))
                for m in range(KC):
                    for j in range(2):
                        last = v.scalar_tensor_tensor(out=qm[:, p, m, j, :], in0=PE_M2[:, m * S:(m + 1) * S],
                                                      scalar=cols[:, 0, m:m + 1], in1=qscale[:, j, :], op0=ALU.add, op1=ALU.mult)
                last.then_inc(q_sb, 1)

            def evac_v(t, b, p, first):
                v.wait_ge(v_pe[t], b + 1)
                if not first:
                    v.wait_ge(pv2_last[3], heads_done(b - 2, H - 1))
                v.tensor_tensor(v2[:, p, t, :, 0:D2], PE_J2[0:SK, 0:C].rearrange("p (h d) -> p h d", h=H),
                                rows[0:SK, 1, :].rearrange("p (h d) -> p h d", h=H), ALU.add).then_inc(v_sb[t], 1)

            def rowmax2(h, b, first):
                v.wait_ge(scores2[h % 4], heads_done(b, h))
                if not first:
                    v.wait_ge(exp2[h % 4], heads_done(b - 1, h))
                v.tensor_reduce(nm2[:, h:h + 1], PE_S2[h % 3][0:S, 0:S2], AX.X, ALU.max, negate=True).then_inc(max2[h % 4], 1)

            def evac_pt2(h, b, first):
                v.wait_ge(turn2[h % 4], heads_done(b, h))
                if h >= 2:
                    v.wait_ge(pv2_last[(h - 2) % 4], heads_done(b, h - 2))
                elif not first:
                    v.wait_ge(pv2_last[(H - 2 + h) % 4], heads_done(b - 1, H - 2 + h))
                v.tensor_copy(pT2[:, h % 2], PE_T2[h % 2][0:SK, 0:KT * S].rearrange("p (k n) -> p k n", k=KT)).then_inc(pt2[h % 4], 1)

            def evac_ot(b, first):
                v.wait_ge(pv2_last[3], heads_done(b, H - 1))
                if not first:
                    v.wait_ge(on_pe, b)
                v.tensor_copy(oT2[:], PE_V2[:, 0:4 * S].rearrange("p (k n) -> p k n", k=4)).then_inc(ot2, 1)

            def normalise2(b):
                o = PE_M2[0:S, :].rearrange("p (h d) -> p h d", h=H)
                v.wait_ge(on_pe, b + 1)
                v.reciprocal(rc2[:].unsqueeze(2), o[:, :, D2:D2 + 1]).then_inc(rc_done, 1)
                v.wait_ge(rc_done, b + 1)
                v.tensor_tensor(o2[:].rearrange("p (h d) -> p h d", h=H), o[:, :, 0:D2],
                                rc2[:].unsqueeze(2).to_broadcast([S, H, D2]), ALU.mult).then_inc(on_sb, 1)

            def ln2_a(b, p):
                layernorm_a(PE_M2[0:S, 0:C], wo_pe, xb2, b, p, y2, st2, ag2, ve2)

            def ln2_b(b, p, early):
                v.wait_ge(rstd2, b + 1)
                if not early:
                    v.wait_ge(x2t_pe, b - 1)
                    v.wait_ge(x2_kept, b - 1)
                v.tensor_scalar(x2c[:, p], ybuf[:, p], mv[:, p, 0:1], rstd[:, p:p + 1], ALU.subtract, ALU.mult).then_inc(x2_done, 1)

            v.wait_ge(prep, 9)
            v.wait_ge(v2_ones, 2)
            evac_q(0, 0, True)
            for t in range(KT):
                evac_v(t, 0, 0, True)

            def stage2(b, p, i, first, last):
                for h in range(H + 3):
                    if h < H:
                        rowmax2(h, b, first)
                    if not last:
                        if h == 5:
                            evac_q(b + 1, 1 - p, first)
                        if h in (10, 12, 14):
                            evac_v((h - 10) // 2, b + 1, 1 - p, first)
                    if not first:
                        if h == 3:
                            normalise2(b - 1)
                        if h == 9:
                            ln2_a(b - 1, 1 - p)
                        if h == 11:
                            ln2_b(b - 1, 1 - p, isinstance(b, int) and b <= 2)
                    if 2 <= h < H + 2 and h % 2 == 1:
                        evac_pt2(h - 2, b, first)
                evac_ot(b, first)

            over_batches(v, stage2)
            normalise2(B - 1)
            ln2_a(B - 1, 1)
            ln2_b(B - 1, 1, False)

            n = [0]

            def chain(ins):
                n[0] += 1
                ins.then_inc(s_route, 1)
                v.wait_ge(s_route, n[0])

            v.wait_ge(s_logit, 1)
            chain(v.tensor_copy(logit[:], bank[0][0:S, 0:B * E].rearrange("p (b e) -> p b e", b=B)))
            for b in range(B):
                m = v.max(top8[:, b], logit[:, b])
            chain(m)
            for b in range(B):
                m = v.max_index(tidx[:, b], top8[:, b], logit[:, b])
            chain(m)
            v.wait_ge(consts, 10)
            chain(v.tensor_tensor(onehot[:], eidx[0:S].unsqueeze(1).to_broadcast([S, B, E]),
                                  tidx[:, :, 0:1].to_broadcast([S, B, E]), ALU.is_equal))
            assert n[0] == ROUTE_ONEHOT
            def shared_product(k):
                v.wait_ge(sh_g, k + 1)
                v.tensor_tensor(hTs[:, k % HT, :], gs[:], bank[3 + 2 * (k % 2)][:, 0:4 * S], ALU.mult).then_inc(sh_h, 1)

            shared_product(0)
            v.wait_ge(s_incl, 1)
            chain(v.tensor_copy(incl[:], bank[1][0:S, 0:B * E].rearrange("p (b e) -> p b e", b=B)))
            v.memset(cnt[:, 0, :], 0.0)
            chain(v.memset(ends[:, 0:1], 0.0))
            for b in range(B):
                chain(v.tensor_tensor(cnt[:, b + 1, :], bank[1][:, (B + b) * E:(B + b + 1) * E], cnt[:, b, :], ALU.add))
            shared_product(1)
            chain(v.tensor_tensor(fills[:], steps7[:].unsqueeze(1).to_broadcast([128, E, 7]),
                                  cnt[:, B, :].unsqueeze(2).to_broadcast([128, E, 7]), ALU.is_lt))
            chain(v.tensor_reduce(ntile[:], fills[:], AX.X, ALU.add))
            for e in range(E):
                if e == 0:
                    v.tensor_copy(ends[:, 1:2], ntile[:, 0:1]).then_inc(s_eload, 1)
                else:
                    v.wait_ge(s_eload, e)
                    v.tensor_tensor(ends[:, e + 1:e + 2], ends[:, e:e + 1], ntile[:, e:e + 1], ALU.add).then_inc(s_eload, 1)
            v.wait_ge(s_eload, E)
            chain(v.tensor_tensor(pos[:], incl[:], cnt[0:S, 0:B, :], ALU.add))
            chain(v.scalar_tensor_tensor(out=incl[:], in0=ends[0:S, 0:E].unsqueeze(1).to_broadcast([S, B, E]), scalar=float(TILE),
                                         in1=pos[:], op0=ALU.mult, op1=ALU.add))
            chain(v.tensor_tensor(pos[:], incl[:], onehot[:], ALU.mult))
            chain(v.tensor_reduce(slotf[:], pos[:], AX.X, ALU.add))
            chain(v.tensor_scalar(slot[:], slotf[:], -1.0, None, ALU.add))
            assert n[0] == ROUTE_SLOTS
            chain(v.tensor_tensor(past[:], tiles_i[:].unsqueeze(2).to_broadcast([1, ROUTED_TILES, E - 1]),
                                  ends[0:1, 1:E].unsqueeze(1).to_broadcast([1, ROUTED_TILES, E - 1]), ALU.is_ge))
            chain(v.tensor_reduce(expertf[:], past[:], AX.X, ALU.add))
            chain(v.tensor_copy(expert[:], expertf[:]))
            assert n[0] == ROUTE_EXPERTS

            def shared_sum(b):
                v.wait_ge(sh_y, b + 1)
                v.tensor_tensor(ysh[:, b], bank[6 + b % 2][0:S, 0:C], xres[:, b], ALU.add).then_inc(sh_ysb, 1)

            v.wait_ge(x2_kept, B)
            shared_product(2)
            shared_product(3)
            for b in range(4):
                shared_sum(b)
            for k in range(4, 8):
                if k == 4:
                    v.wait_ge(sh_y, 4)
                shared_product(k)
            for b in range(4, B):
                shared_sum(b)

            def evac_x(t, p, early):
                v.wait_ge(xst_pe, t + 1)
                if not early:
                    v.wait_ge(gu_pe, t - 1)
                v.tensor_copy(xsT[:, p], bank[0][:, 0:KC * 128].rearrange("p (k n) -> p k n", k=KC)).then_inc(xst_sb, 1)

            def product(t, p, early):
                v.wait_ge(g_sb, t + 1)
                if not early:
                    v.wait_ge(ht_pe, t - 1)
                v.tensor_tensor(hr[:, p], gr[:], bank[4 + p][:], ALU.mult).then_inc(h_sb, 1)

            def evac_y(t, p, i, early):
                v.wait_ge(yr_pe, t + 1)
                if not early:
                    v.wait_ge(ys_stored[p], i * 16)
                v.tensor_copy(yr[:, p], bank[6][:, 0:C]).then_inc(yr_sb, 1)

            evac_x(0, 0, True)
            product(0, 0, True)
            evac_x(1, 1, True)
            product(1, 1, True)
            evac_x(2, 0, False)
            evac_y(0, 0, 0, True)
            product(2, 0, False)
            evac_x(3, 1, False)
            evac_y(1, 1, 0, True)

            with v.Fori(1, (ROUTED_TILES - 2) // 2) as i:
                for p in range(2):
                    product(i * 2 + 1 + p, 1 - p, False)
                    evac_x(i * 2 + 2 + p, p, False)
                    evac_y(i * 2 + p, p, i, False)
            product(ROUTED_TILES - 1, 1, False)
            evac_y(ROUTED_TILES - 2, 0, ROUTED_TILES // 2 - 1, False)
            evac_y(ROUTED_TILES - 1, 1, ROUTED_TILES // 2 - 1, False)

            f = [0]

            def fchain(ins):
                f[0] += 1
                ins.then_inc(fin, 1)
                v.wait_ge(fin, f[0])

            def final(b):
                v.wait_ge(rstd3, b + 1)
                v.tensor_scalar(ygat[:, b], ysh[:, b], mv3[:, b, 0:1], rs3[:, b:b + 1], ALU.subtract, ALU.mult).then_inc(done3, 1)

            v.wait_ge(gathered, 16 * B)
            for b in range(B):
                fchain(v.tensor_tensor(ysh[:, b], ysh[:, b], ygat[:, b], ALU.add))
                fchain(v.bn_stats(st3[:, b], ysh[:, b]))
                fchain(v.bn_aggr(mv3[:, b], st3[:, b]))
                v.tensor_scalar(ve3[:, b:b + 1], mv3[:, b, 1:2], EPS, None, ALU.add).then_inc(ve3s, 1)
                if b >= 1:
                    final(b - 1)
            final(B - 1)


def kernel(**inputs):
    import numpy as np
    import concourse.bacc as bacc
    from concourse.bass_utils import run_bass_kernel_spmd

    g = {k: np.asarray(v) for k, v in inputs.items()}

    def tiles(w):
        return np.ascontiguousarray(w.reshape(-1, 128, w.shape[1]).transpose(1, 0, 2))

    def per_batch(x):
        return np.ascontiguousarray(x.transpose(0, 2, 1).reshape(B, KC, 128, -1).transpose(0, 2, 1, 3))

    gates = list(g["L0_ffn_gate"]) + [g["L0_ffn_w_gate_s"]]
    ups = list(g["L0_ffn_up"]) + [g["L0_ffn_w_up_s"]]
    downs = list(g["L0_ffn_down"]) + [g["L0_ffn_w_down_s"]]
    arrays = {
        "xT": per_batch(g["x"]),
        "x": np.ascontiguousarray(g["x"].transpose(1, 0, 2)),
        "ctxT": per_batch(g["ctx_1024"]),
        "mask": np.ascontiguousarray(g["mask_1x1xSxS2_ik0"].reshape(S, S2)),
        "wqkv": tiles(g["L0_attn_w_qkv"]),
        "wout": tiles(g["L0_attn_w_out"]),
        "b_out": g["L0_attn_b_out"].reshape(1, C),
        "bv": g["L0_xattn_bv"].reshape(1, C),
        "bo": g["L0_xattn_bo"].reshape(1, C),
        "bq": np.ascontiguousarray(g["L0_xattn_bq"].reshape(KC, 128).T),
        "bk": np.ascontiguousarray(g["L0_xattn_bk"].reshape(KC, 128).T),
        "router": tiles(g["L0_ffn_router"].T),
        "wq": tiles(g["L0_xattn_Wq"].T),
        "wk": tiles(g["L0_xattn_Wk"].T),
        "wv": tiles(g["L0_xattn_Wv"].T),
        "wo": tiles(g["L0_xattn_Wo"].T),
        "ug": np.stack([tiles(np.concatenate([a, b]).T) for a, b in zip(gates, ups)]),
        "dn": np.stack([tiles(d.T) for d in downs]),
    }
    nc = bacc.Bacc("TRN2", target_bir_lowering=False, num_devices=1)
    aps = {n: nc.dram_tensor("in_" + n, v.shape, dt.from_np(v.dtype), kind="ExternalInput").ap() for n, v in arrays.items()}
    out = nc.dram_tensor("out_x", (B, S, C), F32, kind="ExternalOutput").ap()
    build(nc, aps, out)
    r = run_bass_kernel_spmd(nc, [{"in_" + n: v for n, v in arrays.items()}], core_ids=[0])
    return r.results[0]["out_x"]
```

```python
from contextlib import ExitStack

import concourse.bass as bass
from concourse import mybir

dt = mybir.dt
F32, F32R, BF16, I32, U32 = dt.float32, dt.float32r, dt.bfloat16, dt.int32, dt.uint32
ALU = mybir.AluOpType
ACT = mybir.ActivationFunctionType
AX = mybir.AxisListType

B, S, C = 8, 112, 256
KC = C // 128
H = 16
D1 = 64
INNER = H * D1
G1 = 4
S2 = 375
KT = 3
SK = S2 // KT
D2 = C // H
VP = 32
E, HID = 8, 512
HT = HID // 128
T = B * S
TILE = 128
ROUTED_TILES = (T - E) // TILE + E
EPS = 1e-5
MASKED = 1e30
S2P = S2 + 1
PAIRS_H = H // 2
PARTS_K, PARTS_Q = (0, 1, 0, 1), (0, 0, 1, 1)
STACK_DMAS = len(PARTS_K) * 2
LAG = 3
PT_RING = 8
FEWEST_PAIRS = (T + 2 * TILE - 1) // (2 * TILE)
EXTRA_PAIRS = ROUTED_TILES // 2 - FEWEST_PAIRS
PAIRS = B // 2


def build(nc, a, out):
    ctx = ExitStack()
    with ctx:
        def sb(name, shape, d=F32):
            return ctx.enter_context(nc.sbuf_tensor(name, shape, d))

        def sem(name):
            return ctx.enter_context(nc.semaphore(name))

        def sems(name, n):
            return [sem(f"{name}_{j}") for j in range(n)]

        bank = [ctx.enter_context(nc.psum_tensor(f"bank{j}", [128, 512], F32)) for j in range(8)]
        slots_x = nc.dram_tensor("slots_x", (ROUTED_TILES * TILE, C), F32, kind="Internal").ap()
        slots_y = nc.dram_tensor("slots_y", (ROUTED_TILES * TILE, C), F32, kind="Internal").ap()

        k_parts = nc.dram_tensor("k_parts", (2, 2, C, S2P), F32, kind="Internal").ap()
        q_parts = nc.dram_tensor("q_parts", (2, 2, C, S), F32, kind="Internal").ap()

        ident = sb("ident", [128, 128])
        minus_half = sb("minus_half", [S, 1])
        xres = sb("xres", [S, B, C])
        x2T = sb("x2T", [128, KC, T])
        wx = sb("wx", [128, 4, KC, C])
        cols = sb("cols", [128, 2, KC])
        rows = sb("rows", [128, 3, C])
        ybuf = sb("ybuf", [S, 2, C])
        stats = sb("stats", [S, 2, 6])
        mv = sb("mv", [S, 2, 2])
        veps = sb("veps", [S, 2])
        rstd = sb("rstd", [S, 2])
        xb = sb("xb", [S, 2, C])
        ugs = sb("ugs", [128, KC, 2 * HID])
        dns = sb("dns", [128, HT, C])
        zeros = sb("zeros", [128, C])

        UG, DN = KC * 2 * HID, HT * C
        ARENA = E * (UG + DN)
        with ExitStack() as upper:
            upper.enter_context(nc.sbuf_tensor("lower_half", [128, ARENA // 2], F32))
            kst = upper.enter_context(nc.sbuf_tensor("kst", [128, 2, PAIRS_H, S2P], F32R))
            qst = upper.enter_context(nc.sbuf_tensor("qst", [128, 2, PAIRS_H, S], F32R))
            p2_more = upper.enter_context(nc.sbuf_tensor("p2_more", [S, 4, S2], F32))
            pT2 = upper.enter_context(nc.sbuf_tensor("pT2", [128, PT_RING, KT, S], F32))
        arena = sb("arena", [128, ARENA])
        top = [0]

        def carve(n):
            top[0] += n
            assert top[0] <= ARENA // 2 or top[0] - n >= ARENA // 2 and top[0] <= ARENA
            return arena[:, top[0] - n:top[0]]

        wout = carve(INNER // 128 * C).rearrange("p (k n) -> p k n", n=C)
        v1 = [carve(INNER)[0:S] for _ in range(2)]
        qT = [carve(8 * S).rearrange("p (k n) -> p k n", k=8) for _ in range(2)]
        kT = [carve(8 * S).rearrange("p (k n) -> p k n", k=8) for _ in range(2)]
        p1 = [carve(G1 * S)[0:S].rearrange("p (k n) -> p k n", k=G1) for _ in range(4)]
        pT1 = [carve(G1 * S)[0:S].rearrange("p (k n) -> p k n", k=G1) for _ in range(2)]
        oT1 = [carve(8 * S).rearrange("p (k n) -> p k n", k=8) for _ in range(2)]
        top[0] = ARENA // 2
        wqkv = carve(KC * 3 * INNER).rearrange("p (k n) -> p k n", k=KC)
        xT = [carve(KC * S).rearrange("p (k n) -> p k n", k=KC) for _ in range(2)]
        by_expert = arena[:, :].rearrange("p (e n) -> p e n", e=E)
        ug = by_expert[:, :, 0:UG].rearrange("p e (k n) -> p e k n", k=KC)
        dn = by_expert[:, :, UG:UG + DN].rearrange("p e (k n) -> p e k n", k=HT)
        nm1 = sb("nm1", [S, H])
        rs1 = sb("rs1", [S, H])
        rc1 = sb("rc1", [S, H])

        mid = sb("mid", [128, 1, 2 * KC * S2])
        ctxT = mid[:, 0, :].rearrange("p (b k n) -> p b k n", b=2, k=KC)
        k_hl = sb("k_hl", [128, 2, KC, S2P], F32R)
        q_hl = sb("q_hl", [128, 2, KC, S], F32R)
        v2_all = sb("v2", [128, 2 * KT * H * VP])
        v2 = v2_all[0:SK, :].rearrange("p (b k h d) -> p b k h d", b=2, k=KT, h=H)
        qf = sb("qf", [128, KC, S])
        qscale = sb("qscale", [128, S])
        x1c = sb("x1c", [S, 2, C])
        x1T = sb("x1T", [128, KC, S])
        p2_all = sb("p2", [128, 4 * S2])
        p2 = [p2_all[0:S, j * S2:(j + 1) * S2] for j in range(4)] + [p2_more[:, j, :] for j in range(4)]
        nm2 = sb("nm2", [S, H])
        oT2 = sb("oT2", [128, 4, S])
        o2 = sb("o2", [S, C])
        rc2 = sb("rc2", [S, H])
        on2T = sb("on2T", [128, KC, S])
        mask_i = sb("mask_i", [S, S2], I32)
        mask0 = sb("mask0", [S, S2])
        allm = sb("allm", [S, 1])
        anym = sb("anym", [S, 1])
        anyw = sb("anyw", [S, 128])
        bias = mask0
        x2c = sb("x2c", [S, 2, C])

        hTs = sb("hTs", [128, HT, 4 * S])
        gs = sb("gs", [128, 4 * S])
        routerT = sb("routerT", [128, KC, E])
        upto = sb("upto", [S, S])
        ones = sb("ones", [S, 128])
        logit = sb("logit", [S, B, E])
        top8 = sb("top8", [S, B, 8])
        tidx = sb("tidx", [S, B, 8], U32)
        choice = sb("choice", [S, B])
        onehot = sb("onehot", [S, B, E])
        incl = sb("incl", [S, B, E])
        cnt = sb("cnt", [128, B + 1, E])
        fills = sb("fills", [128, E, 7])
        ntile = sb("ntile", [128, E])
        ends = sb("ends", [128, E + 1])
        pos = sb("pos", [S, B, E])
        slotf = sb("slotf", [S, B])
        slot = sb("slot", [S, B], U32)
        steps7 = sb("steps7", [128, 7])
        eidx = sb("eidx", [128, E])
        tiles_i = sb("tiles_i", [1, ROUTED_TILES])
        past = sb("past", [1, ROUTED_TILES, E - 1])
        expertf = sb("expertf", [1, ROUTED_TILES])
        expert = sb("expert", [1, ROUTED_TILES], I32)
        taken = sb("taken", [1, EXTRA_PAIRS])
        extraf = sb("extraf", [1, 1])
        extra_i = sb("extra_i", [1, 1], I32)
        xs = sb("xs", [128, 2, C])
        xsT = sb("xsT", [128, 2, KC, 128])
        lgT = mid[0:E, 0, 0:T]
        hr = mid[:, 0, 0:2 * HID].rearrange("p (b n) -> p b n", b=2)
        hrT = sb("hrT", [128, 2, HT, 128])
        gr = p2_all[:, 2 * C:2 * C + HID]
        yr = p2_all[:, 0:2 * C].rearrange("p (b n) -> p b n", b=2)
        ysh = v2_all[0:S, 0:B * C].rearrange("p (b n) -> p b n", b=B)
        ygat = xres
        mv3 = sb("mv3", [S, B, 2])
        st3 = sb("st3", [S, B, 6])
        ve3 = sb("ve3", [S, B])
        rs3 = sb("rs3", [S, B])

        pause = sem("pause")
        consts = sem("consts")
        w_loaded = {n: sem(f"w_{n}") for n in ("v", "q", "k", "out", "x", "small", "mask", "shared")}
        w_experts = sem("w_experts")
        xT_loaded = sems("xT_loaded", 2)
        zeroed = sem("zeroed")
        proj1 = sems("proj1", 6)
        evac1 = sems("evac1", 6)
        scores1 = sems("scores1", 4)
        max1, norm1, turn1, pt1 = sem("max1"), sem("norm1"), sem("turn1"), sem("pt1")
        exp1 = sems("exp1", 4)
        rcp1 = sem("rcp1")
        pv1 = sems("pv1", 4)
        ot1 = sems("ot1", 2)
        wout1 = sem("wout1")
        xb1 = sem("xb1")
        y1, st1, ag1, ve1, rstd1, x1_done = (sem(n) for n in ("y1", "st1", "ag1", "ve1", "rstd1", "x1_done"))

        ctx_loaded = sems("ctx_loaded", 2)
        prep = sem("prep")
        q_any = sem("q_any")
        v2_ones = sem("v2_ones")
        x1c_done = sem("x1c_done")
        xb2 = sem("xb2")
        x1t_pe, x1t_sb, q_pe, q_sb = (sem(n) for n in ("x1t_pe", "x1t_sb", "q_pe", "q_sb"))
        k_pe, k_hi, k_lo, v_pe, v_sb = sem("k_pe"), sem("k_hi"), sem("k_lo"), sem("v_pe"), sem("v_sb")
        q_hi, q_lo = sem("q_hi"), sem("q_lo")
        k_stored, q_stored = sem("k_stored"), sem("q_stored")
        kst_loaded, qst_loaded = sems("kst_loaded", 2), sems("qst_loaded", 2)
        scores2 = sems("scores2", 4)
        max2 = sems("max2", 4)
        exp2 = sems("exp2", 4)
        turn2 = sems("turn2", 4)
        pt2 = sems("pt2", 4)
        pv2 = sem("pv2")
        ot2 = sem("ot2")
        on_pe, rc_done, on_sb, ont_pe, ont_sb = (sem(n) for n in ("on_pe", "rc_done", "on_sb", "ont_pe", "ont_sb"))
        wo_pe = sem("wo_pe")
        y2, st2, ag2, ve2, rstd2, x2_done, x2_kept = (sem(n) for n in ("y2", "st2", "ag2", "ve2", "rstd2", "x2_done", "x2_kept"))
        x2t_pe, x2t_sb = sem("x2t_pe"), sem("x2t_sb")

        lgt_sb = sem("lgt_sb")
        s_logit, s_route, s_incl, s_eload = sem("s_logit"), sem("s_route"), sem("s_incl"), sem("s_eload")
        sh_gu, sh_g, sh_h, sh_y, sh_ysb = (sem(n) for n in ("sh_gu", "sh_g", "sh_h", "sh_y", "sh_ysb"))
        scattered, gathered = sem("scattered"), sems("gathered", B)
        xs_loaded, ys_stored = sems("xs_loaded", 2), sems("ys_stored", 2)
        xst_pe, xst_sb, gu_pe, g_sb, h_sb, ht_pe, ht_sb, yr_pe, yr_sb = (
            sem(n) for n in ("xst_pe", "xst_sb", "gu_pe", "g_sb", "h_sb", "ht_pe", "ht_sb", "yr_pe", "yr_sb"))
        sum3, stats3, aggr3, ve3s, rstd3, done3, stored = sem("sum3"), sem("stats3"), sem("aggr3"), sem("ve3s"), sem("rstd3"), sem("done3"), sem("stored")

        PE_S1, PE_J1, PE_T1, PE_U1, PE_W1 = bank[0:2], bank[2:4], bank[4], bank[5:7], bank[7]
        PE_S2, PE_T2, PE_V2, PE_M2, PE_J2 = bank[0:3], bank[3:5], bank[5], bank[6], bank[7]

        def head1(g, n):
            return 2 * G1 * (g // 2) + 2 * n + g % 2

        def heads_done(b, h):
            return b * (H // 4) + (h // 4 + 1)

        def over_batches(eng, step):
            for p in range(2):
                step(p, p, 0, p == 0, False)
            with eng.Fori(1, PAIRS - 1) as i:
                for p in range(2):
                    step(i * 2 + p, p, i, False, False)
            for p in range(2):
                step(B - 2 + p, p, PAIRS - 1, False, p == 1)

        def late(b):
            return isinstance(b, int) and b >= B - 2

        def wait_ring(eng, h, b, first):
            if h >= PT_RING:
                eng.wait_ge(pv2, 4 * b + (h - PT_RING) // 4 + 1)
            elif not first:
                eng.wait_ge(pv2, 4 * b + (h + H - PT_RING) // 4 + 1 - 4)

        ROUTE_ONEHOT, ROUTE_SLOTS, ROUTE_EXPERTS = 4, 21, 27
        
        def routed_pairs(eng):
            eng.wait_ge(s_route, ROUTE_EXPERTS)
            return eng.value_load(extra_i[0:1, 0:1], min_val=0, max_val=EXTRA_PAIRS) + FEWEST_PAIRS

        block = ctx.enter_context(nc.Block())

        @block.sync
        def _(sp):
            for p in range(2):
                sp.dma_start(xT[p], a["xT"][p]).then_inc(xT_loaded[p], 16)
            for n, part in (("v", 2), ("q", 0), ("k", 1)):
                cut = slice(part * INNER, (part + 1) * INNER)
                sp.dma_start(wqkv[:, :, cut], a["wqkv"][:, :, cut]).then_inc(w_loaded[n], 16)
            sp.dma_start(wout, a["wout"]).then_inc(w_loaded["out"], 16)
            sp.dma_start(xres[:], a["x"]).then_inc(w_loaded["x"], 16)
            for j, n in enumerate(("b_out", "bv", "bo")):
                sp.dma_start(rows[:, j, :], a[n].to_broadcast([128, C])).then_inc(w_loaded["small"], 16)
            sp.dma_start(mask_i[:], a["mask"]).then_inc(w_loaded["mask"], 16)
            sp.dma_start(cols[:, 0, :], a["bq"]).then_inc(w_loaded["small"], 16)
            sp.dma_start(cols[:, 1, :], a["bk"]).then_inc(w_loaded["small"], 16)
            sp.dma_start(routerT[:], a["router"]).then_inc(w_loaded["small"], 16)
            for j, n in enumerate(("wq", "wk", "wv", "wo")):
                sp.dma_start(wx[:, j], a[n]).then_inc(w_loaded["small"], 16)
            for p in range(2):
                sp.dma_start(ctxT[:, p], a["ctxT"][p]).then_inc(ctx_loaded[p], 16)
            sp.dma_start(ugs[:], a["ug"][E]).then_inc(w_loaded["shared"], 16)
            sp.dma_start(dns[:], a["dn"][E]).then_inc(w_loaded["shared"], 16)

            def load_xT(b, p, i):
                sp.wait_ge(proj1[5], b - 1)
                sp.dma_start(xT[p], a["xT"][b]).then_inc(xT_loaded[p], 16)

            with sp.Fori(1, PAIRS) as i:
                for p in range(2):
                    load_xT(i * 2 + p, p, i)
            sp.wait_ge(consts, 3)
            for t in range(ROUTED_TILES):
                sp.dma_start(slots_x[t * TILE:(t + 1) * TILE, :], zeros[:]).then_inc(zeroed, 16)
            for t in range(2 * FEWEST_PAIRS, ROUTED_TILES):
                sp.dma_start(slots_y[t * TILE:(t + 1) * TILE, :], zeros[:]).then_inc(zeroed, 16)
            def stack(b, p, early):
                sp.wait_ge(q_lo, b + 1)
                sp.dma_start(q_parts[p].rearrange("c (m x) n -> x c m n", x=128), q_hl[:].bitcast(F32)).then_inc(q_stored, 16)
                sp.wait_ge(k_lo, b * KC + KC)
                sp.dma_start(k_parts[p].rearrange("c (m x) n -> x c m n", x=128), k_hl[:].bitcast(F32)).then_inc(k_stored, 16)
                if not early:
                    sp.wait_ge(scores2[3], heads_done(b - 2, H - 1))
                    sp.sem_inc(pause, 1)
                for parts, parts_stored, held, dst, loaded in ((PARTS_Q, q_stored, q_parts, qst, qst_loaded),
                                                               (PARTS_K, k_stored, k_parts, kst, kst_loaded)):
                    sp.wait_ge(parts_stored, (b + 1) * 16)
                    by_head = held[p].rearrange("c (h a r) n -> c a r h n", a=2, r=D2)
                    for copy in range(4):
                        for odd in range(2):
                            to = 64 * odd + D2 * copy
                            sp.dma_start(dst[to:to + D2, p].bitcast(F32), by_head[parts[copy], odd]).then_inc(loaded[p], 16)

            def load_ctx(b, p):
                sp.wait_ge(v_pe, (b - 2) * KT + KT)
                sp.dma_start(ctxT[:, p], a["ctxT"][b]).then_inc(ctx_loaded[p], 16)

            def stage2(b, p, i, first, last):
                if not late(b):
                    load_ctx(b + 2, p)
                    stack(b + 2, p, False)
                if p == 0:
                    sp.dma_start(ug[:, bass.ds(i, 1)], a["ug"][bass.ds(i, 1)].rearrange("e p k n -> p e k n")).then_inc(w_experts, 16)
                else:
                    sp.dma_start(dn[:, bass.ds(i, 1)], a["dn"][bass.ds(i, 1)].rearrange("e p k n -> p e k n")).then_inc(w_experts, 16)

            sp.wait_ge(proj1[5], B)
            for p in range(2):
                stack(p, p, True)
            sp.wait_ge(wout1, B)
            over_batches(sp, stage2)
            sp.wait_ge(pv2, 4 * B)
            for e in range(E // 2, E):
                sp.dma_start(ug[:, e], a["ug"][e]).then_inc(w_experts, 16)
                sp.dma_start(dn[:, e], a["dn"][e]).then_inc(w_experts, 16)

            def load_tile(t, p, first):
                if not first:
                    sp.wait_ge(xst_pe, t - 1)
                sp.dma_start(xs[:, p], slots_x[bass.ds(t * TILE, TILE), :]).then_inc(xs_loaded[p], 16)

            def store_tile(t, p):
                sp.wait_ge(yr_sb, t + 1)
                sp.dma_start(slots_y[bass.ds(t * TILE, TILE), :], yr[:, p]).then_inc(ys_stored[p], 16)

            sp.wait_ge(scattered, 16 * B)
            for p in range(2):
                load_tile(p, p, True)
            pairs = routed_pairs(sp)
            with sp.Fori(0, pairs - 1) as i:
                for p in range(2):
                    load_tile(i * 2 + 2 + p, p, False)
                for p in range(2):
                    store_tile(i * 2 + p, p)
            for p in range(2):
                store_tile(pairs * 2 - 2 + p, p)
            for b in range(B):
                sp.wait_ge(done3, b + 1)
                sp.dma_start(out[b], ygat[:, b]).then_inc(stored, 16)
            sp.wait_ge(stored, 16 * B)

        @block.gpsimd
        def _(g):
            g.memset(ident[:], 0.0).then_inc(consts, 1)
            g.memset(minus_half[:], -0.5).then_inc(consts, 1)
            g.memset(zeros[:], 0.0).then_inc(consts, 1)
            g.wait_ge(consts, 3)
            g.affine_select(out=ident[:], in_=ident[:], compare_op=ALU.not_equal, fill=1.0, base=0,
                            pattern=[[-1, 128]], channel_multiplier=1).then_inc(consts, 1)
            g.wait_ge(consts, 4)
            g.memset(k_hl[:, :, :, S2:S2P].bitcast(F32), 0.0).then_inc(consts, 1)
            g.wait_ge(consts, 5)
            g.memset(ones[:], 1.0).then_inc(consts, 1)
            g.memset(v2_all[:], 0.0).then_inc(v2_ones, 1)
            g.wait_ge(v2_ones, 1)
            g.memset(v2[:, :, :, :, D2:D2 + 1], 1.0).then_inc(v2_ones, 1)
            g.wait_ge(consts, 6)
            g.affine_select(out=upto[:], in_=ones[:, 0:S], compare_op=ALU.is_ge, fill=0.0, base=0,
                            pattern=[[1, S]], channel_multiplier=-1).then_inc(consts, 1)
            g.iota(steps7[:], pattern=[[TILE, 7]], base=0, channel_multiplier=0,
                   allow_small_or_imprecise_dtypes=True).then_inc(consts, 1)
            g.iota(eidx[:], pattern=[[1, E]], base=0, channel_multiplier=0,
                   allow_small_or_imprecise_dtypes=True).then_inc(consts, 1)
            g.iota(tiles_i[:], pattern=[[1, ROUTED_TILES]], base=0, channel_multiplier=0,
                   allow_small_or_imprecise_dtypes=True).then_inc(consts, 1)

            g.wait_ge(w_loaded["x"], 16)
            g.wait_ge(w_loaded["small"], 16 * 10)

            def copy_x1(b, p, first):
                g.wait_ge(x1_done, b + 1)
                if not first:
                    g.wait_ge(x1t_pe, b - 1)
                    g.wait_ge(xb2, b - 1)
                g.sem_inc(pause, 1)
                g.tensor_copy(x1c[:, p], xres[:, b]).then_inc(x1c_done, 1)

            def split_q(b, first):
                g.wait_ge(q_sb, b + 1)
                if not first:
                    g.wait_ge(q_stored, b * 16)
                g.sem_inc(pause, 1)
                g.tensor_copy(q_hl[:, 0], qf[:]).then_inc(q_hi, 1)
                g.wait_ge(q_hi, b + 1)
                g.tensor_tensor(q_hl[:, 1], qf[:], q_hl[:, 0].bitcast(F32), ALU.subtract).then_inc(q_lo, 1)

            def stage1(b, p, i, first, last):
                if not (isinstance(b, int) and b < 2):
                    g.wait_ge(y1, b - 1)
                g.tensor_tensor(xb[:, p], xres[:, b], rows[0:S, 0], ALU.add).then_inc(xb1, 1)
                if last:
                    copy_x1(0, 0, True)
                    split_q(0, True)
                g.wait_ge(ve1, b + 1)
                g.tensor_tensor(rstd[:, p:p + 1], veps[:, p:p + 1], minus_half[:], ALU.pow).then_inc(rstd1, 1)

            over_batches(g, stage1)

            def stage2(b, p, i, first, last):
                g.wait_ge(x1c_done, b + 1)
                if not (isinstance(b, int) and b < 2):
                    g.wait_ge(y2, b - 1)
                g.tensor_tensor(xb[:, p], x1c[:, p], rows[0:S, 2], ALU.add).then_inc(xb2, 1)
                if not late(b):
                    copy_x1(b + 2, p, False)
                    split_q(b + 2, False)
                if not first:
                    tail(b - 1, 1 - p)

            def tail(b, p):
                g.wait_ge(ve2, b + 1)
                g.tensor_tensor(rstd[:, p:p + 1], veps[:, p:p + 1], minus_half[:], ALU.pow).then_inc(rstd2, 1)
                g.wait_ge(x2_done, b + 1)
                g.sem_inc(pause, 1)
                g.tensor_copy(xres[:, b], x2c[:, p]).then_inc(x2_kept, 1)

            copy_x1(1, 1, True)
            split_q(1, False)
            over_batches(g, stage2)
            tail(B - 1, 1)

            g.wait_ge(s_route, ROUTE_SLOTS)
            g.wait_ge(zeroed, 16 * (ROUTED_TILES + 2 * EXTRA_PAIRS))
            g.wait_ge(x2_kept, B)
            for b in range(B):
                g.indirect_dma_start(slots_x, bass.IndirectOffsetOnAxis(slot[:, b:b + 1], 0), xres[:, b], None).then_inc(scattered, 16)
            pairs = routed_pairs(g)
            for p in range(2):
                g.wait_ge(ys_stored[p], pairs * 16)
            g.sem_inc(pause, 1)
            for b in range(B):
                g.indirect_dma_start(ygat[:, b], None, slots_y, bass.IndirectOffsetOnAxis(slot[:, b:b + 1], 0)).then_inc(gathered[b], 16)
            for half in range(2):
                g.wait_ge(ve3s, half + 1)
                cut = slice(4 * half, 4 * half + 4)
                g.tensor_tensor(rs3[:, cut], ve3[:, cut], minus_half[:].to_broadcast([S, 4]), ALU.pow).then_inc(rstd3, 1)


        @block.tensor
        def _(pe):
            pe.wait_ge(consts, 4)

            def project1(c, b, p, i, first):
                if c == 0:
                    pe.wait_ge(xT_loaded[p], (i + 1) * 16)
                if first and c in (0, 2, 4):
                    pe.wait_ge(w_loaded["vqk"[c // 2]], 16)
                if c >= 2:
                    pe.wait_ge(evac1[c - 2], b + 1)
                elif not first:
                    pe.wait_ge(evac1[c + 4], b)
                J = PE_J1[c % 2]
                if c < 2:
                    for k in range(KC):
                        mm = pe.matmul(J[0:S, :], xT[p][:, k, :], wqkv[:, k, 2 * INNER + 512 * c:2 * INNER + 512 * (c + 1)],
                                       start=(k == 0), stop=(k == KC - 1))
                else:
                    for n in range(4):
                        col = (c - 2) * 512 + n * 128
                        for k in range(KC):
                            mm = pe.matmul(J[:, n * S:(n + 1) * S], wqkv[:, k, col:col + 128], xT[p][:, k, :],
                                           start=(k == 0), stop=(k == KC - 1))
                mm.then_inc(proj1[c], 1)

            def score1(g, b, p, first):
                pe.wait_ge(evac1[5 if g >= 2 else 4], b + 1)
                pe.wait_ge(evac1[3 if g >= 2 else 2], b + 1)
                if g >= 2:
                    pe.wait_ge(exp1[g - 2], b + 1)
                elif not first:
                    pe.wait_ge(exp1[g + 2], b)
                for n in range(G1):
                    h = head1(g, n)
                    r = slice(64 * (h % 2), 64 * (h % 2) + 64)
                    mm = pe.matmul(PE_S1[g % 2][0:S, n * S:(n + 1) * S], qT[p][r, h // 2, :], kT[p][r, h // 2, :],
                                   start=True, stop=True)
                mm.then_inc(scores1[g], 1)

            def turn(g, b, first):
                pe.wait_ge(norm1, b * 4 + (g + 1))
                if g >= 1:
                    pe.wait_ge(pt1, b * 4 + g)
                elif not first:
                    pe.wait_ge(pt1, b * 4)
                for n in range(G1):
                    mm = pe.transpose(PE_T1[0:S, n * S:(n + 1) * S], p1[g][:, n, :], ident[0:S, 0:S])
                mm.then_inc(turn1, 1)

            def value1(g, b, p, first):
                pe.wait_ge(pt1, b * 4 + (g + 1))
                if g == 0:
                    pe.wait_ge(evac1[1], b + 1)
                if g % 2 == 0 and not first:
                    pe.wait_ge(ot1[g // 2], b)
                for n in range(G1):
                    h = head1(g, n)
                    col = (h // 2 % 4) * S
                    mm = pe.matmul(PE_U1[g // 2][64 * (h % 2):64 * (h % 2) + 64, col:col + S],
                                   v1[p][:, h * D1:(h + 1) * D1], pT1[g % 2][:, n, :], start=True, stop=True)
                mm.then_inc(pv1[g], 1)

            def out1(b, p, first):
                pe.wait_ge(ot1[1], b + 1)
                pe.wait_ge(ot1[0], b + 1)
                if first:
                    pe.wait_ge(w_loaded["out"], 16)
                else:
                    pe.wait_ge(y1, b)
                    if isinstance(b, int) and b == B - 2:
                        pe.wait_ge(prep, 6)
                for k in range(8):
                    mm = pe.matmul(PE_W1[0:S, 0:C], oT1[p][:, k, :], wout[:, k, :], start=(k == 0), stop=(k == 7))
                mm.then_inc(wout1, 1)

            M = PE_M2

            def turn_x1(b, p, M=PE_M2):
                pe.wait_ge(x1c_done, b + 1)
                for k in range(KC):
                    mm = pe.transpose(M[:, k * S:(k + 1) * S], x1c[:, p, k * 128:(k + 1) * 128], ident[0:S, 0:S])
                mm.then_inc(x1t_pe, 1)

            def project_q(b, p, M=PE_M2):
                pe.wait_ge(x1t_sb, b + 1)
                for m in range(KC):
                    for k in range(KC):
                        mm = pe.matmul(M[:, m * S:(m + 1) * S], wx[:, 0, k, m * 128:(m + 1) * 128], x1T[:, k, :],
                                       start=(k == 0), stop=(k == KC - 1))
                mm.then_inc(q_pe, 1)

            def project_k(m, b, p, i, J=PE_J2):
                if m == 0:
                    pe.wait_ge(ctx_loaded[p], (i + 1) * 16)
                if J is PE_J2:
                    if m == 0:
                        pe.wait_ge(v_sb, b * KT)
                    else:
                        pe.wait_ge(k_lo, b * KC + m)
                for k in range(KC):
                    mm = pe.matmul(J[:, 0:S2], wx[:, 1, k, m * 128:(m + 1) * 128], ctxT[:, p, k, :],
                                   start=(k == 0), stop=(k == KC - 1))
                mm.then_inc(k_pe, 1)

            def project_v(t, b, p, J=PE_J2):
                if J is PE_J2:
                    if t == 0:
                        pe.wait_ge(k_lo, b * KC + KC)
                    else:
                        pe.wait_ge(v_sb, b * KT + t)
                for k in range(KC):
                    mm = pe.matmul(J[0:SK, 0:C], ctxT[:, p, k, t * SK:(t + 1) * SK], wx[:, 2, k, :],
                                   start=(k == 0), stop=(k == KC - 1))
                mm.then_inc(v_pe, 1)

            for c in range(6):
                project1(c, 0, 0, 0, True)

            def first_of_stage2(c):
                if c == 0:
                    pe.wait_ge(w_loaded["small"], 16 * 10)
                    pe.wait_ge(evac1[4], B)
                    project_k(0, 0, 0, 0, PE_J1[0])
                elif c == 1:
                    pe.wait_ge(evac1[5], B)
                    project_k(1, 0, 0, 0, PE_J1[1])
                elif c == 2:
                    pe.wait_ge(k_lo, 1)
                    turn_x1(0, 0, PE_J1[0])
                elif c == 3:
                    pe.wait_ge(k_lo, 2)
                    project_q(0, 0, PE_J1[1])
                elif c == 4:
                    project_v(0, 0, 0, PE_J1[0])
                else:
                    pe.wait_ge(q_sb, 1)
                    project_v(1, 0, 0, PE_J1[1])

            def stage1(b, p, i, first, last):
                j = i + p
                proj = first_of_stage2 if last else (lambda c: project1(c, b + 1, 1 - p, j, False))
                score1(0, b, p, first)
                score1(1, b, p, first)
                if not first:
                    out1(b - 1, 1 - p, isinstance(b, int) and b == 1)
                proj(0)
                score1(2, b, p, first)
                proj(1)
                score1(3, b, p, first)
                turn(0, b, first)
                for g in range(4):
                    proj(g + 2)
                    value1(g, b, p, first)
                    if g < 3:
                        turn(g + 1, b, first)
                if isinstance(b, int) and b == B - 2:
                    pe.wait_ge(prep, 5)
                    pe.wait_ge(y1, b)
                    pe.matmul(PE_W1[:, 0:S], anyw[:], ident[0:S, 0:S], start=True, stop=True).then_inc(q_any, 1)

            over_batches(pe, stage1)
            pe.wait_ge(v_sb, 1)
            project_v(2, 0, 0, PE_J1[0])
            out1(B - 1, 1, False)

            def score2(h, b, p, i, first):
                if h >= 3:
                    pe.wait_ge(max2[(h - 3) % 4], heads_done(b, h - 3))
                elif not first:
                    before = max(j for j in range(H) if (j + 1 - p) % 3 == (h + p) % 3)
                    pe.wait_ge(max2[before % 4], heads_done(b - 1, before))
                if h == 0:
                    pe.wait_ge(qst_loaded[p], (i + 1) * 16 * STACK_DMAS)
                    pe.wait_ge(kst_loaded[p], (i + 1) * 16 * STACK_DMAS)
                r = slice(64 * (h % 2), 64 * (h % 2) + 64)
                pe.matmul(PE_S2[(h + p) % 3][0:S, 0:S2P], qst[r, p, h // 2, :], kst[r, p, h // 2, :],
                          start=True, stop=True).then_inc(scores2[h % 4], 1)

            def turn2_(h, b, first):
                pe.wait_ge(exp2[h % 4], heads_done(b, h))
                if h >= 2:
                    pe.wait_ge(pt2[(h - 2) % 4], heads_done(b, h - 2))
                elif not first:
                    pe.wait_ge(pt2[(H - 2 + h) % 4], heads_done(b - 1, H - 2 + h))
                else:
                    pe.wait_ge(k_lo, 2 * KC)
                for t in range(KT):
                    mm = pe.transpose(PE_T2[h % 2][0:SK, t * S:(t + 1) * S], p2[h % 8][:, t * SK:(t + 1) * SK], ident[0:S, 0:S])
                mm.then_inc(turn2[h % 4], 1)

            def value2(q, b, p, first):
                for j in range(4):
                    pe.wait_ge(pt2[j], heads_done(b, 4 * q + j))
                if q == 0:
                    pe.wait_ge(v_sb, b * KT + KT)
                    if not first:
                        pe.wait_ge(ot2, b)
                for t in range(KT):
                    for j in range(4):
                        h = 4 * q + j
                        mm = pe.matmul(PE_V2[VP * j:VP * j + VP, q * S:(q + 1) * S], v2[:, p, t, h, :], pT2[0:SK, h % PT_RING, t, :],
                                       start=(t == 0), stop=(t == KT - 1))
                mm.then_inc(pv2, 1)

            def turn_o(b):
                pe.wait_ge(ot2, b + 1)
                for n in range(4):
                    mm = pe.transpose(M[0:S, n * 128:(n + 1) * 128], oT2[:, n, :], ident[:])
                mm.then_inc(on_pe, 1)

            def turn_on(b):
                pe.wait_ge(on_sb, b + 1)
                for k in range(KC):
                    mm = pe.transpose(M[:, k * S:(k + 1) * S], o2[:, k * 128:(k + 1) * 128], ident[0:S, 0:S])
                mm.then_inc(ont_pe, 1)

            def out2(b):
                pe.wait_ge(ont_sb, b + 1)
                for k in range(KC):
                    mm = pe.matmul(M[0:S, 0:C], on2T[:, k, :], wx[:, 3, k, :], start=(k == 0), stop=(k == KC - 1))
                mm.then_inc(wo_pe, 1)

            def turn_x2(b, p):
                pe.wait_ge(x2_done, b + 1)
                for k in range(KC):
                    mm = pe.transpose(M[:, k * S:(k + 1) * S], x2c[:, p, k * 128:(k + 1) * 128], ident[0:S, 0:S])
                mm.then_inc(x2t_pe, 1)

            turn_x1(1, 1)
            project_q(1, 1)
            project_k(0, 1, 1, 0, PE_T2[1])
            pe.wait_ge(v_sb, 2)
            project_k(1, 1, 1, 0, PE_T2[0])
            pe.wait_ge(v_sb, KT)
            pe.wait_ge(y1, B)

            def stage2(b, p, i, first, last):
                def turn_x1_next():
                    if isinstance(b, int) and b < 2:
                        pe.wait_ge(q_sb, b + 2)
                    else:
                        pe.wait_ge(x2t_sb, b - 1)
                    turn_x1(b + 2, p)

                def turn_o_prev():
                    if late(b):
                        pe.wait_ge(x2t_sb, b - 1)
                    else:
                        pe.wait_ge(q_sb, b + 3)
                    turn_o(b - 1)

                nxt = {} if last else {
                    6: lambda: project_v(0, b + 1, 1 - p), 8: lambda: project_v(1, b + 1, 1 - p), 10: lambda: project_v(2, b + 1, 1 - p)}
                nxt.update({} if late(b) else {
                    1: turn_x1_next, 4: lambda: project_q(b + 2, p),
                    12: lambda: project_k(0, b + 2, p, i + 1), 14: lambda: project_k(1, b + 2, p, i + 1)})
                prev = {} if first else {
                    7: turn_o_prev, 9: lambda: turn_on(b - 1), 11: lambda: out2(b - 1), 14: lambda: turn_x2(b - 1, 1 - p)}

                for h in range(H):
                    score2(h, b, p, i, first)
                    if h >= LAG:
                        turn2_(h - LAG, b, first)
                    elif not first:
                        turn2_(H - LAG + h, b - 1, False)
                    if h in nxt:
                        nxt[h]()
                    if h in prev:
                        prev[h]()
                    if h % 4 == 1 and h >= 9:
                        value2((h - 9) // 4, b, p, first)
                    elif h % 4 == 1 and not first:
                        value2((h + 7) // 4, b - 1, 1 - p, isinstance(b, int) and b == 1)

            over_batches(pe, stage2)
            for h in range(H - LAG, H):
                turn2_(h, B - 1, False)
            for q in (2, 3):
                value2(q, B - 1, 1, False)
            def logits_t(b, n, bk):
                pe.wait_ge(x2t_sb, b + n)
                for k in range(KC):
                    mm = pe.matmul(bk[0:E, 0:n * S], routerT[:, k, :], x2T[:, k, b * S:(b + n) * S],
                                   start=(k == 0), stop=(k == KC - 1))
                mm.then_inc(s_logit, 1)

            def shared(n, part):
                if part == 0 and n >= 2:
                    pe.wait_ge(sh_h, n - 1)
                grp, m = n // HT, n % HT
                for k in range(KC):
                    mm = pe.matmul(bank[2 + 2 * (n % 2) + part][:, 0:4 * S], ugs[:, k, part * HID + m * 128:part * HID + (m + 1) * 128],
                                   x2T[:, k, grp * 4 * S:(grp + 1) * 4 * S], start=(k == 0), stop=(k == KC - 1))
                mm.then_inc(sh_gu, 1)

            def shared_down(grp):
                pe.wait_ge(sh_h, (grp + 1) * HT)
                for n in range(4):
                    b = grp * 4 + n
                    if b >= 2:
                        pe.wait_ge(sh_ysb, b - 1)
                    for m in range(HT):
                        mm = pe.matmul(bank[6 + b % 2][0:S, 0:C], hTs[:, m, n * S:(n + 1) * S], dns[:, m, :],
                                       start=(m == 0), stop=(m == HT - 1))
                    mm.then_inc(sh_y, 1)

            pe.wait_ge(w_loaded["shared"], 32)
            logits_t(0, 4, bank[0])
            turn_o(B - 1)
            logits_t(4, 3, bank[1])
            turn_on(B - 1)
            shared(0, 0)
            out2(B - 1)
            shared(0, 1)
            shared(1, 0)
            turn_x2(B - 1, 1)
            shared(1, 1)
            logits_t(B - 1, 1, bank[7])
            for b in range(B):
                if b in (0, B - 1):
                    pe.wait_ge(lgt_sb, 2 if b == 0 else 3)
                mm = pe.transpose(bank[6][0:S, b * E:(b + 1) * E], lgT[:, b * S:(b + 1) * S], ident[0:E, 0:E])
            mm.then_inc(s_logit, 1)
            shared(2, 0)
            shared(2, 1)
            pe.wait_ge(s_route, ROUTE_ONEHOT)
            pe.matmul(bank[1][0:S, 0:B * E], upto[:], onehot[:].rearrange("p b e -> p (b e)"), start=True, stop=True)
            pe.matmul(bank[1][:, B * E:2 * B * E], ones[:], onehot[:].rearrange("p b e -> p (b e)"),
                      start=True, stop=True).then_inc(s_incl, 1)
            for n in (3, 4):
                shared(n, 0)
                shared(n, 1)
            shared_down(0)
            for n in (5, 6, 7):
                shared(n, 0)
                shared(n, 1)

            pairs = routed_pairs(pe)
            XB, GB, UB, HB, YB = bank[0], bank[2:4], bank[4:6], bank[1], bank[6]

            def head_tile(t, p, i, first):
                pe.wait_ge(xs_loaded[p], (i + 1) * 16)
                if not first:
                    pe.wait_ge(xst_sb, t)
                for k in range(KC):
                    mm = pe.transpose(XB[:, k * 128:(k + 1) * 128], xs[:, p, k * 128:(k + 1) * 128], ident[:])
                mm.then_inc(xst_pe, 1)

            def gate(t, p, e, early):
                pe.wait_ge(xst_sb, t + 1)
                if not early:
                    pe.wait_ge(h_sb, t - 1)
                for k in range(KC):
                    mm = pe.matmul(GB[p][:, :], xsT[:, p, k, :], arena[:, bass.ds(e[k], HID)], start=(k == 0), stop=(k == KC - 1))
                mm.then_inc(gu_pe, 1)

            def up(t, p, e):
                for k in range(KC):
                    mm = pe.matmul(UB[p][:, :], xsT[:, p, k, :], arena[:, bass.ds(e[KC + k], HID)], start=(k == 0), stop=(k == KC - 1))
                mm.then_inc(gu_pe, 1)

            def turn_h(t, p, first):
                pe.wait_ge(h_sb, t + 1)
                if not first:
                    pe.wait_ge(ht_sb, t)
                for m in range(HT):
                    mm = pe.transpose(HB[:, m * 128:(m + 1) * 128], hr[:, p, m * 128:(m + 1) * 128], ident[:])
                mm.then_inc(ht_pe, 1)

            def down(t, p, e, first):
                pe.wait_ge(ht_sb, t + 1)
                if not first:
                    pe.wait_ge(yr_sb, t)
                else:
                    pe.wait_ge(sh_ysb, B)
                for m in range(HT):
                    mm = pe.matmul(YB[:, 0:C], hrT[:, p, m, :], arena[:, bass.ds(e[m], C)], start=(m == 0), stop=(m == HT - 1))
                mm.then_inc(yr_pe, 1)

            def of_expert(t, offsets):
                e = pe.value_load(expert[0:1, bass.ds(t, 1)], min_val=0, max_val=E - 1)
                return [pe.snap(e * (UG + DN) + o) for o in offsets]

            def gates_ups(t):
                return of_expert(t, [part * HID + k * 2 * HID for part in range(2) for k in range(KC)])

            def downs(t):
                return of_expert(t, [UG + m * C for m in range(HT)])

            last = pairs * 2 - 1
            head_tile(0, 0, 0, True)
            shared_down(1)
            pe.wait_ge(w_experts, 32 * E)
            e = gates_ups(0)
            gate(0, 0, e, True)
            up(0, 0, e)
            head_tile(1, 1, 0, False)
            e, d = gates_ups(1), downs(0)
            gate(1, 1, e, True)
            turn_h(0, 0, True)
            up(1, 1, e)
            head_tile(2, 0, 1, False)
            down(0, 0, d, True)

            def step(t, p, i):
                e = gates_ups(t + 1)
                gate(t + 1, 1 - p, e, False)
                d = downs(t)
                turn_h(t, p, False)
                up(t + 1, 1 - p, e)
                if i is not None:
                    head_tile(t + 2, p, i + 1, False)
                down(t, p, d, False)

            with pe.Fori(0, pairs - 2) as i:
                step(i * 2 + 1, 1, i)
                step(i * 2 + 2, 0, i + 1)
            step(last - 2, 1, pairs - 2)
            step(last - 1, 0, None)
            d = downs(last)
            turn_h(last, 1, False)
            down(last, 1, d, False)

        @block.scalar
        def _(act):
            def evac_v(c, b, p, first):
                act.wait_ge(proj1[c], b + 1)
                if not first:
                    act.wait_ge(pv1[3], b - 1)
                act.activation(v1[p][:, 512 * c:512 * (c + 1)], PE_J1[c][0:S, :], ACT.Copy).then_inc(evac1[c], 1)

            def exps(g, b, first):
                act.wait_ge(max1, b * 4 + (g + 1))
                if not first:
                    act.wait_ge(turn1, b * 4 + (g - 3))
                for n in range(G1):
                    h = G1 * g + n
                    e = act.activation(p1[g][:, n, :], PE_S1[g % 2][0:S, n * S:(n + 1) * S], ACT.Exp,
                                       bias=nm1[:, h:h + 1], accum_out=rs1[:, h:h + 1])
                e.then_inc(exp1[g], 1)

            def evac_o(half, b, p, early):
                act.wait_ge(pv1[2 * half + 1], b + 1)
                if half == 0 and not early:
                    act.wait_ge(wout1, b - 1)
                act.activation(oT1[p][:, 4 * half:4 * half + 4, :],
                               PE_U1[half][:, 0:4 * S].rearrange("p (k n) -> p k n", k=4), ACT.Copy).then_inc(ot1[half], 1)

            def evac_k(m, b, first, J=PE_J2):
                act.wait_ge(k_pe, b * KC + (m + 1))
                if m == 0 and not first:
                    act.wait_ge(k_stored, b * 16)
                act.activation(k_hl[:, 0, m, 0:S2], J[:, 0:S2], ACT.Identity, bias=cols[:, 1, m:m + 1]).then_inc(k_hi, 1)

            def turn_evac(kind, b, p, M=PE_M2):
                if kind == "x1":
                    act.wait_ge(x1t_pe, b + 1)
                    act.activation(x1T[:], M[:, 0:KC * S].rearrange("p (k n) -> p k n", k=KC), ACT.Copy).then_inc(x1t_sb, 1)
                if kind == "on":
                    act.wait_ge(ont_pe, b + 1)
                    act.activation(on2T[:], M[:, 0:KC * S].rearrange("p (k n) -> p k n", k=KC), ACT.Copy).then_inc(ont_sb, 1)
                if kind == "x2":
                    act.wait_ge(x2t_pe, b + 1)
                    act.activation(x2T[:, :, bass.ds(b * S, S)], M[:, 0:KC * S].rearrange("p (k n) -> p k n", k=KC),
                                   ACT.Copy).then_inc(x2t_sb, 1)

            for c in range(2):
                evac_v(c, 0, 0, True)

            def stage1(b, p, i, first, last):
                early = isinstance(b, int) and b < 2
                exps(0, b, first)
                exps(1, b, first)
                if not last:
                    evac_v(0, b + 1, 1 - p, first)
                else:
                    evac_k(0, 0, True, PE_J1[0])
                exps(2, b, first)
                if not last:
                    evac_v(1, b + 1, 1 - p, first)
                else:
                    evac_k(1, 0, True, PE_J1[1])
                exps(3, b, first)
                if last:
                    turn_evac("x1", 0, 0, PE_J1[0])
                evac_o(0, b, p, early)
                evac_o(1, b, p, early)

            over_batches(act, stage1)

            def exps2(h, b):
                act.wait_ge(max2[h % 4], heads_done(b, h))
                act.activation(p2[h % 8], p2[h % 8], ACT.Exp, bias=nm2[:, h:h + 1], scale=-1.0).then_inc(exp2[h % 4], 1)

            def evac_pt(h, b, first):
                act.wait_ge(turn2[h % 4], heads_done(b, h))
                wait_ring(act, h, b, first)
                act.activation(pT2[0:SK, h % PT_RING], PE_T2[h % 2][0:SK, 0:KT * S].rearrange("p (k n) -> p k n", k=KT),
                               ACT.Copy).then_inc(pt2[h % 4], 1)

            turn_evac("x1", 1, 1)
            for m in range(KC):
                evac_k(m, 1, False, PE_T2[1 - m])

            def stage2(b, p, i, first, last):
                for h in range(H):
                    if h in (13, 15) and not late(b):
                        evac_k(h // 15, b + 2, False)
                    if (h - LAG) % 4 != 3:
                        if h >= LAG:
                            evac_pt(h - LAG, b, first)
                        elif not first:
                            evac_pt(H - LAG + h, b - 1, False)
                    exps2(h, b)
                    if not late(b):
                        if h == 2:
                            turn_evac("x1", b + 2, p)
                    if not first:
                        if h == 10:
                            turn_evac("on", b - 1, 1 - p)
                        if h == 15:
                            turn_evac("x2", b - 1, 1 - p)

            over_batches(act, stage2)
            for h in range(H - LAG, H - 1):
                evac_pt(h, B - 1, False)
            def evac_logits(n, b0, b1, bk):
                act.wait_ge(s_logit, n)
                act.activation(lgT[:, b0 * S:b1 * S], bk[0:E, 0:(b1 - b0) * S], ACT.Copy).then_inc(lgt_sb, 1)

            def shared_silu(n):
                act.wait_ge(sh_gu, 2 * n + 1)
                if n >= 1:
                    act.wait_ge(sh_h, n)
                act.activation(gs[:], bank[2 + 2 * (n % 2)][:, 0:4 * S], ACT.Silu).then_inc(sh_g, 1)

            evac_logits(1, 0, 4, bank[0])
            turn_evac("on", B - 1, 1)
            evac_logits(2, 4, B - 1, bank[1])
            shared_silu(0)
            turn_evac("x2", B - 1, 1)

            for n in range(1, 2 * HT):
                shared_silu(n)

            def tile_ahead(t, p):
                act.wait_ge(gu_pe, t * 2 + 3)
                act.wait_ge(h_sb, t + 1)
                act.activation(gr[:], bank[2 + 1 - p][:], ACT.Silu).then_inc(g_sb, 1)
                act.wait_ge(ht_pe, t + 1)
                act.activation(hrT[:, p], bank[1][:].rearrange("p (k n) -> p k n", k=HT), ACT.Copy).then_inc(ht_sb, 1)

            pairs = routed_pairs(act)
            act.wait_ge(gu_pe, 1)
            act.wait_ge(sh_h, 2 * HT)
            act.activation(gr[:], bank[2][:], ACT.Silu).then_inc(g_sb, 1)
            tile_ahead(0, 0)
            with act.Fori(0, pairs - 1) as i:
                tile_ahead(i * 2 + 1, 1)
                tile_ahead(i * 2 + 2, 0)
            act.wait_ge(ht_pe, pairs * 2)
            act.activation(hrT[:, 1], bank[1][:].rearrange("p (k n) -> p k n", k=HT), ACT.Copy).then_inc(ht_sb, 1)

        @block.vector
        def _(v):
            def evac_qk(c, b, p, first):
                v.wait_ge(proj1[c], b + 1)
                if not first:
                    v.wait_ge(scores1[3], b - 1)
                dst = (qT if c < 4 else kT)[p][:, 4 * (c % 2):4 * (c % 2) + 4, :]
                v.tensor_scalar(dst, PE_J1[c % 2][:, 0:4 * S].rearrange("p (k n) -> p k n", k=4),
                                D1 ** -0.5 if c < 4 else 1.0, None, ALU.mult).then_inc(evac1[c], 1)

            def rowmax(g, b, first):
                v.wait_ge(scores1[g], b + 1)
                if not first:
                    v.wait_ge(exp1[g], b)
                v.tensor_reduce(nm1[:, G1 * g:G1 * g + G1], PE_S1[g % 2][0:S, 0:G1 * S].rearrange("p (k n) -> p k n", k=G1),
                                AX.X, ALU.max, negate=True).then_inc(max1, 1)

            def normalise(g, b):
                c = slice(G1 * g, G1 * g + G1)
                v.wait_ge(exp1[g], b + 1)
                v.reciprocal(rc1[:, c], rs1[:, c]).then_inc(rcp1, 1)
                v.wait_ge(rcp1, b * 4 + (g + 1))
                v.tensor_tensor(p1[g], p1[g], rc1[:, c].unsqueeze(2).to_broadcast([S, G1, S]), ALU.mult).then_inc(norm1, 1)

            def evac_pt(g, b, first):
                v.wait_ge(turn1, b * 4 + (g + 1))
                if g >= 2:
                    v.wait_ge(pv1[g - 2], b + 1)
                elif not first:
                    v.wait_ge(pv1[g + 2], b)
                v.tensor_copy(pT1[g % 2], PE_T1[0:S, 0:G1 * S].rearrange("p (k n) -> p k n", k=G1)).then_inc(pt1, 1)

            def layernorm_a(src, done, added, b, p, sy, ss, sa, sv):
                v.wait_ge(done, b + 1)
                v.wait_ge(added, b + 1)
                v.tensor_tensor(ybuf[:, p], src, xb[:, p], ALU.add).then_inc(sy, 1)
                v.wait_ge(sy, b + 1)
                v.bn_stats(stats[:, p], ybuf[:, p]).then_inc(ss, 1)
                v.wait_ge(ss, b + 1)
                v.sem_inc(pause, 1)
                v.bn_aggr(mv[:, p], stats[:, p]).then_inc(sa, 1)
                v.wait_ge(sa, b + 1)
                v.tensor_scalar(veps[:, p:p + 1], mv[:, p, 1:2], EPS, None, ALU.add).then_inc(sv, 1)

            def ln1_a(b, p):
                layernorm_a(PE_W1[0:S, 0:C], wout1, xb1, b, p, y1, st1, ag1, ve1)

            def ln1_b(b, p):
                v.wait_ge(rstd1, b + 1)
                v.tensor_scalar(xres[:, b], ybuf[:, p], mv[:, p, 0:1], rstd[:, p:p + 1], ALU.subtract, ALU.mult).then_inc(x1_done, 1)

            def mask_bias():
                v.wait_ge(w_loaded["mask"], 16)
                v.tensor_scalar(mask0[:], mask_i[:], 0.0, None, ALU.is_equal).then_inc(prep, 1)
                v.wait_ge(prep, 1)
                v.tensor_reduce(allm[:], mask0[:], AX.X, ALU.min).then_inc(prep, 1)
                v.wait_ge(prep, 2)
                v.tensor_scalar(anym[:], allm[:], -1.0, 1.0, ALU.mult, ALU.add).then_inc(prep, 1)
                v.wait_ge(prep, 3)
                v.wait_ge(consts, 6)
                v.tensor_scalar(anyw[:], ones[:], anym[:], None, ALU.mult).then_inc(prep, 1)
                v.tensor_scalar(bias[:], mask0[:], anym[:], MASKED, ALU.mult, ALU.mult).then_inc(prep, 1)

            def query_scale():
                v.wait_ge(q_any, 1)
                v.tensor_scalar(qscale[:], PE_W1[:, 0:S], -D2 ** -0.5, None, ALU.mult).then_inc(prep, 1)

            def evac_q(b, first, M=PE_M2):
                v.wait_ge(q_pe, b + 1)
                if not first:
                    v.wait_ge(q_lo, b)
                for m in range(KC):
                    last = v.scalar_tensor_tensor(out=qf[:, m, :], in0=M[:, m * S:(m + 1) * S],
                                                  scalar=cols[:, 0, m:m + 1], in1=qscale[:], op0=ALU.add, op1=ALU.mult)
                last.then_inc(q_sb, 1)

            def split_k(m, b, J=PE_J2):
                v.wait_ge(k_hi, b * KC + (m + 1))
                v.scalar_tensor_tensor(out=k_hl[:, 1, m, 0:S2], in0=J[:, 0:S2], scalar=cols[:, 1, m:m + 1],
                                       in1=k_hl[:, 0, m, 0:S2].bitcast(F32), op0=ALU.add, op1=ALU.subtract).then_inc(k_lo, 1)

            def evac_v(t, b, p, first, J=PE_J2):
                v.wait_ge(v_pe, b * KT + (t + 1))
                if not first and t == 0:
                    v.wait_ge(pv2, 4 * b - 4)
                v.tensor_tensor(v2[:, p, t, :, 0:D2], J[0:SK, 0:C].rearrange("p (h d) -> p h d", h=H),
                                rows[0:SK, 1, :].rearrange("p (h d) -> p h d", h=H), ALU.add).then_inc(v_sb, 1)

            for c in range(2, 6):
                evac_qk(c, 0, 0, True)

            def stage1(b, p, i, first, last):
                if last:
                    query_scale()
                rowmax(0, b, first)
                rowmax(1, b, first)
                if not first:
                    ln1_a(b - 1, 1 - p)
                normalise(0, b)
                rowmax(2, b, first)
                normalise(1, b)
                if last:
                    split_k(0, 0, PE_J1[0])
                rowmax(3, b, first)
                if last:
                    split_k(1, 0, PE_J1[1])
                if not first:
                    ln1_b(b - 1, 1 - p)
                evac_pt(0, b, first)
                if not last:
                    evac_qk(2, b + 1, 1 - p, first)
                normalise(2, b)
                evac_pt(1, b, first)
                if not last:
                    evac_qk(3, b + 1, 1 - p, first)
                else:
                    v.wait_ge(v2_ones, 2)
                    evac_q(0, True, PE_J1[1])
                normalise(3, b)
                evac_pt(2, b, first)
                if not last:
                    evac_qk(4, b + 1, 1 - p, first)
                else:
                    evac_v(0, 0, 0, True, PE_J1[0])
                evac_pt(3, b, first)
                if not last:
                    evac_qk(5, b + 1, 1 - p, first)
                else:
                    evac_v(1, 0, 0, True, PE_J1[1])
                if first:
                    mask_bias()

            over_batches(v, stage1)
            evac_v(2, 0, 0, True, PE_J1[0])
            ln1_a(B - 1, 1)
            ln1_b(B - 1, 1)
            def mask_and_max(h, b, p, first):
                v.wait_ge(scores2[h % 4], heads_done(b, h))
                if h >= 8:
                    v.wait_ge(turn2[h % 4], heads_done(b, h - 8))
                elif not first:
                    v.wait_ge(turn2[h % 4], heads_done(b - 1, h + 8))
                v.sem_inc(pause, 1)
                v.tensor_tensor_reduce(p2[h % 8], PE_S2[(h + p) % 3][0:S, 0:S2], bias[:], 1.0, 3e38, ALU.add, ALU.min,
                                       accum_out=nm2[:, h:h + 1]).then_inc(max2[h % 4], 1)

            def evac_pt2(h, b, first):
                v.wait_ge(turn2[h % 4], heads_done(b, h))
                wait_ring(v, h, b, first)
                v.tensor_copy(pT2[0:SK, h % PT_RING], PE_T2[h % 2][0:SK, 0:KT * S].rearrange("p (k n) -> p k n", k=KT)).then_inc(pt2[h % 4], 1)

            def evac_ot(b, first):
                v.wait_ge(pv2, 4 * b + 4)
                if not first:
                    v.wait_ge(on_pe, b)
                v.tensor_copy(oT2[:], PE_V2[:, 0:4 * S].rearrange("p (k n) -> p k n", k=4)).then_inc(ot2, 1)

            def normalise2(b):
                o = PE_M2[0:S, :].rearrange("p (h d) -> p h d", h=H)
                v.wait_ge(on_pe, b + 1)
                v.reciprocal(rc2[:].unsqueeze(2), o[:, :, D2:D2 + 1]).then_inc(rc_done, 1)
                v.wait_ge(rc_done, b + 1)
                v.tensor_tensor(o2[:].rearrange("p (h d) -> p h d", h=H), o[:, :, 0:D2],
                                rc2[:].unsqueeze(2).to_broadcast([S, H, D2]), ALU.mult).then_inc(on_sb, 1)

            def ln2_a(b, p):
                layernorm_a(PE_M2[0:S, 0:C], wo_pe, xb2, b, p, y2, st2, ag2, ve2)

            def ln2_b(b, p, early):
                v.wait_ge(rstd2, b + 1)
                if not early:
                    v.wait_ge(x2t_pe, b - 1)
                    v.wait_ge(x2_kept, b - 1)
                v.tensor_scalar(x2c[:, p], ybuf[:, p], mv[:, p, 0:1], rstd[:, p:p + 1], ALU.subtract, ALU.mult).then_inc(x2_done, 1)

            evac_q(1, False)
            for m in range(KC):
                split_k(m, 1, PE_T2[1 - m])

            def stage2(b, p, i, first, last):
                for h in range(H):
                    mask_and_max(h, b, p, first)
                    if (h - LAG) % 4 == 3:
                        if h >= LAG:
                            evac_pt2(h - LAG, b, first)
                        elif not first:
                            evac_pt2(H - LAG + h, b - 1, False)
                    if not late(b):
                        if h == 5:
                            evac_q(b + 2, False)
                        if h in (13, 15):
                            split_k(h // 15, b + 2)
                    if not last and h in (7, 9, 11):
                        evac_v((h - 7) // 2, b + 1, 1 - p, first)
                    if not first:
                        if h == 6:
                            evac_ot(b - 1, isinstance(b, int) and b == 1)
                        if h == 8:
                            normalise2(b - 1)
                        if h == 12:
                            ln2_a(b - 1, 1 - p)
                        if h == 13:
                            ln2_b(b - 1, 1 - p, isinstance(b, int) and b <= 2)

            over_batches(v, stage2)
            evac_pt2(H - 1, B - 1, False)
            evac_ot(B - 1, False)
            normalise2(B - 1)
            ln2_a(B - 1, 1)
            ln2_b(B - 1, 1, False)

            def shared_product(k):
                v.wait_ge(sh_g, k + 1)
                v.wait_ge(sh_gu, 2 * k + 2)
                v.tensor_tensor(hTs[:, k % HT, :], gs[:], bank[3 + 2 * (k % 2)][:, 0:4 * S], ALU.mult).then_inc(sh_h, 1)

            n = [0]

            def chain(ins):
                n[0] += 1
                ins.then_inc(s_route, 1)
                v.wait_ge(s_route, n[0])

            v.wait_ge(s_logit, 3)
            v.tensor_copy(lgT[:, (B - 1) * S:B * S], bank[7][0:E, 0:S]).then_inc(lgt_sb, 1)
            shared_product(0)
            v.wait_ge(s_logit, 4)
            chain(v.tensor_copy(logit[:], bank[6][0:S, 0:B * E].rearrange("p (b e) -> p b e", b=B)))
            for b in range(B):
                m = v.max(top8[:, b], logit[:, b])
            chain(m)
            for b in range(B):
                m = v.max_index(tidx[:, b], top8[:, b], logit[:, b])
            chain(m)
            v.wait_ge(consts, 10)
            chain(v.tensor_tensor(onehot[:], eidx[0:S].unsqueeze(1).to_broadcast([S, B, E]),
                                  tidx[:, :, 0:1].to_broadcast([S, B, E]), ALU.is_equal))
            assert n[0] == ROUTE_ONEHOT
            shared_product(1)
            v.wait_ge(s_incl, 1)
            chain(v.tensor_copy(incl[:], bank[1][0:S, 0:B * E].rearrange("p (b e) -> p b e", b=B)))
            v.memset(cnt[:, 0, :], 0.0)
            chain(v.memset(ends[:, 0:1], 0.0))
            for b in range(B):
                chain(v.tensor_tensor(cnt[:, b + 1, :], bank[1][:, (B + b) * E:(B + b + 1) * E], cnt[:, b, :], ALU.add))
            shared_product(2)
            chain(v.tensor_tensor(fills[:], steps7[:].unsqueeze(1).to_broadcast([128, E, 7]),
                                  cnt[:, B, :].unsqueeze(2).to_broadcast([128, E, 7]), ALU.is_lt))
            chain(v.tensor_reduce(ntile[:], fills[:], AX.X, ALU.add))
            for e in range(E):
                if e == 0:
                    v.tensor_copy(ends[:, 1:2], ntile[:, 0:1]).then_inc(s_eload, 1)
                else:
                    v.wait_ge(s_eload, e)
                    v.tensor_tensor(ends[:, e + 1:e + 2], ends[:, e:e + 1], ntile[:, e:e + 1], ALU.add).then_inc(s_eload, 1)
            v.wait_ge(s_eload, E)
            chain(v.tensor_tensor(pos[:], incl[:], cnt[0:S, 0:B, :], ALU.add))
            chain(v.scalar_tensor_tensor(out=incl[:], in0=ends[0:S, 0:E].unsqueeze(1).to_broadcast([S, B, E]), scalar=float(TILE),
                                         in1=pos[:], op0=ALU.mult, op1=ALU.add))
            chain(v.tensor_tensor(pos[:], incl[:], onehot[:], ALU.mult))
            chain(v.tensor_reduce(slotf[:], pos[:], AX.X, ALU.add))
            chain(v.tensor_scalar(slot[:], slotf[:], -1.0, None, ALU.add))
            assert n[0] == ROUTE_SLOTS
            chain(v.tensor_tensor(past[:], tiles_i[:].unsqueeze(2).to_broadcast([1, ROUTED_TILES, E - 1]),
                                  ends[0:1, 1:E].unsqueeze(1).to_broadcast([1, ROUTED_TILES, E - 1]), ALU.is_ge))
            chain(v.tensor_reduce(expertf[:], past[:], AX.X, ALU.add))
            chain(v.tensor_copy(expert[:], expertf[:]))
            chain(v.tensor_tensor(taken[:], tiles_i[:].rearrange("a (n two) -> a n two", two=2)[:, FEWEST_PAIRS:, 0],
                                  ends[0:1, E:E + 1].to_broadcast([1, EXTRA_PAIRS]), ALU.is_lt))
            chain(v.tensor_reduce(extraf[:], taken[:], AX.X, ALU.add))
            chain(v.tensor_copy(extra_i[:], extraf[:]))
            assert n[0] == ROUTE_EXPERTS

            def shared_sum(b):
                v.wait_ge(sh_y, b + 1)
                v.tensor_tensor(ysh[:, b], bank[6 + b % 2][0:S, 0:C], xres[:, b], ALU.add).then_inc(sh_ysb, 1)

            v.wait_ge(x2_kept, B)
            shared_product(3)
            for b in range(4):
                shared_sum(b)
            for k in range(4, 8):
                if k == 4:
                    v.wait_ge(sh_y, 4)
                shared_product(k)

            def evac_x(t, p, early):
                v.wait_ge(xst_pe, t + 1)
                if not early:
                    v.wait_ge(gu_pe, t * 2 - 2)
                v.tensor_copy(xsT[:, p], bank[0][:, 0:KC * 128].rearrange("p (k n) -> p k n", k=KC)).then_inc(xst_sb, 1)

            def product(t, p, early):
                v.wait_ge(g_sb, t + 1)
                v.wait_ge(gu_pe, t * 2 + 2)
                if not early:
                    v.wait_ge(ht_pe, t - 1)
                v.tensor_tensor(hr[:, p], gr[:], bank[4 + p][:], ALU.mult).then_inc(h_sb, 1)

            def evac_y(t, p, i, early):
                v.wait_ge(yr_pe, t + 1)
                if not early:
                    v.wait_ge(ys_stored[p], i * 16)
                v.tensor_copy(yr[:, p], bank[6][:, 0:C]).then_inc(yr_sb, 1)

            evac_x(0, 0, True)
            for b in range(4, B):
                shared_sum(b)
            product(0, 0, True)
            evac_x(1, 1, True)
            product(1, 1, True)
            evac_x(2, 0, False)
            evac_y(0, 0, 0, True)
            product(2, 0, False)
            evac_x(3, 1, False)
            evac_y(1, 1, 0, True)

            pairs = routed_pairs(v)
            with v.Fori(1, pairs - 1) as i:
                for p in range(2):
                    product(i * 2 + 1 + p, 1 - p, False)
                    evac_x(i * 2 + 2 + p, p, False)
                    evac_y(i * 2 + p, p, i, False)
            product(pairs * 2 - 1, 1, False)
            evac_y(pairs * 2 - 2, 0, pairs - 1, False)
            evac_y(pairs * 2 - 1, 1, pairs - 1, False)

            def final(b):
                v.tensor_scalar(ygat[:, b], ysh[:, b], mv3[:, b, 0:1], rs3[:, b:b + 1], ALU.subtract, ALU.mult).then_inc(done3, 1)

            for n in range(B + 2):
                if n < B:
                    v.wait_ge(gathered[n], 16)
                    v.tensor_tensor(ysh[:, n], ysh[:, n], ygat[:, n], ALU.add).then_inc(sum3, 1)
                if 1 <= n < B + 1:
                    v.wait_ge(sum3, n)
                    v.bn_stats(st3[:, n - 1], ysh[:, n - 1]).then_inc(stats3, 1)
                if n >= 2:
                    v.wait_ge(stats3, n - 1)
                    v.bn_aggr(mv3[:, n - 2], st3[:, n - 2]).then_inc(aggr3, 1)
                if n in (5, 9):
                    half = (n - 5) // 4
                    v.wait_ge(aggr3, 4 * half + 4)
                    v.tensor_scalar(ve3[:, 4 * half:4 * half + 4], mv3[:, 4 * half:4 * half + 4, 1], EPS, None, ALU.add).then_inc(ve3s, 1)
            for b in range(B):
                if b % 4 == 0:
                    v.wait_ge(rstd3, b // 4 + 1)
                final(b)


def kernel(**inputs):
    import numpy as np
    import concourse.bacc as bacc
    from concourse.bass_utils import run_bass_kernel_spmd

    g = {k: np.asarray(v) for k, v in inputs.items()}

    def tiles(w):
        return np.ascontiguousarray(w.reshape(-1, 128, w.shape[1]).transpose(1, 0, 2))

    def per_batch(x):
        return np.ascontiguousarray(x.transpose(0, 2, 1).reshape(B, KC, 128, -1).transpose(0, 2, 1, 3))

    gates = list(g["L0_ffn_gate"]) + [g["L0_ffn_w_gate_s"]]
    ups = list(g["L0_ffn_up"]) + [g["L0_ffn_w_up_s"]]
    downs = list(g["L0_ffn_down"]) + [g["L0_ffn_w_down_s"]]
    arrays = {
        "xT": per_batch(g["x"]),
        "x": np.ascontiguousarray(g["x"].transpose(1, 0, 2)),
        "ctxT": per_batch(g["ctx_1024"]),
        "mask": np.ascontiguousarray(g["mask_1x1xSxS2_ik0"].reshape(S, S2)),
        "wqkv": tiles(g["L0_attn_w_qkv"]),
        "wout": tiles(g["L0_attn_w_out"]),
        "b_out": g["L0_attn_b_out"].reshape(1, C),
        "bv": g["L0_xattn_bv"].reshape(1, C),
        "bo": g["L0_xattn_bo"].reshape(1, C),
        "bq": np.ascontiguousarray(g["L0_xattn_bq"].reshape(KC, 128).T),
        "bk": np.ascontiguousarray(g["L0_xattn_bk"].reshape(KC, 128).T),
        "router": tiles(g["L0_ffn_router"].T),
        "wq": tiles(g["L0_xattn_Wq"].T),
        "wk": tiles(g["L0_xattn_Wk"].T),
        "wv": tiles(g["L0_xattn_Wv"].T),
        "wo": tiles(g["L0_xattn_Wo"].T),
        "ug": np.stack([tiles(np.concatenate([a, b]).T) for a, b in zip(gates, ups)]),
        "dn": np.stack([tiles(d.T) for d in downs]),
    }
    nc = bacc.Bacc("TRN2", target_bir_lowering=False, num_devices=1)
    aps = {n: nc.dram_tensor("in_" + n, v.shape, dt.from_np(v.dtype), kind="ExternalInput").ap() for n, v in arrays.items()}
    out = nc.dram_tensor("out_x", (B, S, C), F32, kind="ExternalOutput").ap()
    build(nc, aps, out)
    r = run_bass_kernel_spmd(nc, [{"in_" + n: v for n, v in arrays.items()}], core_ids=[0])
    return r.results[0]["out_x"]
```

```python
from contextlib import ExitStack

import concourse.bass as bass
from concourse import mybir

dt = mybir.dt
F32, F32R, I32, U32 = dt.float32, dt.float32r, dt.int32, dt.uint32
ALU = mybir.AluOpType
ACT = mybir.ActivationFunctionType
AX = mybir.AxisListType

B, S, C = 8, 112, 256
KC = C // 128
H = 16
D1 = 64
INNER = H * D1
G1 = 4
S2 = 375
KT = 3
SK = S2 // KT
D2 = C // H
VP = 32
E, HID = 8, 512
HT = HID // 128
T = B * S
TILE = 128
ROUTED_TILES = (T - E) // TILE + E
EPS = 1e-5
MASKED = 1e30
S2P = S2 + 1
PAIRS_H = H // 2
PARTS_K, PARTS_Q = (0, 1, 0, 1), (0, 0, 1, 1)
STACK_DMAS = len(PARTS_K) * 2
LAG = 3
PT_RING = 8
FEWEST_TILES = -(-T // TILE)
EXTRA_TILES = ROUTED_TILES - FEWEST_TILES
PAIRS = B // 2


def build(nc, a, out):
    ctx = ExitStack()
    with ctx:
        def sb(name, shape, d=F32):
            return ctx.enter_context(nc.sbuf_tensor(name, shape, d))

        def sem(name):
            return ctx.enter_context(nc.semaphore(name))

        def sems(name, n):
            return [sem(f"{name}_{j}") for j in range(n)]

        bank = [ctx.enter_context(nc.psum_tensor(f"bank{j}", [128, 512], F32)) for j in range(8)]
        slots_x = nc.dram_tensor("slots_x", (ROUTED_TILES * TILE, C), F32, kind="Internal").ap()
        slots_y = nc.dram_tensor("slots_y", (ROUTED_TILES * TILE, C), F32, kind="Internal").ap()

        k_parts = nc.dram_tensor("k_parts", (2, 2, C, S2P), F32, kind="Internal").ap()
        q_parts = nc.dram_tensor("q_parts", (2, 2, C, S), F32, kind="Internal").ap()

        ident = sb("ident", [128, 128])
        minus_half = sb("minus_half", [S, 1])
        xres = sb("xres", [S, B, C])
        x2T = sb("x2T", [128, KC, T])
        wx = sb("wx", [128, 4, KC, C])
        cols = sb("cols", [128, 2, KC])
        rows = sb("rows", [128, 3, C])
        ybuf = sb("ybuf", [S, 2, C])
        stats = sb("stats", [S, 2, 6])
        mv = sb("mv", [S, 2, 2])
        veps = sb("veps", [S, 2])
        rstd = sb("rstd", [S, 2])
        xb = sb("xb", [S, 2, C])
        ugs = sb("ugs", [128, KC, 2 * HID])
        dns = sb("dns", [128, HT, C])
        zeros = sb("zeros", [128, C])

        UG, DN = KC * 2 * HID, HT * C
        ARENA = E * (UG + DN)
        with ExitStack() as upper:
            upper.enter_context(nc.sbuf_tensor("lower_half", [128, ARENA // 2], F32))
            kst = upper.enter_context(nc.sbuf_tensor("kst", [128, 2, PAIRS_H, S2P], F32R))
            qst = upper.enter_context(nc.sbuf_tensor("qst", [128, 2, PAIRS_H, S], F32R))
            p2_more = upper.enter_context(nc.sbuf_tensor("p2_more", [S, 4, S2], F32))
            pT2 = upper.enter_context(nc.sbuf_tensor("pT2", [128, PT_RING, KT, S], F32))
        arena = sb("arena", [128, ARENA])
        top = [0]

        def carve(n):
            top[0] += n
            assert top[0] <= ARENA // 2 or top[0] - n >= ARENA // 2 and top[0] <= ARENA
            return arena[:, top[0] - n:top[0]]

        wout = carve(INNER // 128 * C).rearrange("p (k n) -> p k n", n=C)
        v1 = [carve(INNER)[0:S] for _ in range(2)]
        qT = [carve(8 * S).rearrange("p (k n) -> p k n", k=8) for _ in range(2)]
        kT = [carve(8 * S).rearrange("p (k n) -> p k n", k=8) for _ in range(2)]
        p1 = [carve(G1 * S)[0:S].rearrange("p (k n) -> p k n", k=G1) for _ in range(4)]
        pT1 = [carve(G1 * S)[0:S].rearrange("p (k n) -> p k n", k=G1) for _ in range(2)]
        oT1 = [carve(8 * S).rearrange("p (k n) -> p k n", k=8) for _ in range(2)]
        top[0] = ARENA // 2
        wqkv = carve(KC * 3 * INNER).rearrange("p (k n) -> p k n", k=KC)
        xT = [carve(KC * S).rearrange("p (k n) -> p k n", k=KC) for _ in range(2)]
        top[0] = ARENA - 2 * G1 * S
        pT1 += [carve(G1 * S)[0:S].rearrange("p (k n) -> p k n", k=G1) for _ in range(2)]
        by_expert = arena[:, :].rearrange("p (e n) -> p e n", e=E)
        ug = by_expert[:, :, 0:UG].rearrange("p e (k n) -> p e k n", k=KC)
        dn = by_expert[:, :, UG:UG + DN].rearrange("p e (k n) -> p e k n", k=HT)
        nm1 = sb("nm1", [S, H])
        rs1 = sb("rs1", [S, H])
        rc1 = sb("rc1", [S, H])

        mid = sb("mid", [128, 1, 2 * KC * S2])
        ctxT = mid[:, 0, :].rearrange("p (b k n) -> p b k n", b=2, k=KC)
        k_hl = sb("k_hl", [128, 2, KC, S2P], F32R)
        q_hl = sb("q_hl", [128, 2, KC, S], F32R)
        v2_all = sb("v2", [128, 2 * KT * H * VP])
        v2 = v2_all[0:SK, :].rearrange("p (b k h d) -> p b k h d", b=2, k=KT, h=H)
        qf = sb("qf", [128, KC, S])
        qscale = sb("qscale", [128, S])
        x1c = sb("x1c", [S, 2, C])
        x1T = sb("x1T", [128, KC, S])
        p2_all = sb("p2", [128, 4 * S2])
        p2 = [p2_all[0:S, j * S2:(j + 1) * S2] for j in range(4)] + [p2_more[:, j, :] for j in range(4)]
        nm2 = sb("nm2", [S, H])
        oT2 = sb("oT2", [128, 4, S])
        o2 = sb("o2", [S, C])
        rc2 = sb("rc2", [S, H])
        on2T = sb("on2T", [128, KC, S])
        mask_i = sb("mask_i", [S, S2], I32)
        mask0 = sb("mask0", [S, S2])
        allm = sb("allm", [S, 1])
        anym = sb("anym", [S, 1])
        anyw = sb("anyw", [S, 128])
        bias = mask0
        x2c = sb("x2c", [S, 2, C])

        hTs = sb("hTs", [128, HT, 4 * S])
        gs = sb("gs", [128, 4 * S])
        routerT = sb("routerT", [128, KC, E])
        upto = sb("upto", [S, S])
        ones = sb("ones", [S, 128])
        logit = sb("logit", [S, B, E])
        top8 = sb("top8", [S, B, 8])
        tidx = sb("tidx", [S, B, 8], U32)
        choice = sb("choice", [S, B])
        onehot = sb("onehot", [S, B, E])
        incl = sb("incl", [S, B, E])
        cnt = sb("cnt", [128, B + 1, E])
        fills = sb("fills", [128, E, 7])
        ntile = sb("ntile", [128, E])
        ends = sb("ends", [128, E + 1])
        pos = sb("pos", [S, B, E])
        slotf = sb("slotf", [S, B])
        slot = sb("slot", [S, B], U32)
        steps7 = sb("steps7", [128, 7])
        eidx = sb("eidx", [128, E])
        tiles_i = sb("tiles_i", [1, ROUTED_TILES])
        past = sb("past", [1, ROUTED_TILES, E - 1])
        expertf = sb("expertf", [1, ROUTED_TILES])
        expert = sb("expert", [1, ROUTED_TILES], I32)
        taken = sb("taken", [1, EXTRA_TILES])
        extraf = sb("extraf", [1, 1])
        extra_i = sb("extra_i", [1, 1], I32)
        xs = sb("xs", [128, C])
        xsT = sb("xsT", [128, KC, 128])
        lgT = mid[0:E, 0, 0:T]
        hr = mid[:, 0, 0:HID]
        hrT = sb("hrT", [128, HT, 128])
        gr = p2_all[:, 2 * C:2 * C + HID]
        yr = p2_all[:, 0:C]
        ysh = v2_all[0:S, 0:B * C].rearrange("p (b n) -> p b n", b=B)
        ygat = xres
        mv3 = sb("mv3", [S, B, 2])
        st3 = sb("st3", [S, B, 6])
        ve3 = sb("ve3", [S, B])
        rs3 = sb("rs3", [S, B])

        pause = sem("pause")
        consts = sem("consts")
        w_loaded = {n: sem(f"w_{n}") for n in ("v0", "v1", "q", "k", "out", "x", "small", "mask", "shared")}
        w_experts = sem("w_experts")
        xT_loaded = sems("xT_loaded", 2)
        zeroed = sem("zeroed")
        proj1 = sems("proj1", 6)
        evac1 = sems("evac1", 6)
        scores1 = sems("scores1", 4)
        max1, norm1, turn1, pt1 = sem("max1"), sem("norm1"), sem("turn1"), sem("pt1")
        exp1 = sems("exp1", 4)
        rcp1 = sem("rcp1")
        pv1 = sems("pv1", 2)
        ot1 = sems("ot1", 2)
        wout1 = sem("wout1")
        xb1 = sem("xb1")
        y1, st1, ag1, ve1, rstd1, x1_done = (sem(n) for n in ("y1", "st1", "ag1", "ve1", "rstd1", "x1_done"))

        ctx_loaded = sems("ctx_loaded", 2)
        prep = sem("prep")
        q_any = sem("q_any")
        v2_ones = sem("v2_ones")
        x1c_done = sem("x1c_done")
        xb2 = sem("xb2")
        x1t_pe, x1t_sb, q_pe, q_sb = (sem(n) for n in ("x1t_pe", "x1t_sb", "q_pe", "q_sb"))
        k_pe, k_hi, k_lo, v_pe, v_sb = sem("k_pe"), sem("k_hi"), sem("k_lo"), sem("v_pe"), sem("v_sb")
        q_hi, q_lo = sem("q_hi"), sem("q_lo")
        k_stored, q_stored = sem("k_stored"), sem("q_stored")
        kst_loaded, qst_loaded = sems("kst_loaded", 2), sems("qst_loaded", 2)
        scores2 = sems("scores2", 4)
        max2 = sems("max2", 4)
        exp2 = sems("exp2", 4)
        turn2 = sems("turn2", 4)
        pt2 = sems("pt2", 4)
        pv2 = sem("pv2")
        ot2 = sem("ot2")
        on_pe, rc_done, on_sb, ont_pe, ont_sb = (sem(n) for n in ("on_pe", "rc_done", "on_sb", "ont_pe", "ont_sb"))
        wo_pe = sem("wo_pe")
        y2, st2, ag2, ve2, rstd2, x2_done, x2_kept = (sem(n) for n in ("y2", "st2", "ag2", "ve2", "rstd2", "x2_done", "x2_kept"))
        x2t_pe, x2t_sb = sem("x2t_pe"), sem("x2t_sb")

        lgt_sb = sem("lgt_sb")
        s_logit, s_route, s_incl, s_eload = sem("s_logit"), sem("s_route"), sem("s_incl"), sem("s_eload")
        sh_gu, sh_g, sh_h, sh_y, sh_ysb = (sem(n) for n in ("sh_gu", "sh_g", "sh_h", "sh_y", "sh_ysb"))
        scattered, gathered = sem("scattered"), sems("gathered", B)
        xs_loaded, ys_stored = sem("xs_loaded"), sem("ys_stored")
        xst_pe, xst_sb, gu_pe, g_sb, h_sb, ht_pe, ht_sb, yr_pe, yr_sb = (
            sem(n) for n in ("xst_pe", "xst_sb", "gu_pe", "g_sb", "h_sb", "ht_pe", "ht_sb", "yr_pe", "yr_sb"))
        sum3, stats3, aggr3, ve3s, rstd3, done3, stored = sem("sum3"), sem("stats3"), sem("aggr3"), sem("ve3s"), sem("rstd3"), sem("done3"), sem("stored")

        PE_S1, PE_J1, PE_T1, PE_U1, PE_W1 = bank[0:2], bank[2:4], bank[4], bank[5:7], bank[7]
        PE_S2, PE_T2, PE_V2, PE_M2, PE_J2 = bank[0:3], bank[3:5], bank[5], bank[6], bank[7]

        def head1(g, n):
            return 2 * G1 * (g // 2) + 2 * n + g % 2

        def heads_done(b, h):
            return b * (H // 4) + (h // 4 + 1)

        def over_batches(eng, step):
            for p in range(2):
                step(p, p, 0, p == 0, False)
            with eng.Fori(1, PAIRS - 1) as i:
                for p in range(2):
                    step(i * 2 + p, p, i, False, False)
            for p in range(2):
                step(B - 2 + p, p, PAIRS - 1, False, p == 1)

        def late(b):
            return isinstance(b, int) and b >= B - 2

        def wait_ring(eng, h, b, first):
            if h >= PT_RING:
                eng.wait_ge(pv2, 4 * b + (h - PT_RING) // 4 + 1)
            elif not first:
                eng.wait_ge(pv2, 4 * b + (h + H - PT_RING) // 4 + 1 - 4)

        ROUTE_ONEHOT, ROUTE_SLOTS, ROUTE_EXPERTS = 4, 21, 27
        
        def routed_tiles(eng):
            eng.wait_ge(s_route, ROUTE_EXPERTS)
            return eng.value_load(extra_i[0:1, 0:1], min_val=0, max_val=EXTRA_TILES) + FEWEST_TILES

        block = ctx.enter_context(nc.Block())

        @block.sync
        def _(sp):
            sp.dma_start(xT[0], a["xT"][0]).then_inc(xT_loaded[0], 16)
            half = INNER // 2
            for n, start, size in (("v0", 4 * half, half), ("v1", 5 * half, half), ("q", 0, INNER), ("k", INNER, INNER)):
                sp.dma_start(wqkv[:, :, start:start + size], a["wqkv"][:, :, start:start + size]).then_inc(w_loaded[n], 16)
            sp.dma_start(xT[1], a["xT"][1]).then_inc(xT_loaded[1], 16)
            sp.dma_start(wout, a["wout"]).then_inc(w_loaded["out"], 16)
            sp.dma_start(xres[:], a["x"]).then_inc(w_loaded["x"], 16)
            for j, n in enumerate(("b_out", "bv", "bo")):
                sp.dma_start(rows[:, j, :], a[n].to_broadcast([128, C])).then_inc(w_loaded["small"], 16)
            sp.dma_start(mask_i[:], a["mask"]).then_inc(w_loaded["mask"], 16)
            sp.dma_start(cols[:, 0, :], a["bq"]).then_inc(w_loaded["small"], 16)
            sp.dma_start(cols[:, 1, :], a["bk"]).then_inc(w_loaded["small"], 16)
            sp.dma_start(routerT[:], a["router"]).then_inc(w_loaded["small"], 16)
            for j, n in enumerate(("wq", "wk", "wv", "wo")):
                sp.dma_start(wx[:, j], a[n]).then_inc(w_loaded["small"], 16)
            for p in range(2):
                sp.dma_start(ctxT[:, p], a["ctxT"][p]).then_inc(ctx_loaded[p], 16)
            sp.dma_start(ugs[:], a["ug"][E]).then_inc(w_loaded["shared"], 16)
            sp.dma_start(dns[:], a["dn"][E]).then_inc(w_loaded["shared"], 16)

            def load_xT(b, p, i):
                sp.wait_ge(proj1[5], b - 1)
                sp.dma_start(xT[p], a["xT"][b]).then_inc(xT_loaded[p], 16)

            with sp.Fori(1, PAIRS) as i:
                for p in range(2):
                    load_xT(i * 2 + p, p, i)
            sp.wait_ge(consts, 3)
            for t in range(ROUTED_TILES):
                sp.dma_start(slots_x[t * TILE:(t + 1) * TILE, :], zeros[:]).then_inc(zeroed, 16)
            for t in range(FEWEST_TILES, ROUTED_TILES):
                sp.dma_start(slots_y[t * TILE:(t + 1) * TILE, :], zeros[:]).then_inc(zeroed, 16)
            def load_ctx(b, p):
                sp.wait_ge(v_pe, (b - 2) * KT + KT)
                sp.dma_start(ctxT[:, p], a["ctxT"][b]).then_inc(ctx_loaded[p], 16)

            queries = (PARTS_Q, q_lo, 1, q_stored, q_parts, q_hl, qst, qst_loaded)
            keys = (PARTS_K, k_lo, KC, k_stored, k_parts, k_hl, kst, kst_loaded)

            def store_parts(which, b, p):
                _, split, per_batch, parts_stored, held, src, _, _ = which
                sp.wait_ge(split, b * per_batch + per_batch)
                sp.dma_start(held[p].rearrange("c (m x) n -> x c m n", x=128), src[:].bitcast(F32)).then_inc(parts_stored, 16)

            def stack_parts(which, b, p):
                parts, _, _, parts_stored, held, _, dst, loaded = which
                sp.wait_ge(parts_stored, (b + 1) * 16)
                by_head = held[p].rearrange("c (h a r) n -> c a r h n", a=2, r=D2)
                for copy in range(4):
                    for odd in range(2):
                        to = 64 * odd + D2 * copy
                        sp.dma_start(dst[to:to + D2, p].bitcast(F32), by_head[parts[copy], odd]).then_inc(loaded[p], 16)

            def stack(b, p):
                store_parts(queries, b, p)
                store_parts(keys, b, p)
                if not (isinstance(b, int) and b < 2):
                    sp.wait_ge(scores2[3], heads_done(b - 2, H - 1))
                    sp.sem_inc(pause, 1)
                stack_parts(queries, b, p)
                stack_parts(keys, b, p)

            def stage2(b, p, i, first, last):
                if not first and not late(b):
                    load_ctx(b + 2, p)
                if p == 0:
                    sp.dma_start(ug[:, bass.ds(i, 1)], a["ug"][bass.ds(i, 1)].rearrange("e p k n -> p e k n")).then_inc(w_experts, 16)
                else:
                    sp.dma_start(dn[:, bass.ds(i, 1)], a["dn"][bass.ds(i, 1)].rearrange("e p k n -> p e k n")).then_inc(w_experts, 16)
                if not late(b):
                    stack(b + 2, p)

            store_parts(queries, 0, 0)
            store_parts(keys, 0, 0)
            sp.wait_ge(proj1[5], B)
            stack_parts(queries, 0, 0)
            stack_parts(keys, 0, 0)
            load_ctx(2, 0)
            stack(1, 1)
            sp.wait_ge(wout1, B)
            over_batches(sp, stage2)
            sp.wait_ge(pv2, 4 * B)
            for e in range(E // 2, E):
                sp.dma_start(ug[:, e], a["ug"][e]).then_inc(w_experts, 16)
                sp.dma_start(dn[:, e], a["dn"][e]).then_inc(w_experts, 16)

            def load_tile(t):
                sp.dma_start(xs[:], slots_x[bass.ds(t * TILE, TILE), :]).then_inc(xs_loaded, 16)

            def store_tile(t):
                sp.wait_ge(yr_sb, t + 1)
                sp.dma_start(slots_y[bass.ds(t * TILE, TILE), :], yr).then_inc(ys_stored, 16)

            sp.wait_ge(scattered, 16 * B)
            load_tile(0)
            sp.wait_ge(xst_pe, 1)
            load_tile(1)
            tiles = routed_tiles(sp)
            with sp.Fori(0, tiles - 2) as t:
                sp.wait_ge(xst_pe, t + 2)
                load_tile(t + 2)
                store_tile(t)
            store_tile(tiles - 2)
            store_tile(tiles - 1)
            parts = ((0, B // 2), (B // 2, B - 2), (B - 2, B))
            for start, end in parts:
                sp.wait_ge(done3, end)
                sp.dma_start(out[start:end].rearrange("b s c -> s b c"), ygat[:, start:end]).then_inc(stored, 16)
            sp.wait_ge(stored, 16 * len(parts))

        @block.gpsimd
        def _(g):
            g.memset(ident[:], 0.0).then_inc(consts, 1)
            g.memset(minus_half[:], -0.5).then_inc(consts, 1)
            g.memset(zeros[:], 0.0).then_inc(consts, 1)
            g.wait_ge(consts, 3)
            g.affine_select(out=ident[:], in_=ident[:], compare_op=ALU.not_equal, fill=1.0, base=0,
                            pattern=[[-1, 128]], channel_multiplier=1).then_inc(consts, 1)
            g.wait_ge(consts, 4)
            g.memset(k_hl[:, :, :, S2:S2P].bitcast(F32), 0.0).then_inc(consts, 1)
            g.wait_ge(consts, 5)
            g.memset(ones[:], 1.0).then_inc(consts, 1)
            g.memset(v2_all[:], 0.0).then_inc(v2_ones, 1)
            g.wait_ge(v2_ones, 1)
            g.memset(v2[:, :, :, :, D2:D2 + 1], 1.0).then_inc(v2_ones, 1)
            g.wait_ge(consts, 6)
            g.affine_select(out=upto[:], in_=ones[:, 0:S], compare_op=ALU.is_ge, fill=0.0, base=0,
                            pattern=[[1, S]], channel_multiplier=-1).then_inc(consts, 1)
            g.iota(steps7[:], pattern=[[TILE, 7]], base=0, channel_multiplier=0,
                   allow_small_or_imprecise_dtypes=True).then_inc(consts, 1)
            g.iota(eidx[:], pattern=[[1, E]], base=0, channel_multiplier=0,
                   allow_small_or_imprecise_dtypes=True).then_inc(consts, 1)
            g.iota(tiles_i[:], pattern=[[1, ROUTED_TILES]], base=0, channel_multiplier=0,
                   allow_small_or_imprecise_dtypes=True).then_inc(consts, 1)

            g.wait_ge(w_loaded["x"], 16)
            g.wait_ge(w_loaded["small"], 16 * 10)

            def copy_x1(b, p, first):
                g.wait_ge(x1_done, b + 1)
                if not first:
                    g.wait_ge(x1t_pe, b - 1)
                    g.wait_ge(xb2, b - 1)
                g.sem_inc(pause, 1)
                g.tensor_copy(x1c[:, p], xres[:, b]).then_inc(x1c_done, 1)

            def split_q(b, first):
                g.wait_ge(q_sb, b + 1)
                if not first:
                    g.wait_ge(q_stored, b * 16)
                g.sem_inc(pause, 1)
                g.tensor_copy(q_hl[:, 0], qf[:]).then_inc(q_hi, 1)
                g.wait_ge(q_hi, b + 1)
                g.tensor_tensor(q_hl[:, 1], qf[:], q_hl[:, 0].bitcast(F32), ALU.subtract).then_inc(q_lo, 1)

            def stage1(b, p, i, first, last):
                if not (isinstance(b, int) and b < 2):
                    g.wait_ge(y1, b - 1)
                g.tensor_tensor(xb[:, p], xres[:, b], rows[0:S, 0], ALU.add).then_inc(xb1, 1)
                if isinstance(b, int) and b == B - 2:
                    for x in range(2):
                        copy_x1(x, x, True)
                if last:
                    split_q(0, True)
                g.wait_ge(ve1, b + 1)
                g.tensor_tensor(rstd[:, p:p + 1], veps[:, p:p + 1], minus_half[:], ALU.pow).then_inc(rstd1, 1)

            over_batches(g, stage1)

            def add_bo(b, p):
                g.wait_ge(x1c_done, b + 1)
                if not (isinstance(b, int) and b < 2):
                    g.wait_ge(y2, b - 1)
                g.tensor_tensor(xb[:, p], x1c[:, p], rows[0:S, 2], ALU.add).then_inc(xb2, 1)

            def stage2(b, p, i, first, last):
                if not first:
                    add_bo(b, p)
                if not late(b):
                    if not first:
                        copy_x1(b + 2, p, False)
                    split_q(b + 2, False)
                if not first:
                    tail(b - 1, 1 - p)

            def tail(b, p):
                g.wait_ge(ve2, b + 1)
                g.tensor_tensor(rstd[:, p:p + 1], veps[:, p:p + 1], minus_half[:], ALU.pow).then_inc(rstd2, 1)
                g.wait_ge(x2_done, b + 1)
                g.sem_inc(pause, 1)
                g.tensor_copy(xres[:, b], x2c[:, p]).then_inc(x2_kept, 1)

            add_bo(0, 0)
            copy_x1(2, 0, False)
            split_q(1, False)
            over_batches(g, stage2)
            tail(B - 1, 1)

            g.wait_ge(s_route, ROUTE_SLOTS)
            g.wait_ge(zeroed, 16 * (ROUTED_TILES + EXTRA_TILES))
            g.wait_ge(x2_kept, B)
            for b in range(B):
                g.indirect_dma_start(slots_x, bass.IndirectOffsetOnAxis(slot[:, b:b + 1], 0), xres[:, b], None).then_inc(scattered, 16)
            g.wait_ge(ys_stored, routed_tiles(g) * 16)
            g.sem_inc(pause, 1)
            for b in range(B):
                g.indirect_dma_start(ygat[:, b], None, slots_y, bass.IndirectOffsetOnAxis(slot[:, b:b + 1], 0)).then_inc(gathered[b], 16)
            for half in range(2):
                g.wait_ge(ve3s, half + 1)
                cut = slice(4 * half, 4 * half + 4)
                g.tensor_tensor(rs3[:, cut], ve3[:, cut], minus_half[:].to_broadcast([S, 4]), ALU.pow).then_inc(rstd3, 1)


        @block.tensor
        def _(pe):
            def project1(c, b, p, i, first):
                if c == 0:
                    pe.wait_ge(xT_loaded[p], (i + 1) * 16)
                if first and c in (0, 1, 2, 4):
                    pe.wait_ge(w_loaded[("v0", "v1", "q", None, "k")[c]], 16)
                if c >= 2:
                    pe.wait_ge(evac1[c - 2], b + 1)
                elif not first:
                    pe.wait_ge(evac1[c + 4], b)
                J = PE_J1[c % 2]
                if c < 2:
                    for k in range(KC):
                        mm = pe.matmul(J[0:S, :], xT[p][:, k, :], wqkv[:, k, 2 * INNER + 512 * c:2 * INNER + 512 * (c + 1)],
                                       start=(k == 0), stop=(k == KC - 1))
                else:
                    for n in range(4):
                        col = (c - 2) * 512 + n * 128
                        for k in range(KC):
                            mm = pe.matmul(J[:, n * S:(n + 1) * S], wqkv[:, k, col:col + 128], xT[p][:, k, :],
                                           start=(k == 0), stop=(k == KC - 1))
                mm.then_inc(proj1[c], 1)

            def score1(pair, b, p, first):
                pe.wait_ge(evac1[5 if pair else 4], b + 1)
                pe.wait_ge(evac1[3 if pair else 2], b + 1)
                for g in range(2):
                    if pair:
                        pe.wait_ge(exp1[g], b + 1)
                    elif not first:
                        pe.wait_ge(exp1[g + 2], b)
                for n in range(G1):
                    for g in (2 * pair, 2 * pair + 1):
                        h = head1(g, n)
                        r = slice(64 * (h % 2), 64 * (h % 2) + 64)
                        mm = pe.matmul(PE_S1[g % 2][0:S, n * S:(n + 1) * S], qT[p][r, h // 2, :], kT[p][r, h // 2, :],
                                       start=True, stop=True)
                        if n == G1 - 1:
                            mm.then_inc(scores1[g], 1)

            def turn(g, b, first):
                if first:
                    pe.wait_ge(consts, 4)
                pe.wait_ge(norm1, b * 4 + (g + 1))
                if g >= 1:
                    pe.wait_ge(pt1, b * 4 + g)
                elif not first:
                    pe.wait_ge(pt1, b * 4)
                for n in range(G1):
                    mm = pe.transpose(PE_T1[0:S, n * S:(n + 1) * S], p1[g][:, n, :], ident[0:S, 0:S])
                mm.then_inc(turn1, 1)

            def value1(pair, b, p, first):
                pe.wait_ge(pt1, b * 4 + (2 * pair + 2))
                if pair == 0:
                    pe.wait_ge(evac1[1], b + 1)
                if not first:
                    pe.wait_ge(ot1[pair], b)
                for n in range(G1):
                    for g in (2 * pair, 2 * pair + 1):
                        h = head1(g, n)
                        col = (h // 2 % 4) * S
                        mm = pe.matmul(PE_U1[pair][64 * (h % 2):64 * (h % 2) + 64, col:col + S],
                                       v1[p][:, h * D1:(h + 1) * D1], pT1[g][:, n, :], start=True, stop=True)
                mm.then_inc(pv1[pair], 1)

            def out1(b, p, first):
                pe.wait_ge(ot1[1], b + 1)
                pe.wait_ge(ot1[0], b + 1)
                if first:
                    pe.wait_ge(w_loaded["out"], 16)
                else:
                    pe.wait_ge(y1, b)
                    if isinstance(b, int) and b == B - 2:
                        pe.wait_ge(prep, 6)
                for k in range(8):
                    mm = pe.matmul(PE_W1[0:S, 0:C], oT1[p][:, k, :], wout[:, k, :], start=(k == 0), stop=(k == 7))
                mm.then_inc(wout1, 1)

            M = PE_M2

            def turn_x1(b, p, M=PE_M2):
                pe.wait_ge(x1c_done, b + 1)
                for k in range(KC):
                    mm = pe.transpose(M[:, k * S:(k + 1) * S], x1c[:, p, k * 128:(k + 1) * 128], ident[0:S, 0:S])
                mm.then_inc(x1t_pe, 1)

            def project_q(b, p, M=PE_M2):
                pe.wait_ge(x1t_sb, b + 1)
                for m in range(KC):
                    for k in range(KC):
                        mm = pe.matmul(M[:, m * S:(m + 1) * S], wx[:, 0, k, m * 128:(m + 1) * 128], x1T[:, k, :],
                                       start=(k == 0), stop=(k == KC - 1))
                mm.then_inc(q_pe, 1)

            def project_k(m, b, p, i, J=PE_J2):
                if m == 0:
                    pe.wait_ge(ctx_loaded[p], (i + 1) * 16)
                if J is PE_J2:
                    if m == 0:
                        pe.wait_ge(v_sb, b * KT)
                    else:
                        pe.wait_ge(k_lo, b * KC + m)
                for k in range(KC):
                    mm = pe.matmul(J[:, 0:S2], wx[:, 1, k, m * 128:(m + 1) * 128], ctxT[:, p, k, :],
                                   start=(k == 0), stop=(k == KC - 1))
                mm.then_inc(k_pe, 1)

            def project_v(t, b, p, J=PE_J2):
                if J is PE_J2:
                    if t == 0:
                        pe.wait_ge(k_lo, b * KC + KC)
                    else:
                        pe.wait_ge(v_sb, b * KT + t)
                for k in range(KC):
                    mm = pe.matmul(J[0:SK, 0:C], ctxT[:, p, k, t * SK:(t + 1) * SK], wx[:, 2, k, :],
                                   start=(k == 0), stop=(k == KC - 1))
                mm.then_inc(v_pe, 1)

            for c in range(6):
                project1(c, 0, 0, 0, True)

            def first_of_stage2(c):
                J = PE_J1[c % 2]
                if c == 0:
                    pe.wait_ge(w_loaded["small"], 16 * 10)
                    pe.wait_ge(evac1[4], B)
                    turn_x1(0, 0, J)
                elif c == 1:
                    pe.wait_ge(evac1[5], B)
                    project_q(0, 0, J)
                elif c == 2:
                    project_k(0, 0, 0, 0, J)
                elif c == 3:
                    pe.wait_ge(q_sb, 1)
                    project_k(1, 0, 0, 0, J)
                else:
                    pe.wait_ge(k_lo, c - 3)
                    project_v(c - 4, 0, 0, J)

            def stage1(b, p, i, first, last):
                j = i + p
                proj = first_of_stage2 if last else (lambda c: project1(c, b + 1, 1 - p, j, False))
                score1(0, b, p, first)
                if not first:
                    out1(b - 1, 1 - p, isinstance(b, int) and b == 1)
                proj(0)
                if first:
                    proj(1)
                score1(1, b, p, first)
                if not first:
                    proj(1)
                turn(0, b, first)
                proj(2)
                turn(1, b, first)
                proj(3)
                value1(0, b, p, first)
                turn(2, b, first)
                proj(4)
                turn(3, b, first)
                proj(5)
                value1(1, b, p, first)
                if isinstance(b, int) and b == B - 2:
                    pe.wait_ge(prep, 5)
                    pe.wait_ge(y1, b)
                    pe.matmul(PE_W1[:, 0:S], anyw[:], ident[0:S, 0:S], start=True, stop=True).then_inc(q_any, 1)

            over_batches(pe, stage1)
            pe.wait_ge(v_sb, 1)
            project_v(2, 0, 0, PE_J1[0])
            out1(B - 1, 1, False)

            def score2(h, b, p, i, first):
                if h >= 3:
                    pe.wait_ge(max2[(h - 3) % 4], heads_done(b, h - 3))
                elif not first:
                    before = max(j for j in range(H) if (j + 1 - p) % 3 == (h + p) % 3)
                    pe.wait_ge(max2[before % 4], heads_done(b - 1, before))
                if h == 0:
                    pe.wait_ge(qst_loaded[p], (i + 1) * 16 * STACK_DMAS)
                    pe.wait_ge(kst_loaded[p], (i + 1) * 16 * STACK_DMAS)
                r = slice(64 * (h % 2), 64 * (h % 2) + 64)
                pe.matmul(PE_S2[(h + p) % 3][0:S, 0:S2P], qst[r, p, h // 2, :], kst[r, p, h // 2, :],
                          start=True, stop=True).then_inc(scores2[h % 4], 1)

            def turn2_(h, b, first):
                pe.wait_ge(exp2[h % 4], heads_done(b, h))
                if h >= 2:
                    pe.wait_ge(pt2[(h - 2) % 4], heads_done(b, h - 2))
                elif not first:
                    pe.wait_ge(pt2[(H - 2 + h) % 4], heads_done(b - 1, H - 2 + h))
                else:
                    pe.wait_ge(k_lo, 2 * KC)
                for t in range(KT):
                    mm = pe.transpose(PE_T2[h % 2][0:SK, t * S:(t + 1) * S], p2[h % 8][:, t * SK:(t + 1) * SK], ident[0:S, 0:S])
                mm.then_inc(turn2[h % 4], 1)

            def value2(q, b, p, first):
                for j in range(4):
                    pe.wait_ge(pt2[j], heads_done(b, 4 * q + j))
                if q == 0:
                    pe.wait_ge(v_sb, b * KT + KT)
                    if not first:
                        pe.wait_ge(ot2, b)
                for t in range(KT):
                    for j in range(4):
                        h = 4 * q + j
                        mm = pe.matmul(PE_V2[VP * j:VP * j + VP, q * S:(q + 1) * S], v2[:, p, t, h, :], pT2[0:SK, h % PT_RING, t, :],
                                       start=(t == 0), stop=(t == KT - 1))
                mm.then_inc(pv2, 1)

            def turn_o(b):
                pe.wait_ge(ot2, b + 1)
                for n in range(4):
                    mm = pe.transpose(M[0:S, n * 128:(n + 1) * 128], oT2[:, n, :], ident[:])
                mm.then_inc(on_pe, 1)

            def turn_on(b):
                pe.wait_ge(on_sb, b + 1)
                for k in range(KC):
                    mm = pe.transpose(M[:, k * S:(k + 1) * S], o2[:, k * 128:(k + 1) * 128], ident[0:S, 0:S])
                mm.then_inc(ont_pe, 1)

            def out2(b):
                pe.wait_ge(ont_sb, b + 1)
                for k in range(KC):
                    mm = pe.matmul(M[0:S, 0:C], on2T[:, k, :], wx[:, 3, k, :], start=(k == 0), stop=(k == KC - 1))
                mm.then_inc(wo_pe, 1)

            def turn_x2(b, p):
                pe.wait_ge(x2_done, b + 1)
                for k in range(KC):
                    mm = pe.transpose(M[:, k * S:(k + 1) * S], x2c[:, p, k * 128:(k + 1) * 128], ident[0:S, 0:S])
                mm.then_inc(x2t_pe, 1)

            turn_x1(1, 1)
            project_q(1, 1)
            project_k(0, 1, 1, 0, PE_T2[1])
            pe.wait_ge(v_sb, 2)
            project_k(1, 1, 1, 0, PE_T2[0])
            pe.wait_ge(v_sb, KT)
            pe.wait_ge(y1, B)

            def stage2(b, p, i, first, last):
                def turn_x1_next():
                    if isinstance(b, int) and b < 2:
                        pe.wait_ge(q_sb, b + 2)
                    else:
                        pe.wait_ge(x2t_sb, b - 1)
                    turn_x1(b + 2, p)

                def turn_o_prev():
                    if late(b):
                        pe.wait_ge(x2t_sb, b - 1)
                    else:
                        pe.wait_ge(q_sb, b + 3)
                    turn_o(b - 1)

                nxt = {} if last else {
                    6: lambda: project_v(0, b + 1, 1 - p), 8: lambda: project_v(1, b + 1, 1 - p), 10: lambda: project_v(2, b + 1, 1 - p)}
                nxt.update({} if late(b) else {
                    2: turn_x1_next, 4: lambda: project_q(b + 2, p),
                    12: lambda: project_k(0, b + 2, p, i + 1), 14: lambda: project_k(1, b + 2, p, i + 1)})
                prev = {} if first else {
                    7: turn_o_prev, 8: lambda: turn_on(b - 1), 11: lambda: out2(b - 1), 15: lambda: turn_x2(b - 1, 1 - p)}

                for h in range(H):
                    score2(h, b, p, i, first)
                    if h >= LAG:
                        turn2_(h - LAG, b, first)
                    elif not first:
                        turn2_(H - LAG + h, b - 1, False)
                    if h in nxt:
                        nxt[h]()
                    if h in prev:
                        prev[h]()
                    if h % 4 == 1 and h >= 9:
                        value2((h - 9) // 4, b, p, first)
                    elif h % 4 == 1 and not first:
                        value2((h + 7) // 4, b - 1, 1 - p, isinstance(b, int) and b == 1)

            over_batches(pe, stage2)
            for h in range(H - LAG, H):
                turn2_(h, B - 1, False)
            for q in (2, 3):
                value2(q, B - 1, 1, False)
            def logits_t(b, n, bk):
                pe.wait_ge(x2t_sb, b + n)
                for k in range(KC):
                    mm = pe.matmul(bk[0:E, 0:n * S], routerT[:, k, :], x2T[:, k, b * S:(b + n) * S],
                                   start=(k == 0), stop=(k == KC - 1))
                mm.then_inc(s_logit, 1)

            def shared(n, part):
                if part == 0 and n >= 2:
                    pe.wait_ge(sh_h, n - 1)
                grp, m = n // HT, n % HT
                for k in range(KC):
                    mm = pe.matmul(bank[2 + 2 * (n % 2) + part][:, 0:4 * S], ugs[:, k, part * HID + m * 128:part * HID + (m + 1) * 128],
                                   x2T[:, k, grp * 4 * S:(grp + 1) * 4 * S], start=(k == 0), stop=(k == KC - 1))
                mm.then_inc(sh_gu, 1)

            def shared_down(grp):
                pe.wait_ge(sh_h, (grp + 1) * HT)
                for n in range(4):
                    b = grp * 4 + n
                    if b >= 2:
                        pe.wait_ge(sh_ysb, b - 1)
                    for m in range(HT):
                        mm = pe.matmul(bank[6 + b % 2][0:S, 0:C], hTs[:, m, n * S:(n + 1) * S], dns[:, m, :],
                                       start=(m == 0), stop=(m == HT - 1))
                    mm.then_inc(sh_y, 1)

            pe.wait_ge(w_loaded["shared"], 32)
            logits_t(0, 4, bank[0])
            turn_o(B - 1)
            logits_t(4, 3, bank[1])
            turn_on(B - 1)
            shared(0, 0)
            out2(B - 1)
            shared(0, 1)
            shared(1, 0)
            turn_x2(B - 1, 1)
            shared(1, 1)
            logits_t(B - 1, 1, bank[7])
            for b in range(B):
                if b in (0, B - 1):
                    pe.wait_ge(lgt_sb, 2 if b == 0 else 3)
                mm = pe.transpose(bank[6][0:S, b * E:(b + 1) * E], lgT[:, b * S:(b + 1) * S], ident[0:E, 0:E])
            mm.then_inc(s_logit, 1)
            shared(2, 0)
            shared(2, 1)
            pe.wait_ge(s_route, ROUTE_ONEHOT)
            pe.matmul(bank[1][0:S, 0:B * E], upto[:], onehot[:].rearrange("p b e -> p (b e)"), start=True, stop=True)
            pe.matmul(bank[1][:, B * E:2 * B * E], ones[:], onehot[:].rearrange("p b e -> p (b e)"),
                      start=True, stop=True).then_inc(s_incl, 1)
            for n in (3, 4):
                shared(n, 0)
                shared(n, 1)
            shared_down(0)
            for n in (5, 6):
                shared(n, 0)
                shared(n, 1)

            tiles = routed_tiles(pe)
            XB, GB, UB, HB, YB = bank[0], bank[2], bank[4], bank[1], bank[6]

            def head_tile(t, first):
                pe.wait_ge(xs_loaded, t * 16 + 16)
                if not first:
                    pe.wait_ge(xst_sb, t)
                for k in range(KC):
                    mm = pe.transpose(XB[:, k * 128:(k + 1) * 128], xs[:, k * 128:(k + 1) * 128], ident[:])
                mm.then_inc(xst_pe, 1)

            def gate(t, e, first):
                pe.wait_ge(xst_sb, t + 1)
                if not first:
                    pe.wait_ge(g_sb, t)
                for k in range(KC):
                    mm = pe.matmul(GB[:, :], xsT[:, k, :], arena[:, bass.ds(e[k], HID)], start=(k == 0), stop=(k == KC - 1))
                mm.then_inc(gu_pe, 1)

            def up(t, e):
                for k in range(KC):
                    mm = pe.matmul(UB[:, :], xsT[:, k, :], arena[:, bass.ds(e[KC + k], HID)], start=(k == 0), stop=(k == KC - 1))
                mm.then_inc(gu_pe, 1)

            def turn_h(t, first):
                pe.wait_ge(h_sb, t + 1)
                if not first:
                    pe.wait_ge(ht_sb, t)
                for m in range(HT):
                    mm = pe.transpose(HB[:, m * 128:(m + 1) * 128], hr[:, m * 128:(m + 1) * 128], ident[:])
                mm.then_inc(ht_pe, 1)

            def down(t, e, first):
                pe.wait_ge(ht_sb, t + 1)
                if first:
                    pe.wait_ge(sh_ysb, B)
                else:
                    pe.wait_ge(yr_sb, t)
                for m in range(HT):
                    mm = pe.matmul(YB[:, 0:C], hrT[:, m, :], arena[:, bass.ds(e[m], C)], start=(m == 0), stop=(m == HT - 1))
                mm.then_inc(yr_pe, 1)

            def of_expert(t, offsets):
                e = pe.value_load(expert[0:1, bass.ds(t, 1)], min_val=0, max_val=E - 1)
                return [pe.snap(e * (UG + DN) + o) for o in offsets]

            def gates_ups(t):
                return of_expert(t, [part * HID + k * 2 * HID for part in range(2) for k in range(KC)])

            def downs(t):
                return of_expert(t, [UG + m * C for m in range(HT)])

            head_tile(0, True)
            e = gates_ups(0)
            shared(7, 0)
            shared(7, 1)
            pe.wait_ge(w_experts, 32 * E)
            pe.wait_ge(sh_h, 7)
            gate(0, e, True)
            shared_down(1)
            up(0, e)
            head_tile(1, False)

            def step(t, first, last):
                e = gates_ups(t + 1)
                gate(t + 1, e, False)
                d = downs(t)
                turn_h(t, first)
                up(t + 1, e)
                if not last:
                    head_tile(t + 2, False)
                down(t, d, first)

            step(0, True, False)
            with pe.Fori(1, tiles - 2) as t:
                step(t, False, False)
            step(tiles - 2, False, True)
            d = downs(tiles - 1)
            turn_h(tiles - 1, False)
            down(tiles - 1, d, False)

        @block.scalar
        def _(act):
            def evac_v(c, b, p, first):
                act.wait_ge(proj1[c], b + 1)
                if not first:
                    act.wait_ge(pv1[1], b - 1)
                act.activation(v1[p][:, 512 * c:512 * (c + 1)], PE_J1[c][0:S, :], ACT.Copy).then_inc(evac1[c], 1)

            def exps(g, b, first):
                act.wait_ge(max1, b * 4 + (g + 1))
                if not first:
                    act.wait_ge(turn1, b * 4 + (g - 3))
                for n in range(G1):
                    h = G1 * g + n
                    e = act.activation(p1[g][:, n, :], PE_S1[g % 2][0:S, n * S:(n + 1) * S], ACT.Exp,
                                       bias=nm1[:, h:h + 1], accum_out=rs1[:, h:h + 1])
                e.then_inc(exp1[g], 1)

            def evac_o(half, b, p, early):
                act.wait_ge(pv1[half], b + 1)
                if half == 0 and not early:
                    act.wait_ge(wout1, b - 1)
                act.activation(oT1[p][:, 4 * half:4 * half + 4, :],
                               PE_U1[half][:, 0:4 * S].rearrange("p (k n) -> p k n", k=4), ACT.Copy).then_inc(ot1[half], 1)

            def evac_k(m, b, first, J=PE_J2):
                act.wait_ge(k_pe, b * KC + (m + 1))
                if m == 0 and not first:
                    act.wait_ge(k_stored, b * 16)
                act.activation(k_hl[:, 0, m, 0:S2], J[:, 0:S2], ACT.Identity, bias=cols[:, 1, m:m + 1]).then_inc(k_hi, 1)

            def turn_evac(kind, b, p, M=PE_M2):
                if kind == "x1":
                    act.wait_ge(x1t_pe, b + 1)
                    act.activation(x1T[:], M[:, 0:KC * S].rearrange("p (k n) -> p k n", k=KC), ACT.Copy).then_inc(x1t_sb, 1)
                if kind == "on":
                    act.wait_ge(ont_pe, b + 1)
                    act.activation(on2T[:], M[:, 0:KC * S].rearrange("p (k n) -> p k n", k=KC), ACT.Copy).then_inc(ont_sb, 1)
                if kind == "x2":
                    act.wait_ge(x2t_pe, b + 1)
                    act.activation(x2T[:, :, bass.ds(b * S, S)], M[:, 0:KC * S].rearrange("p (k n) -> p k n", k=KC),
                                   ACT.Copy).then_inc(x2t_sb, 1)

            for c in range(2):
                evac_v(c, 0, 0, True)

            def stage1(b, p, i, first, last):
                early = isinstance(b, int) and b < 2
                exps(0, b, first)
                exps(1, b, first)
                if not last:
                    evac_v(0, b + 1, 1 - p, first)
                else:
                    turn_evac("x1", 0, 0, PE_J1[0])
                exps(2, b, first)
                if not last:
                    evac_v(1, b + 1, 1 - p, first)
                exps(3, b, first)
                if last:
                    for m in range(KC):
                        evac_k(m, 0, True, PE_J1[m])
                evac_o(0, b, p, early)
                evac_o(1, b, p, early)

            over_batches(act, stage1)

            def exps2(h, b):
                act.wait_ge(max2[h % 4], heads_done(b, h))
                act.activation(p2[h % 8], p2[h % 8], ACT.Exp, bias=nm2[:, h:h + 1], scale=-1.0).then_inc(exp2[h % 4], 1)

            def evac_pt(h, b, first):
                act.wait_ge(turn2[h % 4], heads_done(b, h))
                wait_ring(act, h, b, first)
                act.activation(pT2[0:SK, h % PT_RING], PE_T2[h % 2][0:SK, 0:KT * S].rearrange("p (k n) -> p k n", k=KT),
                               ACT.Copy).then_inc(pt2[h % 4], 1)

            turn_evac("x1", 1, 1)
            for m in range(KC):
                evac_k(m, 1, False, PE_T2[1 - m])

            def stage2(b, p, i, first, last):
                for h in range(H):
                    if h in (13, 15) and not late(b):
                        evac_k(h // 15, b + 2, False)
                    if (h - LAG) % 4 != 3:
                        if h >= LAG:
                            evac_pt(h - LAG, b, first)
                        elif not first:
                            evac_pt(H - LAG + h, b - 1, False)
                    exps2(h, b)
                    if not late(b):
                        if h == 2:
                            turn_evac("x1", b + 2, p)
                    if not first:
                        if h == 9:
                            turn_evac("on", b - 1, 1 - p)
                        if h == 15:
                            turn_evac("x2", b - 1, 1 - p)

            over_batches(act, stage2)
            for h in range(H - LAG, H - 1):
                evac_pt(h, B - 1, False)
            def evac_logits(n, b0, b1, bk):
                act.wait_ge(s_logit, n)
                act.activation(lgT[:, b0 * S:b1 * S], bk[0:E, 0:(b1 - b0) * S], ACT.Copy).then_inc(lgt_sb, 1)

            def shared_silu(n):
                act.wait_ge(sh_gu, 2 * n + 1)
                if n >= 1:
                    act.wait_ge(sh_h, n)
                act.activation(gs[:], bank[2 + 2 * (n % 2)][:, 0:4 * S], ACT.Silu).then_inc(sh_g, 1)

            evac_logits(1, 0, 4, bank[0])
            turn_evac("on", B - 1, 1)
            evac_logits(2, 4, B - 1, bank[1])
            shared_silu(0)
            turn_evac("x2", B - 1, 1)

            for n in range(1, 2 * HT):
                shared_silu(n)

            def tile_silu(t, first):
                act.wait_ge(gu_pe, t * 2 + 1)
                if not first:
                    act.wait_ge(h_sb, t)
                act.activation(gr[:], bank[2][:], ACT.Silu).then_inc(g_sb, 1)

            def evac_h(t, first):
                act.wait_ge(ht_pe, t + 1)
                if not first:
                    act.wait_ge(yr_pe, t)
                act.activation(hrT[:], bank[1][:].rearrange("p (k n) -> p k n", k=HT), ACT.Copy).then_inc(ht_sb, 1)

            tiles = routed_tiles(act)
            tile_silu(0, True)
            tile_silu(1, False)
            evac_h(0, True)
            with act.Fori(1, tiles - 1) as t:
                tile_silu(t + 1, False)
                evac_h(t, False)
            evac_h(tiles - 1, False)

        @block.vector
        def _(v):
            def evac_qk(c, b, p, first):
                v.wait_ge(proj1[c], b + 1)
                if not first:
                    v.wait_ge(scores1[3], b - 1)
                dst = (qT if c < 4 else kT)[p][:, 4 * (c % 2):4 * (c % 2) + 4, :]
                v.tensor_scalar(dst, PE_J1[c % 2][:, 0:4 * S].rearrange("p (k n) -> p k n", k=4),
                                D1 ** -0.5 if c < 4 else 1.0, None, ALU.mult).then_inc(evac1[c], 1)

            def rowmax(g, b, first):
                v.wait_ge(scores1[g], b + 1)
                if not first:
                    v.wait_ge(exp1[g], b)
                v.tensor_reduce(nm1[:, G1 * g:G1 * g + G1], PE_S1[g % 2][0:S, 0:G1 * S].rearrange("p (k n) -> p k n", k=G1),
                                AX.X, ALU.max, negate=True).then_inc(max1, 1)

            def normalise(g, b):
                c = slice(G1 * g, G1 * g + G1)
                v.wait_ge(exp1[g], b + 1)
                v.reciprocal(rc1[:, c], rs1[:, c]).then_inc(rcp1, 1)
                v.wait_ge(rcp1, b * 4 + (g + 1))
                v.tensor_tensor(p1[g], p1[g], rc1[:, c].unsqueeze(2).to_broadcast([S, G1, S]), ALU.mult).then_inc(norm1, 1)

            def evac_pt(g, b, first):
                v.wait_ge(turn1, b * 4 + (g + 1))
                if not first:
                    v.wait_ge(pv1[g // 2], b)
                v.tensor_copy(pT1[g], PE_T1[0:S, 0:G1 * S].rearrange("p (k n) -> p k n", k=G1)).then_inc(pt1, 1)

            def layernorm_a(src, done, added, b, p, sy, ss, sa, sv):
                v.wait_ge(done, b + 1)
                v.wait_ge(added, b + 1)
                v.tensor_tensor(ybuf[:, p], src, xb[:, p], ALU.add).then_inc(sy, 1)
                v.wait_ge(sy, b + 1)
                v.bn_stats(stats[:, p], ybuf[:, p]).then_inc(ss, 1)
                v.wait_ge(ss, b + 1)
                v.sem_inc(pause, 1)
                v.bn_aggr(mv[:, p], stats[:, p]).then_inc(sa, 1)
                v.wait_ge(sa, b + 1)
                v.tensor_scalar(veps[:, p:p + 1], mv[:, p, 1:2], EPS, None, ALU.add).then_inc(sv, 1)

            def ln1_a(b, p):
                layernorm_a(PE_W1[0:S, 0:C], wout1, xb1, b, p, y1, st1, ag1, ve1)

            def ln1_b(b, p):
                v.wait_ge(rstd1, b + 1)
                v.tensor_scalar(xres[:, b], ybuf[:, p], mv[:, p, 0:1], rstd[:, p:p + 1], ALU.subtract, ALU.mult).then_inc(x1_done, 1)

            def mask_bias():
                v.wait_ge(w_loaded["mask"], 16)
                v.tensor_scalar(mask0[:], mask_i[:], 0.0, None, ALU.is_equal).then_inc(prep, 1)
                v.wait_ge(prep, 1)
                v.tensor_reduce(allm[:], mask0[:], AX.X, ALU.min).then_inc(prep, 1)
                v.wait_ge(prep, 2)
                v.tensor_scalar(anym[:], allm[:], -1.0, 1.0, ALU.mult, ALU.add).then_inc(prep, 1)
                v.wait_ge(prep, 3)
                v.wait_ge(consts, 6)
                v.tensor_scalar(anyw[:], ones[:], anym[:], None, ALU.mult).then_inc(prep, 1)
                v.tensor_scalar(bias[:], mask0[:], anym[:], MASKED, ALU.mult, ALU.mult).then_inc(prep, 1)

            def query_scale():
                v.wait_ge(q_any, 1)
                v.tensor_scalar(qscale[:], PE_W1[:, 0:S], -D2 ** -0.5, None, ALU.mult).then_inc(prep, 1)

            def evac_q(b, first, M=PE_M2):
                v.wait_ge(q_pe, b + 1)
                if not first:
                    v.wait_ge(q_lo, b)
                for m in range(KC):
                    last = v.scalar_tensor_tensor(out=qf[:, m, :], in0=M[:, m * S:(m + 1) * S],
                                                  scalar=cols[:, 0, m:m + 1], in1=qscale[:], op0=ALU.add, op1=ALU.mult)
                last.then_inc(q_sb, 1)

            def split_k(m, b, J=PE_J2):
                v.wait_ge(k_hi, b * KC + (m + 1))
                v.scalar_tensor_tensor(out=k_hl[:, 1, m, 0:S2], in0=J[:, 0:S2], scalar=cols[:, 1, m:m + 1],
                                       in1=k_hl[:, 0, m, 0:S2].bitcast(F32), op0=ALU.add, op1=ALU.subtract).then_inc(k_lo, 1)

            def evac_v(t, b, p, first, J=PE_J2):
                v.wait_ge(v_pe, b * KT + (t + 1))
                if not first and t == 0:
                    v.wait_ge(pv2, 4 * b - 4)
                v.tensor_tensor(v2[:, p, t, :, 0:D2], J[0:SK, 0:C].rearrange("p (h d) -> p h d", h=H),
                                rows[0:SK, 1, :].rearrange("p (h d) -> p h d", h=H), ALU.add).then_inc(v_sb, 1)

            for c in range(2, 6):
                evac_qk(c, 0, 0, True)

            def stage1(b, p, i, first, last):
                if last:
                    query_scale()
                rowmax(0, b, first)
                rowmax(1, b, first)
                if not first:
                    ln1_a(b - 1, 1 - p)
                normalise(0, b)
                rowmax(2, b, first)
                normalise(1, b)
                rowmax(3, b, first)
                if not first and not last:
                    ln1_b(b - 1, 1 - p)
                if last:
                    evac_q(0, True, PE_J1[1])
                evac_pt(0, b, first)
                if not last:
                    evac_qk(2, b + 1, 1 - p, first)
                normalise(2, b)
                evac_pt(1, b, first)
                if not last:
                    evac_qk(3, b + 1, 1 - p, first)
                else:
                    split_k(0, 0, PE_J1[0])
                normalise(3, b)
                if last:
                    split_k(1, 0, PE_J1[1])
                evac_pt(2, b, first)
                if not last:
                    evac_qk(4, b + 1, 1 - p, first)
                else:
                    ln1_b(b - 1, 1 - p)
                    v.wait_ge(v2_ones, 2)
                    evac_v(0, 0, 0, True, PE_J1[0])
                evac_pt(3, b, first)
                if not last:
                    evac_qk(5, b + 1, 1 - p, first)
                else:
                    evac_v(1, 0, 0, True, PE_J1[1])
                if first:
                    mask_bias()

            over_batches(v, stage1)
            evac_v(2, 0, 0, True, PE_J1[0])
            ln1_a(B - 1, 1)
            ln1_b(B - 1, 1)
            def mask_and_max(h, b, p, first):
                v.wait_ge(scores2[h % 4], heads_done(b, h))
                if h >= 8:
                    v.wait_ge(turn2[h % 4], heads_done(b, h - 8))
                elif not first:
                    v.wait_ge(turn2[h % 4], heads_done(b - 1, h + 8))
                v.sem_inc(pause, 1)
                v.tensor_tensor_reduce(p2[h % 8], PE_S2[(h + p) % 3][0:S, 0:S2], bias[:], 1.0, 3e38, ALU.add, ALU.min,
                                       accum_out=nm2[:, h:h + 1]).then_inc(max2[h % 4], 1)

            def evac_pt2(h, b, first):
                v.wait_ge(turn2[h % 4], heads_done(b, h))
                wait_ring(v, h, b, first)
                v.tensor_copy(pT2[0:SK, h % PT_RING], PE_T2[h % 2][0:SK, 0:KT * S].rearrange("p (k n) -> p k n", k=KT)).then_inc(pt2[h % 4], 1)

            def evac_ot(b, first):
                v.wait_ge(pv2, 4 * b + 4)
                if not first:
                    v.wait_ge(on_pe, b)
                v.tensor_copy(oT2[:], PE_V2[:, 0:4 * S].rearrange("p (k n) -> p k n", k=4)).then_inc(ot2, 1)

            def normalise2(b):
                o = PE_M2[0:S, :].rearrange("p (h d) -> p h d", h=H)
                v.wait_ge(on_pe, b + 1)
                v.reciprocal(rc2[:].unsqueeze(2), o[:, :, D2:D2 + 1]).then_inc(rc_done, 1)
                v.wait_ge(rc_done, b + 1)
                v.tensor_tensor(o2[:].rearrange("p (h d) -> p h d", h=H), o[:, :, 0:D2],
                                rc2[:].unsqueeze(2).to_broadcast([S, H, D2]), ALU.mult).then_inc(on_sb, 1)

            def ln2_a(b, p):
                layernorm_a(PE_M2[0:S, 0:C], wo_pe, xb2, b, p, y2, st2, ag2, ve2)

            def ln2_b(b, p, early):
                v.wait_ge(rstd2, b + 1)
                if not early:
                    v.wait_ge(x2t_pe, b - 1)
                    v.wait_ge(x2_kept, b - 1)
                v.tensor_scalar(x2c[:, p], ybuf[:, p], mv[:, p, 0:1], rstd[:, p:p + 1], ALU.subtract, ALU.mult).then_inc(x2_done, 1)

            evac_q(1, False)
            for m in range(KC):
                split_k(m, 1, PE_T2[1 - m])

            def stage2(b, p, i, first, last):
                for h in range(H):
                    mask_and_max(h, b, p, first)
                    if (h - LAG) % 4 == 3:
                        if h >= LAG:
                            evac_pt2(h - LAG, b, first)
                        elif not first:
                            evac_pt2(H - LAG + h, b - 1, False)
                    if not late(b):
                        if h == 5:
                            evac_q(b + 2, False)
                        if h in (13, 15):
                            split_k(h // 15, b + 2)
                    if not last and h in (7, 9, 11):
                        evac_v((7, 9, 11).index(h), b + 1, 1 - p, first)
                    if not first:
                        if h == 5:
                            evac_ot(b - 1, isinstance(b, int) and b == 1)
                        if h == 7:
                            normalise2(b - 1)
                        if h == 12:
                            ln2_a(b - 1, 1 - p)
                        if h == 14:
                            ln2_b(b - 1, 1 - p, isinstance(b, int) and b <= 2)

            over_batches(v, stage2)
            evac_pt2(H - 1, B - 1, False)
            evac_ot(B - 1, False)
            normalise2(B - 1)
            ln2_a(B - 1, 1)
            ln2_b(B - 1, 1, False)

            def shared_product(k):
                v.wait_ge(sh_g, k + 1)
                v.wait_ge(sh_gu, 2 * k + 2)
                v.tensor_tensor(hTs[:, k % HT, :], gs[:], bank[3 + 2 * (k % 2)][:, 0:4 * S], ALU.mult).then_inc(sh_h, 1)

            n = [0]

            def chain(ins):
                n[0] += 1
                ins.then_inc(s_route, 1)
                v.wait_ge(s_route, n[0])

            v.wait_ge(s_logit, 3)
            v.tensor_copy(lgT[:, (B - 1) * S:B * S], bank[7][0:E, 0:S]).then_inc(lgt_sb, 1)
            shared_product(0)
            v.wait_ge(s_logit, 4)
            chain(v.tensor_copy(logit[:], bank[6][0:S, 0:B * E].rearrange("p (b e) -> p b e", b=B)))
            for b in range(B):
                m = v.max(top8[:, b], logit[:, b])
            chain(m)
            for b in range(B):
                m = v.max_index(tidx[:, b], top8[:, b], logit[:, b])
            chain(m)
            v.wait_ge(consts, 10)
            chain(v.tensor_tensor(onehot[:], eidx[0:S].unsqueeze(1).to_broadcast([S, B, E]),
                                  tidx[:, :, 0:1].to_broadcast([S, B, E]), ALU.is_equal))
            assert n[0] == ROUTE_ONEHOT
            shared_product(1)
            v.wait_ge(s_incl, 1)
            chain(v.tensor_copy(incl[:], bank[1][0:S, 0:B * E].rearrange("p (b e) -> p b e", b=B)))
            v.memset(cnt[:, 0, :], 0.0)
            chain(v.memset(ends[:, 0:1], 0.0))
            for b in range(B):
                chain(v.tensor_tensor(cnt[:, b + 1, :], bank[1][:, (B + b) * E:(B + b + 1) * E], cnt[:, b, :], ALU.add))
            shared_product(2)
            chain(v.tensor_tensor(fills[:], steps7[:].unsqueeze(1).to_broadcast([128, E, 7]),
                                  cnt[:, B, :].unsqueeze(2).to_broadcast([128, E, 7]), ALU.is_lt))
            chain(v.tensor_reduce(ntile[:], fills[:], AX.X, ALU.add))
            for e in range(E):
                if e == 0:
                    v.tensor_copy(ends[:, 1:2], ntile[:, 0:1]).then_inc(s_eload, 1)
                else:
                    v.wait_ge(s_eload, e)
                    v.tensor_tensor(ends[:, e + 1:e + 2], ends[:, e:e + 1], ntile[:, e:e + 1], ALU.add).then_inc(s_eload, 1)
            v.wait_ge(s_eload, E)
            shared_product(3)
            chain(v.tensor_tensor(pos[:], incl[:], cnt[0:S, 0:B, :], ALU.add))
            chain(v.scalar_tensor_tensor(out=incl[:], in0=ends[0:S, 0:E].unsqueeze(1).to_broadcast([S, B, E]), scalar=float(TILE),
                                         in1=pos[:], op0=ALU.mult, op1=ALU.add))
            chain(v.tensor_tensor(pos[:], incl[:], onehot[:], ALU.mult))
            chain(v.tensor_reduce(slotf[:], pos[:], AX.X, ALU.add))
            chain(v.tensor_scalar(slot[:], slotf[:], -1.0, None, ALU.add))
            assert n[0] == ROUTE_SLOTS
            chain(v.tensor_tensor(past[:], tiles_i[:].unsqueeze(2).to_broadcast([1, ROUTED_TILES, E - 1]),
                                  ends[0:1, 1:E].unsqueeze(1).to_broadcast([1, ROUTED_TILES, E - 1]), ALU.is_ge))
            chain(v.tensor_reduce(expertf[:], past[:], AX.X, ALU.add))
            chain(v.tensor_copy(expert[:], expertf[:]))
            chain(v.tensor_tensor(taken[:], tiles_i[:, FEWEST_TILES:], ends[0:1, E:E + 1].to_broadcast([1, EXTRA_TILES]), ALU.is_lt))
            chain(v.tensor_reduce(extraf[:], taken[:], AX.X, ALU.add))
            chain(v.tensor_copy(extra_i[:], extraf[:]))
            assert n[0] == ROUTE_EXPERTS

            def shared_sum(b):
                v.wait_ge(sh_y, b + 1)
                v.tensor_tensor(ysh[:, b], bank[6 + b % 2][0:S, 0:C], xres[:, b], ALU.add).then_inc(sh_ysb, 1)

            v.wait_ge(x2_kept, B)
            for b in range(4):
                shared_sum(b)
            for k in range(4, 7):
                if k == 4:
                    v.wait_ge(sh_y, 4)
                shared_product(k)

            def evac_x(t, first):
                v.wait_ge(xst_pe, t + 1)
                if not first:
                    v.wait_ge(gu_pe, t * 2)
                v.tensor_copy(xsT[:], bank[0][:, 0:KC * 128].rearrange("p (k n) -> p k n", k=KC)).then_inc(xst_sb, 1)

            def product(t, first):
                v.wait_ge(g_sb, t + 1)
                v.wait_ge(gu_pe, t * 2 + 2)
                if not first:
                    v.wait_ge(ht_pe, t)
                v.tensor_tensor(hr[:], gr[:], bank[4][:], ALU.mult).then_inc(h_sb, 1)

            def evac_y(t, first):
                v.wait_ge(yr_pe, t + 1)
                if not first:
                    v.wait_ge(ys_stored, t * 16)
                v.tensor_copy(yr[:], bank[6][:, 0:C]).then_inc(yr_sb, 1)

            evac_x(0, True)
            shared_product(7)
            for b in range(4, B):
                shared_sum(b)
            evac_x(1, False)
            product(0, True)
            product(1, False)
            evac_x(2, False)
            evac_y(0, True)
            tiles = routed_tiles(v)
            with v.Fori(1, tiles - 2) as t:
                product(t + 1, False)
                evac_x(t + 2, False)
                evac_y(t, False)
            product(tiles - 1, False)
            evac_y(tiles - 2, False)
            evac_y(tiles - 1, False)

            def final(b):
                v.tensor_scalar(ygat[:, b], ysh[:, b], mv3[:, b, 0:1], rs3[:, b:b + 1], ALU.subtract, ALU.mult).then_inc(done3, 1)

            for n in range(B + 2):
                if n < B:
                    v.wait_ge(gathered[n], 16)
                    v.tensor_tensor(ysh[:, n], ysh[:, n], ygat[:, n], ALU.add).then_inc(sum3, 1)
                if 1 <= n < B + 1:
                    v.wait_ge(sum3, n)
                    v.bn_stats(st3[:, n - 1], ysh[:, n - 1]).then_inc(stats3, 1)
                if n >= 2:
                    v.wait_ge(stats3, n - 1)
                    v.bn_aggr(mv3[:, n - 2], st3[:, n - 2]).then_inc(aggr3, 1)
                if n in (5, 9):
                    half = (n - 5) // 4
                    v.wait_ge(aggr3, 4 * half + 4)
                    v.tensor_scalar(ve3[:, 4 * half:4 * half + 4], mv3[:, 4 * half:4 * half + 4, 1], EPS, None, ALU.add).then_inc(ve3s, 1)
            for b in range(B):
                if b % 4 == 0:
                    v.wait_ge(rstd3, b // 4 + 1)
                final(b)


def kernel(**inputs):
    import numpy as np
    import concourse.bacc as bacc
    from concourse.bass_utils import run_bass_kernel_spmd

    g = {k: np.asarray(v) for k, v in inputs.items()}

    def tiles(w):
        return np.ascontiguousarray(w.reshape(-1, 128, w.shape[1]).transpose(1, 0, 2))

    def per_batch(x):
        return np.ascontiguousarray(x.transpose(0, 2, 1).reshape(B, KC, 128, -1).transpose(0, 2, 1, 3))

    gates = list(g["L0_ffn_gate"]) + [g["L0_ffn_w_gate_s"]]
    ups = list(g["L0_ffn_up"]) + [g["L0_ffn_w_up_s"]]
    downs = list(g["L0_ffn_down"]) + [g["L0_ffn_w_down_s"]]
    arrays = {
        "xT": per_batch(g["x"]),
        "x": np.ascontiguousarray(g["x"].transpose(1, 0, 2)),
        "ctxT": per_batch(g["ctx_1024"]),
        "mask": np.ascontiguousarray(g["mask_1x1xSxS2_ik0"].reshape(S, S2)),
        "wqkv": tiles(g["L0_attn_w_qkv"]),
        "wout": tiles(g["L0_attn_w_out"]),
        "b_out": g["L0_attn_b_out"].reshape(1, C),
        "bv": g["L0_xattn_bv"].reshape(1, C),
        "bo": g["L0_xattn_bo"].reshape(1, C),
        "bq": np.ascontiguousarray(g["L0_xattn_bq"].reshape(KC, 128).T),
        "bk": np.ascontiguousarray(g["L0_xattn_bk"].reshape(KC, 128).T),
        "router": tiles(g["L0_ffn_router"].T),
        "wq": tiles(g["L0_xattn_Wq"].T),
        "wk": tiles(g["L0_xattn_Wk"].T),
        "wv": tiles(g["L0_xattn_Wv"].T),
        "wo": tiles(g["L0_xattn_Wo"].T),
        "ug": np.stack([tiles(np.concatenate([a, b]).T) for a, b in zip(gates, ups)]),
        "dn": np.stack([tiles(d.T) for d in downs]),
    }
    nc = bacc.Bacc("TRN2", target_bir_lowering=False, num_devices=1)
    aps = {n: nc.dram_tensor("in_" + n, v.shape, dt.from_np(v.dtype), kind="ExternalInput").ap() for n, v in arrays.items()}
    out = nc.dram_tensor("out_x", (B, S, C), F32, kind="ExternalOutput").ap()
    build(nc, aps, out)
    r = run_bass_kernel_spmd(nc, [{"in_" + n: v for n, v in arrays.items()}], core_ids=[0])
    return r.results[0]["out_x"]
```
